# Optimizing a Trainium2 kernel written in Bass

```python
import numpy as np
import jax
import jax.numpy as jnp

def _softmax(x, axis=-1):
    return jax.nn.softmax(x, axis=axis)

def _gelu(x):
    return jax.nn.gelu(x, approximate=True)

def _silu(x):
    return jax.nn.silu(x)

def _sigmoid(x):
    return jax.nn.sigmoid(x)

def _layernorm(x, axis=-1, eps=1e-05):
    m = jnp.mean(x, axis=axis, keepdims=True)
    v = jnp.var(x, axis=axis, keepdims=True)
    return (x - m) / jnp.sqrt(v + eps)

def _scatter_add(tgt, idx, src, axis=0):
    return tgt.at[idx].add(src)

def _segment_sum(src, seg, n):
    return jax.ops.segment_sum(src, seg, n)
kernel_name = 'mk_gnn_resnorm_d4_gnn_r64_34cb14'

def setup_inputs(seed: int=0):
    np.random.seed(seed)
    _w = jnp.asarray

    def _rec_inputs():
        import jax
        import jax.numpy as jnp
        _gk = jax.random.key(seed)
        x = -0.0003713 + 1 * jax.random.normal(jax.random.fold_in(_gk, 1), (100000, 128), jnp.float32)
        src = jax.random.randint(jax.random.fold_in(_gk, 2), (50000,), 0, 100000, jnp.int32)
        dst = jnp.minimum((100000 * jax.random.uniform(jax.random.fold_in(_gk, 3), (50000,)) ** 2.0).astype(jnp.int32), 99999)
        _o = jnp.argsort(dst, stable=True)
        src = src[_o]
        dst = dst[_o]
        edge_attr_64 = 0.000167468 + 1.0002 * jax.random.normal(jax.random.fold_in(_gk, 12), (50000, 64), jnp.float32)
        edge_type_64 = jax.random.randint(jax.random.fold_in(_gk, 14), (50000,), 0, 64, jnp.int32)
        edge_weight1 = jax.random.uniform(jax.random.fold_in(_gk, 15), (50000, 1), jnp.float32, 0.0, 0.999998)
        return (x, src, dst, edge_attr_64, edge_type_64, edge_weight1)
    x, src, dst, edge_attr_64, edge_type_64, edge_weight1 = _rec_inputs()

    def _L0_gnn_setup():
        import jax, jax.numpy as jnp
        import numpy as np
        N_NODES = 100000
        N_EDGES = 10000
        HID = 128
        EDGE_D = 64
        GLOB_D = 64
        LN_EPS = 1e-05

        def _linear(x, W, b):
            return x @ W.T + b
        key = jax.random.key(seed)
        ks = jax.random.split(key, 16)
        s = lambda d: 1.0 / np.sqrt(d)
        inp = {'node_state': jax.random.normal(ks[0], (N_NODES, HID), jnp.float32), 'edge_index': jax.random.randint(ks[1], (2, N_EDGES), 0, N_NODES, jnp.int64), 'edge_state': jax.random.normal(ks[2], (N_EDGES, EDGE_D), jnp.float32), 'global_state': jax.random.normal(ks[3], (GLOB_D,), jnp.float32), 'Wm1': jax.random.uniform(ks[4], (HID, HID + EDGE_D + GLOB_D), jnp.float32, -s(HID + EDGE_D + GLOB_D), s(HID + EDGE_D + GLOB_D)), 'bm1': jnp.zeros((HID,), jnp.float32), 'Wm2': jax.random.uniform(ks[5], (HID, HID), jnp.float32, -s(HID), s(HID)), 'bm2': jnp.zeros((HID,), jnp.float32), 'Wu1': jax.random.uniform(ks[6], (HID, HID + HID + GLOB_D), jnp.float32, -s(HID + HID + GLOB_D), s(HID + HID + GLOB_D)), 'bu1': jnp.zeros((HID,), jnp.float32), 'Wu2': jax.random.uniform(ks[7], (HID, HID), jnp.float32, -s(HID), s(HID)), 'bu2': jnp.zeros((HID,), jnp.float32), 'ln_g': jnp.ones((HID,), jnp.float32), 'ln_b': jnp.zeros((HID,), jnp.float32)}
        return inp
    _L0_gnn_all = _L0_gnn_setup()
    _L0_gnn_in = {k: v for k, v in _L0_gnn_all.items() if k in ('global_state', 'Wm1', 'bm1', 'Wm2', 'bm2', 'Wu1', 'bu1', 'Wu2', 'bu2', 'ln_g', 'ln_b')}
    del _L0_gnn_all

    def _L1_gnn_setup():
        import jax, jax.numpy as jnp
        import numpy as np
        N_NODES = 50000
        N_EDGES = 12500
        NIN = 128
        NOUT = 128
        NHEAD = 4
        HEAD_DIM = NOUT // NHEAD
        NEG_SLOPE = 0.2
        key = jax.random.key(seed)
        k1, k2, k3, k4, k5 = jax.random.split(key, 5)
        x = jax.random.normal(k1, (N_NODES, NIN), dtype=jnp.float32)
        edge_index = jax.random.randint(k2, (2, N_EDGES), 0, N_NODES, dtype=jnp.int64)
        W = jax.random.normal(k3, (NIN, NOUT), dtype=jnp.float32) / np.sqrt(NIN)
        att_src = jax.random.normal(k4, (NHEAD, HEAD_DIM), dtype=jnp.float32) / np.sqrt(HEAD_DIM)
        att_dst = jax.random.normal(k5, (NHEAD, HEAD_DIM), dtype=jnp.float32) / np.sqrt(HEAD_DIM)
        bias = jnp.zeros((NOUT,), dtype=jnp.float32)
        return {'x': x, 'edge_index': edge_index, 'W': W, 'att_src': att_src, 'att_dst': att_dst, 'bias': bias}
    _L1_gnn_all = _L1_gnn_setup()
    _L1_gnn_in = {k: v for k, v in _L1_gnn_all.items() if k in ('W', 'att_src', 'att_dst', 'bias')}
    del _L1_gnn_all

    def _L2_gnn_setup():
        import jax, jax.numpy as jnp
        import numpy as np
        N_NODES = 50000
        N_EDGES = 12500
        IN_DIM = 128
        OUT_DIM = 128
        NUM_RELS = 64
        NUM_BASES = 4
        key = jax.random.key(seed)
        ks = jax.random.split(key, 8)
        feat = jax.random.normal(ks[0], (N_NODES, IN_DIM), dtype=jnp.float32)
        src = jax.random.randint(ks[1], (N_EDGES,), 0, N_NODES)
        dst = jax.random.randint(ks[2], (N_EDGES,), 0, N_NODES)
        etype = jax.random.randint(ks[3], (N_EDGES,), 0, NUM_RELS)
        norm = jax.random.uniform(ks[4], (N_EDGES, 1), dtype=jnp.float32)
        v_b = jax.random.normal(ks[5], (NUM_BASES, IN_DIM, OUT_DIM), dtype=jnp.float32) * (2.0 / np.sqrt(IN_DIM + OUT_DIM))
        a_rb = jax.random.normal(ks[6], (NUM_RELS, NUM_BASES), dtype=jnp.float32) * (2.0 / np.sqrt(NUM_RELS + NUM_BASES))
        loop_weight = jax.random.normal(ks[7], (IN_DIM, OUT_DIM), dtype=jnp.float32) * (2.0 / np.sqrt(IN_DIM + OUT_DIM))
        return {'feat': feat, 'src': src, 'dst': dst, 'etype': etype, 'norm': norm, 'v_b': v_b, 'a_rb': a_rb, 'loop_weight': loop_weight}
    _L2_gnn_all = _L2_gnn_setup()
    _L2_gnn_in = {k: v for k, v in _L2_gnn_all.items() if k in ('v_b', 'a_rb', 'loop_weight')}
    del _L2_gnn_all

    def _L3_gnn_setup():
        import jax, jax.numpy as jnp
        import numpy as np
        N, E, C = (50000, 9375, 128)

        def _spline_conv(x, src, dst, u, W, root, b):
            n = x.shape[0]
            h0 = x @ W[0]
            h1 = x @ W[1]
            msg = (1.0 - u) * h0[src] + u * h1[src]
            agg = jax.ops.segment_sum(msg, dst, num_segments=n)
            deg = jax.ops.segment_sum(jnp.ones((src.shape[0],), msg.dtype), dst, num_segments=n)
            agg = agg / jnp.maximum(deg, 1.0)[:, None]
            return agg + x @ root + b
        key = jax.random.key(seed)
        ks = jax.random.split(key, 9)
        s = 1.0 / np.sqrt(C)
        return {'x': jax.random.normal(ks[0], (N, C), jnp.float32), 'edge_index': jax.random.randint(ks[1], (2, E), 0, N, jnp.int32), 'edge_attr': jax.random.uniform(ks[2], (E, 1), jnp.float32), 'W1': jax.random.normal(ks[3], (2, C, C), jnp.float32) * s, 'root1': jax.random.normal(ks[4], (C, C), jnp.float32) * s, 'b1': jax.random.normal(ks[5], (C,), jnp.float32) * 0.01, 'W2': jax.random.normal(ks[6], (2, C, C), jnp.float32) * s, 'root2': jax.random.normal(ks[7], (C, C), jnp.float32) * s, 'b2': jax.random.normal(ks[8], (C,), jnp.float32) * 0.01}
    _L3_gnn_all = _L3_gnn_setup()
    _L3_gnn_in = {k: v for k, v in _L3_gnn_all.items() if k in ('W1', 'root1', 'b1', 'W2', 'root2', 'b2')}
    del _L3_gnn_all
    return {'x': x, 'src': src, 'dst': dst, 'edge_attr_64': edge_attr_64, 'edge_type_64': edge_type_64, 'edge_weight1': edge_weight1, 'L0_gnn_global_state': _L0_gnn_in['global_state'], 'L0_gnn_Wm1': _L0_gnn_in['Wm1'], 'L0_gnn_bm1': _L0_gnn_in['bm1'], 'L0_gnn_Wm2': _L0_gnn_in['Wm2'], 'L0_gnn_bm2': _L0_gnn_in['bm2'], 'L0_gnn_Wu1': _L0_gnn_in['Wu1'], 'L0_gnn_bu1': _L0_gnn_in['bu1'], 'L0_gnn_Wu2': _L0_gnn_in['Wu2'], 'L0_gnn_bu2': _L0_gnn_in['bu2'], 'L0_gnn_ln_g': _L0_gnn_in['ln_g'], 'L0_gnn_ln_b': _L0_gnn_in['ln_b'], 'L1_gnn_W': _L1_gnn_in['W'], 'L1_gnn_att_src': _L1_gnn_in['att_src'], 'L1_gnn_att_dst': _L1_gnn_in['att_dst'], 'L1_gnn_bias': _L1_gnn_in['bias'], 'L2_gnn_v_b': _L2_gnn_in['v_b'], 'L2_gnn_a_rb': _L2_gnn_in['a_rb'], 'L2_gnn_loop_weight': _L2_gnn_in['loop_weight'], 'L3_gnn_W1': _L3_gnn_in['W1'], 'L3_gnn_root1': _L3_gnn_in['root1'], 'L3_gnn_b1': _L3_gnn_in['b1'], 'L3_gnn_W2': _L3_gnn_in['W2'], 'L3_gnn_root2': _L3_gnn_in['root2'], 'L3_gnn_b2': _L3_gnn_in['b2']}

def reference(x, src, dst, edge_attr_64, edge_type_64, edge_weight1, L0_gnn_global_state, L0_gnn_Wm1, L0_gnn_bm1, L0_gnn_Wm2, L0_gnn_bm2, L0_gnn_Wu1, L0_gnn_bu1, L0_gnn_Wu2, L0_gnn_bu2, L0_gnn_ln_g, L0_gnn_ln_b, L1_gnn_W, L1_gnn_att_src, L1_gnn_att_dst, L1_gnn_bias, L2_gnn_v_b, L2_gnn_a_rb, L2_gnn_loop_weight, L3_gnn_W1, L3_gnn_root1, L3_gnn_b1, L3_gnn_W2, L3_gnn_root2, L3_gnn_b2):
    import jax
    import jax.numpy as jnp

    def _L0_gnn_ref(node_state, edge_index, edge_state, global_state, Wm1, bm1, Wm2, bm2, Wu1, bu1, Wu2, bu2, ln_g, ln_b):
        import jax, jax.numpy as jnp
        import numpy as np
        N_NODES = 100000
        N_EDGES = 10000
        HID = 128
        EDGE_D = 64
        GLOB_D = 64
        LN_EPS = 1e-05

        def _linear(x, W, b):
            return x @ W.T + b
        src, dst = (edge_index[0], edge_index[1])
        num_nodes = node_state.shape[0]
        num_edges = edge_state.shape[0]
        g_edges = jnp.broadcast_to(global_state[None, :], (num_edges, GLOB_D))
        msg_in = jnp.concatenate([node_state[src], edge_state, g_edges], axis=-1)
        messages = _linear(jax.nn.relu(_linear(msg_in, Wm1, bm1)), Wm2, bm2)
        aggregated = jax.ops.segment_sum(messages, dst, num_segments=num_nodes)
        degree = jax.ops.segment_sum(jnp.ones((num_edges,), node_state.dtype), dst, num_segments=num_nodes)
        aggregated = aggregated / jnp.maximum(degree, 1.0)[:, None]
        g_nodes = jnp.broadcast_to(global_state[None, :], (num_nodes, GLOB_D))
        upd_in = jnp.concatenate([node_state, aggregated, g_nodes], axis=-1)
        delta = _linear(jax.nn.relu(_linear(upd_in, Wu1, bu1)), Wu2, bu2)
        h = node_state + delta
        mu = jnp.mean(h, axis=-1, keepdims=True)
        var = jnp.mean(jnp.square(h - mu), axis=-1, keepdims=True)
        return (h - mu) * jax.lax.rsqrt(var + LN_EPS) * ln_g + ln_b

    def _L1_gnn_ref(x, edge_index, W, att_src, att_dst, bias):
        import jax, jax.numpy as jnp
        import numpy as np
        N_NODES = 50000
        N_EDGES = 12500
        NIN = 128
        NOUT = 128
        NHEAD = 4
        HEAD_DIM = NOUT // NHEAD
        NEG_SLOPE = 0.2
        N = x.shape[0]
        xp = (x @ W).reshape(N, NHEAD, HEAD_DIM)
        a_src = jnp.einsum('nhc,hc->nh', xp, att_src)
        a_dst = jnp.einsum('nhc,hc->nh', xp, att_dst)
        loops = jnp.arange(N, dtype=edge_index.dtype)
        src = jnp.concatenate([edge_index[0], loops])
        dst = jnp.concatenate([edge_index[1], loops])
        e = jax.nn.leaky_relu(a_src[src] + a_dst[dst], NEG_SLOPE)
        m = jax.ops.segment_max(e, dst, num_segments=N)
        e = jnp.exp(e - m[dst])
        s = jax.ops.segment_sum(e, dst, num_segments=N)
        alpha = e / s[dst]
        msg = alpha[:, :, None] * xp[src]
        out = jax.ops.segment_sum(msg, dst, num_segments=N)
        return out.reshape(N, NOUT) + bias

    def _L2_gnn_ref(feat, src, dst, etype, norm, v_b, a_rb, loop_weight):
        import jax, jax.numpy as jnp
        import numpy as np
        N_NODES = 50000
        N_EDGES = 12500
        IN_DIM = 128
        OUT_DIM = 128
        NUM_RELS = 64
        NUM_BASES = 4
        num_nodes = feat.shape[0]
        num_bases = v_b.shape[0]
        h_b = jnp.einsum('ni,bio->nbo', feat, v_b)
        coef = a_rb[etype]
        msg = coef[:, 0:1] * h_b[src, 0]
        for b in range(1, num_bases):
            msg = msg + coef[:, b:b + 1] * h_b[src, b]
        msg = msg * norm
        agg = jax.ops.segment_sum(msg, dst, num_segments=num_nodes)
        h = agg + feat @ loop_weight
        return jax.nn.relu(h)

    def _L3_gnn_ref(x, edge_index, edge_attr, W1, root1, b1, W2, root2, b2):
        import jax, jax.numpy as jnp
        import numpy as np
        N, E, C = (50000, 9375, 128)

        def _spline_conv(x, src, dst, u, W, root, b):
            n = x.shape[0]
            h0 = x @ W[0]
            h1 = x @ W[1]
            msg = (1.0 - u) * h0[src] + u * h1[src]
            agg = jax.ops.segment_sum(msg, dst, num_segments=n)
            deg = jax.ops.segment_sum(jnp.ones((src.shape[0],), msg.dtype), dst, num_segments=n)
            agg = agg / jnp.maximum(deg, 1.0)[:, None]
            return agg + x @ root + b
        src, dst = (edge_index[0], edge_index[1])
        h = _spline_conv(x, src, dst, edge_attr, W1, root1, b1)
        return _spline_conv(h, src, dst, edge_attr, W2, root2, b2)
    edge_index = jnp.stack([src, dst])
    x = _layernorm(x + _L0_gnn_ref(x, edge_index, edge_attr_64, L0_gnn_global_state, L0_gnn_Wm1, L0_gnn_bm1, L0_gnn_Wm2, L0_gnn_bm2, L0_gnn_Wu1, L0_gnn_bu1, L0_gnn_Wu2, L0_gnn_bu2, L0_gnn_ln_g, L0_gnn_ln_b), axis=-1)
    x = _layernorm(x + _L1_gnn_ref(x, edge_index, L1_gnn_W, L1_gnn_att_src, L1_gnn_att_dst, L1_gnn_bias), axis=-1)
    x = _layernorm(x + _L2_gnn_ref(x, src, dst, edge_type_64, edge_weight1, L2_gnn_v_b, L2_gnn_a_rb, L2_gnn_loop_weight), axis=-1)
    x = _layernorm(x + _L3_gnn_ref(x, edge_index, edge_weight1, L3_gnn_W1, L3_gnn_root1, L3_gnn_b1, L3_gnn_W2, L3_gnn_root2, L3_gnn_b2), axis=-1)
    return x

_drawn_inputs = setup_inputs


def setup_inputs(seed=0):
    import zlib

    import numpy as np

    out = dict(_drawn_inputs(seed))
    spreads = {'L0_gnn_bm1': (0.0, 2.0),
     'L0_gnn_bm2': (0.0, 2.0),
     'L0_gnn_bu1': (0.0, 0.273),
     'L0_gnn_bu2': (0.0, 0.1),
     'L0_gnn_ln_g': (1.0, 0.2),
     'L0_gnn_ln_b': (0.0, 0.1),
     'L1_gnn_bias': (0.0, 0.1)}
    factors = {'edge_attr_64': 8.0,
     'L0_gnn_Wm1': 6.457,
     'L0_gnn_Wm2': 5.242,
     'L3_gnn_b1': 6.455,
     'L3_gnn_b2': 8.0}
    for name, (base, spread) in spreads.items():
        noise = np.random.default_rng([zlib.crc32(name.encode()), seed]).standard_normal(out[name].shape)
        drawn = base * np.exp(spread * noise) if base else spread * noise
        out[name] = jnp.asarray(drawn.astype(out[name].dtype))
    for name, factor in factors.items():
        out[name] = (out[name] * factor).astype(out[name].dtype)
    return out
```

```python
from contextlib import ExitStack

import concourse.bass as bass
from concourse import mybir

F32 = mybir.dt.float32
I32 = mybir.dt.int32
ALU = mybir.AluOpType
ACT = mybir.ActivationFunctionType
AX = mybir.AxisListType

P = 128
C = 128
N = 100000
TILES = 392
RING = 7
ET = 2 * RING
ESTEPS = TILES // ET
ED = 64
RELS = 64
BASES = 4
HEADS = 4
HD = C // HEADS
RB = 8
BLOCK = P * RB
BLOCKS = -(-N // BLOCK)
SLOTS = 4
NSTEPS = BLOCKS // SLOTS
TAIL = BLOCKS - NSTEPS * SLOTS
W = 136
HEAD = N
ROWS = -(-(N + P) // BLOCK) * BLOCK
AWAY = float(1 << 22)
PAD_DST = 1 << 21
LOW = 1.0e30
LN_EPS = 1e-5


def up_to(eng, sem, count, per=1):
    if isinstance(count, int) and count <= 0:
        return
    eng.wait_ge(sem, count * per)


def edge_steps(eng, body):
    body(0)
    with eng.Fori(1, ESTEPS - 1) as i:
        body(i)
    body(ESTEPS - 1)


def node_blocks(eng, body):
    for u in range(SLOTS):
        body(u, u, 0)
    with eng.Fori(1, NSTEPS) as i:
        for u in range(SLOTS):
            body(i * SLOTS + u, u, i)
    for u in range(TAIL):
        body(NSTEPS * SLOTS + u, u, NSTEPS)


def block_rows(block):
    return min(block * BLOCK, N - BLOCK) if isinstance(block, int) else block * BLOCK


def rows_of(table, block, width):
    return table[bass.ds(block_rows(block), BLOCK), :].rearrange("(p j) f -> p (j f)", p=P)


class Chain:

    def __init__(self, eng, sem, per):
        self.eng, self.sem, self.per, self.k, self.item = eng, sem, per, 0, 0

    def start(self, item):
        self.item, self.k = item, 0

    def __call__(self, instruction):
        self.k += 1
        assert self.k <= self.per
        instruction.then_inc(self.sem, 1)
        self.eng.wait_ge(self.sem, self.item * self.per + self.k)


def build(nc, D, out, upto=99):
    with ExitStack() as ctx:
        _build(nc, D, out, ctx, upto)


def _build(nc, D, out, ctx, upto):
    def sb(name, shape, dt=F32, c=ctx):
        return c.enter_context(nc.sbuf_tensor(name, shape, dt))

    def sem(name):
        return ctx.enter_context(nc.semaphore(name))

    class Phase:

        def __init__(self, name):
            self.name, self.sems = name, []

        def __call__(self, what):
            self.sems.append(nc.alloc_semaphore(name=f"{self.name}_{what}"))
            return self.sems[-1]

        def end(self):
            nc.all_engine_barrier()
            nc.clear_and_free_semaphores(self.sems)
            nc.all_engine_barrier()

    AGG = nc.dram_tensor("AGG", [ROWS, W], F32).ap()
    X1 = nc.dram_tensor("X1", [N, C], F32).ap()
    X2 = nc.dram_tensor("X2", [N, C], F32).ap()
    X3 = nc.dram_tensor("X3", [N, C], F32).ap()
    HT = nc.dram_tensor("HT", [N, C], F32).ap()
    head_rows = AGG[HEAD:HEAD + P, :]

    K = {}
    for name in ("ident", "ones"):
        K[name] = sb(name, [P, P])
    wload = []
    def weight(name, rows, cols):
        K[name] = sb("w_" + name, [rows, cols])
        wload.append((K[name][:, :], D[name]))
    weight("wm1x", C, C); weight("wm1e", ED, C); weight("wm1g", 64, C)
    weight("wm2", C, C); weight("wu1x", C, C); weight("wu1a", C, C); weight("wu1g", 64, C)
    weight("wu2", C, C); weight("gstate", 64, 1); weight("bm1", C, 1); weight("bu1", C, 1)
    weight("bm2", 1, C); weight("vb", C, BASES * C); weight("loop", C, C)
    weight("sw1", C, 2 * C); weight("root1", C, C); weight("sw2", C, 2 * C); weight("root2", C, C)
    K["wgat"] = sb("w_gat", [C, C + HEADS])
    K["wdst"] = sb("w_dst", [C, HEADS])
    K["wself"] = sb("w_self", [C, HEADS])
    K["atts"] = sb("w_atts", [C, C]); K["attd"] = sb("w_attd", [C, C])
    K["arb"] = sb("w_arb", [P, BASES * RELS])
    for name in ("bu2", "ln_g", "ln_b", "gbias", "sb1", "sb2"):
        K[name] = sb("r_" + name, [P, C])
    src = sb("src", [P, TILES], I32)
    dsti = sb("dsti", [P, TILES], I32)
    dst_gather = sb("dst_gather", [P, TILES], I32)
    target = sb("target", [P, TILES], I32)
    keep = sb("keep", [P, TILES])
    reset = sb("reset", [P, TILES])
    etype = sb("etype", [P, TILES])
    eweight = sb("eweight", [P, TILES])
    eweight1 = sb("eweight1", [P, TILES])
    coef = sb("coef", [P, TILES, BASES])
    invdeg = sb("invdeg", [P, BLOCKS, RB])
    bias_m = sb("bias_m", [C, 1])
    bias_u = sb("bias_u", [C, 1])
    half = sb("half", [P, RB])
    iota_r = sb("iota_r", [P, RELS])
    t_index = sb("t_index", [P, 1], I32)
    h_index = sb("h_index", [P, 1], I32)
    seam = {n: sb("seam_" + n, [P, P]) for n in ("tt", "th", "ht", "hh")}

    src_now = [sb(f"src_now{h}", [P, RING], I32) for h in range(2)]
    dst_now = [sb(f"dst_now{h}", [P, RING], I32) for h in range(2)]
    target_now = [sb(f"target_now{h}", [P, RING], I32) for h in range(2)]
    xs = [sb(f"xs{q}", [P, C]) for q in range(RING)]
    acc = [sb(f"acc{q}", [P, W]) for q in range(RING)]
    hrow = sb("hrow", [P, W])
    trow = sb("trow", [P, W])

    psum = [ctx.enter_context(nc.psum_tensor(f"bank{i}", [P, 512], F32)) for i in range(8)]

    w_in, idx_in, shift_in, const_done = sem("w_in"), sem("idx_in"), sem("shift_in"), sem("const_done")
    prep, prep_pe, prep_shift, zeroed, iota_done, cols_ready = sem("prep"), sem("prep_pe"), sem("prep_shift"), sem("zeroed"), sem("iota_done"), sem("cols_ready")
    with ExitStack() as c0:
        ZB = 7
        zero = sb("zero", [P, RB * W], c=c0)
        tf = [sb(f"tf{i}", [P, TILES], c=c0) for i in range(5)]
        prev_last = sb("prev_last", [P, 1], I32, c0)
        next_last = sb("next_last", [P, 1], I32, c0)
        cols = sb("cols", [P, 12], c=c0)
        hrf = sb("hrf", [P, 1], c=c0)
        typei = sb("typei", [P, TILES], I32, c0)
        block = c0.enter_context(nc.Block())
        row_loads = [(K[n], D[n]) for n in ("bu2", "ln_g", "ln_b", "gbias", "sb1", "sb2", "atts", "attd", "arb")]
        n_w = len(wload) + 1 + len(row_loads)

        @block.sync
        def _(sp):
            for o, i in ((src, D["src"]), (dsti, D["dst"]), (typei, D["etype"]), (eweight, D["eweight"])):
                sp.dma_start(o[:, :], i).then_inc(idx_in, 16)
            sp.wait_ge(prep_shift, 1)
            sp.dma_start(prev_last[1:P, :], D["dst"][0:P - 1, TILES - 1:TILES],
                         allow_slow_non_contiguous=True).then_inc(shift_in, 16)
            sp.dma_start(next_last[0:P - 1, :], D["dst"][1:P, TILES - 1:TILES],
                         allow_slow_non_contiguous=True).then_inc(shift_in, 16)
            for o, i in wload:
                sp.dma_start(o, i).then_inc(w_in, 16)
            sp.dma_start(K["wgat"][:, 0:C], D["wgat"]).then_inc(w_in, 16)
            for o, i in row_loads:
                sp.dma_start(o[:, :], i.partition_broadcast(P)).then_inc(w_in, 16)

        @block.scalar
        def _(act):
            act.wait_ge(const_done, 1)
            dst = AGG.rearrange("(b p j) f -> p b (j f)", p=P, j=RB)
            for b in range(0, ROWS // BLOCK, ZB):
                act.dma_start(dst[:, b:b + ZB, :],
                              zero[:, :].unsqueeze(1).to_broadcast([P, ZB, RB * W])).then_inc(zeroed, 16)
            act.wait_ge(zeroed, 16 * (ROWS // BLOCK // ZB))

        @block.gpsimd
        def _(pool):
            pool.iota(iota_r[:, :], [[1, RELS]], base=0, channel_multiplier=0,
                      allow_small_or_imprecise_dtypes=True).then_inc(iota_done, 1)
            pool.iota(hrf[:, :], [[0, 1]], base=HEAD, channel_multiplier=1,
                      allow_small_or_imprecise_dtypes=True).then_inc(iota_done, 1)
            pool.memset(K["ident"][:, :], 0.0).then_inc(iota_done, 1)
            pool.wait_ge(iota_done, 3)
            pool.affine_select(out=K["ident"][:, :], in_=K["ident"][:, :], compare_op=ALU.not_equal, fill=1.0,
                               base=0, pattern=[[-1, P]], channel_multiplier=1).then_inc(iota_done, 1)

        @block.vector
        def _(dve):
            n = [0]

            def link(ins):
                n[0] += 1
                ins.then_inc(prep, 1)
                dve.wait_ge(prep, n[0])

            nc.vector.memset(zero[:, :], 0.0).then_inc(const_done, 1)
            link(dve.memset(prev_last[:, :], -1))
            dve.memset(next_last[:, :], -1).then_inc(prep_shift, 1)
            for u in range(RING):
                link(dve.memset(acc[u][:, :], 0.0))
            link(dve.memset(K["ones"][:, :], 1.0))
            link(dve.memset(half[:, :], -0.5))
            dve.wait_ge(idx_in, 64)
            dstf, inhead, notend, a, b = [t[:, :] for t in tf]
            link(dve.tensor_copy(etype[:, :], typei[:, :]))
            link(dve.tensor_scalar(eweight1[:, :], eweight[:, :], -1.0, 1.0, ALU.mult, ALU.add))
            link(dve.tensor_copy(dstf, dsti[:, :]))
            link(dve.tensor_scalar(a, dstf, float(N - 1), None, ALU.min))
            link(dve.tensor_copy(dst_gather[:, :], a))
            link(dve.memset(keep[:, 0:1], 0.0))
            link(dve.tensor_tensor(keep[:, 1:], tf[0][:, 1:], tf[0][:, :-1], ALU.is_equal))
            link(dve.tensor_scalar(reset[:, :], keep[:, :], -1.0, LOW, ALU.add, ALU.mult))
            link(dve.tensor_scalar(inhead, dstf, tf[0][:, 0:1], None, ALU.is_equal))
            link(dve.memset(tf[2][:, TILES - 1:], 1.0))
            link(dve.tensor_copy(tf[2][:, 0:TILES - 1], keep[:, 1:]))
            dve.wait_ge(iota_done, 4)
            link(dve.tensor_scalar(a, dstf, -1.0, hrf[:, 0:1], ALU.mult, ALU.add))
            link(dve.tensor_tensor(a, a, inhead, ALU.mult))
            link(dve.tensor_tensor(a, a, dstf, ALU.add))
            link(dve.scalar_tensor_tensor(b, notend, AWAY, a, ALU.mult, ALU.add))
            link(dve.tensor_copy(target[:, :], b))
            df, dl, pl, nl, e1, e2 = [cols[:, k:k + 1] for k in range(6)]
            dve.wait_ge(shift_in, 32)
            link(dve.tensor_copy(df, tf[0][:, 0:1]))
            link(dve.tensor_copy(dl, tf[0][:, TILES - 1:]))
            link(dve.tensor_copy(pl, prev_last[:, :]))
            link(dve.tensor_copy(nl, next_last[:, :]))
            link(dve.tensor_tensor(e1, dl, nl, ALU.is_equal))
            link(dve.scalar_tensor_tensor(e2, e1, AWAY, dl, ALU.mult, ALU.add))
            link(dve.tensor_copy(t_index[:, :], e2))
            link(dve.tensor_tensor(e1, df, pl, ALU.is_equal))
            link(dve.tensor_tensor(e1, e1, tf[1][:, TILES - 1:], ALU.max))
            link(dve.scalar_tensor_tensor(e2, e1, AWAY, df, ALU.mult, ALU.add))
            link(dve.tensor_copy(h_index[:, :], e2))
            link(dve.tensor_scalar(seam["tt"][:, :], K["ones"][:, :], dl, None, ALU.mult))
            dve.tensor_scalar(seam["hh"][:, :], K["ones"][:, :], df, None, ALU.mult).then_inc(cols_ready, 1)
            dve.wait_ge(prep_pe, 1)
            link(dve.tensor_scalar(seam["th"][:, :], psum[0][:, 128:256], dl, None, ALU.is_equal))
            link(dve.tensor_scalar(seam["ht"][:, :], psum[0][:, 0:128], df, None, ALU.is_equal))
            link(dve.tensor_scalar(seam["tt"][:, :], psum[0][:, 0:128], dl, None, ALU.is_equal))
            link(dve.tensor_scalar(seam["hh"][:, :], psum[0][:, 128:256], df, None, ALU.is_equal))
            dve.wait_ge(w_in, 16 * n_w)
            for name, o in (("atts", K["wgat"][:, C:]), ("attd", K["wdst"][:, :])):
                link(dve.tensor_tensor(K[name][:, :], K["wgat"][:, 0:C], K[name][:, :], ALU.mult))
                link(dve.tensor_reduce(o, K[name][:, :].rearrange("p (h d) -> p h d", h=HEADS), AX.X, ALU.add))
            link(dve.tensor_tensor(K["wself"][:, :], K["wgat"][:, C:], K["wdst"][:, :], ALU.add))
            dve.wait_ge(prep_pe, 2)
            link(dve.tensor_tensor(bias_m[:, :], K["bm1"][:, :], psum[1][:, 0:1], ALU.add))
            link(dve.tensor_tensor(bias_u[:, :], K["bu1"][:, :], psum[1][:, 1:2], ALU.add))

        @block.tensor
        def _(pe):
            pe.wait_ge(iota_done, 4)
            pe.wait_ge(cols_ready, 1)
            pe.matmul(psum[0][:, 0:128], seam["tt"][:, :], K["ident"][:, :], start=True, stop=True)
            pe.matmul(psum[0][:, 128:256], seam["hh"][:, :], K["ident"][:, :],
                      start=True, stop=True).then_inc(prep_pe, 1)
            pe.wait_ge(w_in, 16 * n_w)
            pe.matmul(psum[1][:, 0:1], K["wm1g"][:, :], K["gstate"][:, :], start=True, stop=True)
            pe.matmul(psum[1][:, 1:2], K["wu1g"][:, :], K["gstate"][:, :],
                      start=True, stop=True).then_inc(prep_pe, 1)

    def edge_phase(name, kind, table):
        own = Phase(name)
        edges(name, kind, table, own)
        own.end()

    def edges(name, kind, table, s):
        two = kind == "gat"
        got = [s(f"got{q}") for q in range(RING)]
        sent = [s(f"sent{q}") for q in range(RING)]
        idx_ready, pool_on = s("idx_ready"), s("pool_on")
        turned, xt_ready = s("turned"), s("xt_ready")
        acc_ready, msg_ready = s("acc_ready"), s("msg_ready")
        c = ExitStack()
        with c:
            xt = [sb(f"{name}_xt{k}", [P, 2 * C], c=c) for k in range(2)]
            if two:
                xd = [sb(f"{name}_xd{q}", [P, C], c=c) for q in range(RING)]
                small = sb(f"{name}_small", [P, 8, HEADS], c=c)
                diff = [sb(f"{name}_diff{k}", [P, 2, HEADS], c=c) for k in range(2)]
                part = [sb(f"{name}_part{k}", [P, 2, HEADS], c=c) for k in range(2)]
                scaled = sb(f"{name}_scaled", [P, C], c=c)
                weighed = sb(f"{name}_weighed", [P, C], c=c)
                diff_ready, part_ready = s("diff_ready"), s("part_ready")
            if kind == "mlp":
                ea = [sb(f"{name}_ea{h}", [P, ET // 2 * ED], c=c) for h in range(2)]
                zt = [sb(f"{name}_zt{k}", [P, C], c=c) for k in range(2)]
                onehot = sb(f"{name}_onehot", [P, ET, RELS], c=c)
                prod = sb(f"{name}_prod", [P, ET, RELS], c=c)
                ea_got = [s(f"ea_got{h}") for h in range(2)]
                eat_ready, hid_ready, zt_ready = s("eat_ready"), s("hid_ready"), s("zt_ready")
            step_sem = s("dve_steps")
            run = [sb(f"{name}_run{k}", [P, C], c=c) for k in range(2)]
            block = c.enter_context(nc.Block())
            ACC = 2 if kind == "mlp" else 1

            if kind == "mlp":
                @block.sync
                def _(sp):
                    def body(i):
                        for h in range(2):
                            up_to(sp, turned, i * ET - ET + (h + 1) * ET // 2 if not isinstance(i, int) or i else 0)
                            sp.dma_start(ea[h][:, :], D["eattr"][:, bass.ds(i * (ET * ED) + h * (ET // 2 * ED), ET // 2 * ED)])\
                              .then_inc(ea_got[h], 16)
                    edge_steps(sp, body)

            @block.gpsimd
            def _(pool):
                def gather(h, q):
                    pool.indirect_dma_start(xs[q][:, :], None, table, bass.IndirectOffsetOnAxis(
                        ap=src_now[h][:, q:q + 1], axis=0)).then_inc(got[q], 16)
                    if two:
                        pool.indirect_dma_start(xd[q][:, :], None, table, bass.IndirectOffsetOnAxis(
                            ap=dst_now[h][:, q:q + 1], axis=0)).then_inc(got[q], 16)

                def copy_index(o, table_, t):
                    pool.tensor_copy(o[:, :], table_[:, bass.ds(t, RING)]).then_inc(idx_ready, 1)

                per = 3 if two else 2

                copy_index(src_now[0], src, 0)
                if two:
                    copy_index(dst_now[0], dst_gather, 0)
                pool.wait_ge(idx_ready, per - 1)
                for q in range(RING):
                    gather(0, q)

                def body(i):
                    for h in range(2):
                        last = isinstance(i, int) and i == ESTEPS - 1 and h == 1
                        for q in range(RING):
                            t = i * ET + h * RING + q
                            pool.wait_ge(acc_ready, (t + 1) * ACC)
                            pool.sem_inc(pool_on, 1)
                            if q == 0:
                                copy_index(target_now[h], target, t)
                                if not last:
                                    copy_index(src_now[1 - h], src, t + RING)
                                    if two:
                                        copy_index(dst_now[1 - h], dst_gather, t + RING)
                                pool.wait_ge(idx_ready, per - 1 + (i * 2 + h) * per + (1 if last else per))
                                pool.sem_inc(pool_on, 1)
                            pool.indirect_dma_start(AGG, bass.IndirectOffsetOnAxis(ap=target_now[h][:, q:q + 1], axis=0),
                                                    acc[q][:, :], None, bounds_check=ROWS - 1, oob_is_err=False)\
                                .then_inc(sent[q], 16)
                            if not last:
                                gather(1 - h, q)

                edge_steps(pool, body)
                for q in range(RING):
                    pool.wait_ge(sent[q], 16 * 2 * ESTEPS)

            per_got = 32 if two else 16

            @block.tensor
            def _(pe):
                def turn(i, u, t):
                    k, q = u % 2, u % RING
                    pe.wait_ge(got[q], (i * 2 + u // RING + 1) * per_got)
                    up_to(pe, xt_ready, t - 1)
                    if kind == "mlp":
                        up_to(pe, eat_ready, t - 1)
                        pe.wait_ge(ea_got[u // (ET // 2)], (i + 1) * 16)
                        v = u % (ET // 2)
                        pe.transpose(psum[k][:, 0:C], xs[q][:, :], K["ident"][:, :])
                        pe.transpose(psum[6 + k][0:ED, 0:C], ea[u // (ET // 2)][:, v * ED:(v + 1) * ED],
                                     K["ident"][:, :]).then_inc(turned, 1)
                    elif two:
                        pe.transpose(psum[k][:, 0:C], xs[q][:, :], K["ident"][:, :])
                        pe.transpose(psum[k][:, C:2 * C], xd[q][:, :], K["ident"][:, :]).then_inc(turned, 1)
                    else:
                        pe.transpose(psum[k][:, 0:C], xs[q][:, :], K["ident"][:, :]).then_inc(turned, 1)

                def message(u, t):
                    k = u % 2
                    x_t = xt[k]
                    pe.wait_ge(xt_ready, t + 1)
                    if kind == "mlp":
                        pe.wait_ge(eat_ready, t + 1)
                        up_to(pe, zt_ready, t - 1)
                        pe.matmul(psum[2 + k][:, 0:C], K["wm1x"][:, :], x_t[:, 0:C], start=True, stop=False)
                        pe.matmul(psum[2 + k][:, 0:C], K["wm1e"][:, :], x_t[0:ED, C:2 * C],
                                  start=False, stop=True).then_inc(hid_ready, 1)
                        pe.wait_ge(zt_ready, t + 1)
                        up_to(pe, acc_ready, t - 1, ACC)
                        pe.matmul(psum[4 + k][:, 0:C], zt[k][:, :], K["wm2"][:, :], start=True, stop=False)
                        pe.matmul(psum[4 + k][:, 0:C], K["ones"][0:1, :], K["bm2"][:, :],
                                  start=False, stop=True).then_inc(msg_ready, 1)
                    elif two:
                        up_to(pe, acc_ready, t - 1, ACC)
                        pe.matmul(psum[4 + k][:, 0:C + HEADS], x_t[:, 0:C], K["wgat"][:, :], start=True, stop=False)
                        pe.matmul(psum[4 + k][:, C:C + HEADS], x_t[:, C:2 * C], K["wdst"][:, :],
                                  start=False, stop=True).then_inc(msg_ready, 1)
                    else:
                        up_to(pe, acc_ready, t - 1, ACC)
                        w = K["vb"] if kind == "bases" else K["sw1"] if kind == "spline1" else K["sw2"]
                        n = BASES * C if kind == "bases" else 2 * C
                        pe.matmul(psum[4 + k][:, 0:n], x_t[:, 0:C], w[:, :], start=True, stop=True).then_inc(msg_ready, 1)

                turn(0, 0, 0)

                def body(i):
                    for u in range(ET):
                        t = i * ET + u
                        if u + 1 < ET:
                            turn(i, u + 1, t + 1)
                        elif not (isinstance(i, int) and i == ESTEPS - 1):
                            turn(i + 1, 0, t + 1)
                        message(u, t)

                edge_steps(pe, body)

            @block.scalar
            def _(act):
                def body(i):
                    for u in range(ET):
                        t, k = i * ET + u, u % 2
                        act.wait_ge(turned, t + 1)
                        up_to(act, hid_ready if kind == "mlp" else msg_ready, t - 1)
                        n = 2 * C if two else C
                        act.activation(xt[k][:, 0:n], psum[k][:, 0:n], ACT.Copy).then_inc(xt_ready, 1)
                        if kind == "mlp":
                            act.wait_ge(hid_ready, t + 1)
                            up_to(act, msg_ready, t - 1)
                            act.activation(zt[k][:, :], psum[2 + k][:, 0:C], ACT.Relu,
                                           bias=bias_m[:, 0:1]).then_inc(zt_ready, 1)
                        if two:
                            act.wait_ge(diff_ready, t + 1)
                            up_to(act, acc_ready, t - 1)
                            act.activation(part[k][:, :, :], diff[k][:, :, :], ACT.Exp).then_inc(part_ready, 1)
                edge_steps(act, body)

            @block.vector
            def _(dve):
                steps = {"mlp": 0, "gat": 9, "bases": 4, "spline1": 2, "spline2": 2}[kind]
                link = Chain(dve, step_sem, steps)

                def column(tensor, t):
                    return tensor[:, bass.ds(t, 1)]

                def coefficients(i):
                    lo = bass.ds(i * ET, ET)
                    dve_coef = Chain(dve, step_sem, 10)
                    dve_coef.start(i)
                    dve_coef(dve.tensor_tensor(onehot[:, :, :], etype[:, lo].unsqueeze(2).to_broadcast([P, ET, RELS]),
                                               iota_r[:, :].unsqueeze(1).to_broadcast([P, ET, RELS]), ALU.is_equal))
                    for b in range(BASES):
                        dve_coef(dve.tensor_tensor(prod[:, :, :], onehot[:, :, :],
                                                   K["arb"][:, b * RELS:(b + 1) * RELS].unsqueeze(1)
                                                   .to_broadcast([P, ET, RELS]), ALU.mult))
                        dve_coef(dve.tensor_reduce(coef[:, lo, b], prod[:, :, :], AX.X, ALU.add))
                    dve_coef(dve.tensor_tensor(coef[:, lo, :], coef[:, lo, :],
                                               eweight[:, lo].unsqueeze(2).to_broadcast([P, ET, BASES]), ALU.mult))

                def body(i):
                    for u in range(ET):
                        t, k = i * ET + u, u % 2
                        q = u % RING
                        now, before = acc[q], acc[(q - 1) % RING]
                        msg = psum[4 + k]
                        if kind == "mlp":
                            dve.wait_ge(turned, t + 1)
                            up_to(dve, hid_ready, t - 1)
                            dve.tensor_copy(xt[k][0:ED, C:2 * C], psum[6 + k][0:ED, 0:C]).then_inc(eat_ready, 1)
                        link.start(t)
                        up_to(dve, acc_ready, t, ACC)
                        up_to(dve, sent[q], i * 2 + u // RING, 16)
                        if kind != "gat" and kind != "mlp":
                            link(dve.tensor_scalar(run[0][:, :], before[:, 0:C], column(keep, t), None, ALU.mult))
                        dve.wait_ge(msg_ready, t + 1)
                        if kind == "mlp":
                            dve.scalar_tensor_tensor(now[:, 0:C], before[:, 0:C], column(keep, t), msg[:, 0:C],
                                                     ALU.mult, ALU.add).then_inc(acc_ready, 1)
                            dve.scalar_tensor_tensor(now[:, C:C + 1], before[:, C:C + 1], column(keep, t),
                                                     K["ones"][:, 0:1], ALU.mult, ALU.add).then_inc(acc_ready, 1)
                        elif kind == "bases":
                            for b in range(BASES):
                                cf = coef[:, bass.ds(t, 1), b]
                                o = run[(b + 1) % 2][:, :] if b + 1 < BASES else now[:, 0:C]
                                ins = dve.scalar_tensor_tensor(o, msg[:, b * C:(b + 1) * C], cf, run[b % 2][:, :],
                                                               ALU.mult, ALU.add)
                                if b + 1 < BASES:
                                    link(ins)
                                else:
                                    ins.then_inc(acc_ready, 1)
                        elif kind != "gat":
                            link(dve.scalar_tensor_tensor(run[1][:, :], msg[:, 0:C], column(eweight1, t), run[0][:, :],
                                                          ALU.mult, ALU.add))
                            dve.scalar_tensor_tensor(now[:, 0:C], msg[:, C:2 * C], column(eweight, t), run[1][:, :],
                                                     ALU.mult, ALU.add).then_inc(acc_ready, 1)
                        else:
                            e2, e, m_in = small[:, 0, :], small[:, 1, :], small[:, 2, :]
                            z = msg[:, C:C + HEADS]
                            link(dve.tensor_scalar(e2, z, 0.2, None, ALU.mult))
                            link(dve.tensor_tensor(e, z, e2, ALU.max))
                            link(dve.tensor_scalar(m_in, before[:, C + 4:C + 8], column(reset, t), None, ALU.add))
                            link(dve.tensor_tensor(now[:, C + 4:C + 8], m_in, e, ALU.max))
                            up_to(dve, part_ready, t - 1)
                            link(dve.tensor_tensor(diff[k][:, 1, :], e, now[:, C + 4:C + 8], ALU.subtract))
                            dve.tensor_tensor(diff[k][:, 0, :], m_in, now[:, C + 4:C + 8], ALU.subtract)\
                                .then_inc(diff_ready, 1)
                            dve.wait_ge(part_ready, t + 1)
                            old, new = part[k][:, 0, :], part[k][:, 1, :]
                            heads = lambda v: v.rearrange("p (h d) -> p h d", h=HEADS)
                            spread = lambda v: v.unsqueeze(2).to_broadcast([P, HEADS, HD])
                            link(dve.tensor_tensor(small[:, 3, :], before[:, C:C + 4], old, ALU.mult))
                            link(dve.tensor_tensor(now[:, C:C + 4], small[:, 3, :], new, ALU.add))
                            link(dve.tensor_tensor(heads(scaled[:, :]), heads(before[:, 0:C]), spread(old), ALU.mult))
                            link(dve.tensor_tensor(heads(weighed[:, :]), heads(msg[:, 0:C]), spread(new), ALU.mult))
                            dve.tensor_tensor(now[:, 0:C], scaled[:, :], weighed[:, :], ALU.add).then_inc(acc_ready, 1)
                    if kind == "mlp":
                        coefficients(i)

                edge_steps(dve, body)

        loaded, joined, copied, written, steps2 = s("seam_loaded"), s("seam_joined"), s("seam_copied"), s("seam_written"), s("seam_steps")
        spread_rows, exped = s("seam_rows"), s("seam_exp")
        c = ExitStack()
        with c:
            tail = acc[RING - 1]
            if two:
                sm = sb(f"{name}_sm", [P, 10, HEADS], c=c)
                mx = sb(f"{name}_mx", [P, HEADS, P], c=c)
                bc = sb(f"{name}_bc", [P, 2, HEADS, P], c=c)
                mask = {m: sb(f"{name}_mask_{m}", [P, P], c=c) for m in seam}
                tr = sb(f"{name}_tr", [P, W], c=c)
            block = c.enter_context(nc.Block())

            @block.sync
            def _(sp):
                sp.dma_start(hrow[:, :], head_rows).then_inc(loaded, 16)

            last = tr if two else tail
            width = C + 8 if not two else C + HEADS

            @block.tensor
            def _(pe):
                pe.wait_ge(loaded, 16)
                if two:
                    pe.wait_ge(spread_rows, 1)
                    for a in range(2):
                        for h in range(HEADS):
                            q = pe.matmul(psum[2 + a][:, h * P:(h + 1) * P], bc[:, a, h, :], K["ident"][:, :],
                                          start=True, stop=True)
                    q.then_inc(spread_rows, 1)
                    pe.wait_ge(exped, 2)
                pe.matmul(psum[0][:, 0:width], seam["tt"][:, :], last[:, 0:width], start=True, stop=False)
                pe.matmul(psum[0][:, 0:width], seam["ht"][:, :], hrow[:, 0:width],
                          start=False, stop=True).then_inc(joined, 1)

            @block.vector
            def _(dve):
                n = [0]

                def link(ins):
                    n[0] += 1
                    ins.then_inc(steps2, 1)
                    dve.wait_ge(steps2, n[0])

                if two:
                    heads = lambda v: v.rearrange("p (h d) -> p h d", h=HEADS)
                    spread = lambda v, k: v.unsqueeze(2).to_broadcast([P, HEADS, k])
                    dve.wait_ge(loaded, 16)
                    nosum, mh, mt = sm[:, 0, :], sm[:, 1, :], tail[:, C + 4:C + 8]
                    link(dve.tensor_scalar(nosum, hrow[:, C:C + 4], 0.0, -LOW, ALU.is_equal, ALU.mult))
                    link(dve.tensor_tensor(mh, hrow[:, C + 4:C + 8], nosum, ALU.add))
                    for m in seam:
                        link(dve.tensor_scalar(mask[m][:, :], seam[m][:, :], -1.0, LOW, ALU.add, ALU.mult))
                    link(dve.tensor_copy(bc[:, 0, :, :], spread(mt, P)))
                    dve.tensor_copy(bc[:, 1, :, :], spread(mh, P)).then_inc(spread_rows, 1)
                    dve.wait_ge(spread_rows, 2)
                    for a, (m_t, m_h) in enumerate((("tt", "th"), ("ht", "hh"))):
                        for b, m in enumerate((m_t, m_h)):
                            link(dve.tensor_tensor(mx[:, :, :], psum[2 + b][:, :].rearrange("p (h j) -> p h j", h=HEADS),
                                                   mask[m][:, :].unsqueeze(1).to_broadcast([P, HEADS, P]), ALU.add))
                            link(dve.tensor_reduce(sm[:, 2 + b, :], mx[:, :, :], AX.X, ALU.max))
                        link(dve.tensor_tensor(sm[:, 4 + a, :], sm[:, 2, :], sm[:, 3, :], ALU.max))
                    link(dve.tensor_tensor(sm[:, 6, :], mt, sm[:, 4, :], ALU.subtract))
                    dve.tensor_tensor(sm[:, 7, :], mh, sm[:, 5, :], ALU.subtract).then_inc(exped, 1)
                    dve.wait_ge(copied, 1)
                    ft, fh = sm[:, 8, :], sm[:, 9, :]
                    for o, i, f in ((tr, tail, ft), (hrow, hrow, fh)):
                        link(dve.tensor_tensor(heads(o[:, 0:C]), heads(i[:, 0:C]), spread(f, HD), ALU.mult))
                        ins = dve.tensor_tensor(o[:, C:C + 4], i[:, C:C + 4], f, ALU.mult)
                        if o is tr:
                            link(ins)
                        else:
                            ins.then_inc(exped, 1)
                    dve.wait_ge(joined, 1)
                    link(dve.tensor_copy(trow[:, C + 4:C + 8], sm[:, 4, :]))
                    link(dve.tensor_copy(hrow[:, C + 4:C + 8], sm[:, 5, :]))
                    dve.tensor_copy(trow[:, 0:width], psum[0][:, 0:width]).then_inc(copied, 1)
                else:
                    dve.wait_ge(joined, 1)
                    dve.tensor_copy(trow[:, 0:width], psum[0][:, 0:width]).then_inc(copied, 1)

            if two:
                @block.scalar
                def _(act):
                    act.wait_ge(exped, 1)
                    act.activation(sm[:, 8:10, :], sm[:, 6:8, :], ACT.Exp).then_inc(copied, 1)

            @block.gpsimd
            def _(pool):
                pool.wait_ge(copied, 2 if two else 1)
                pool.wait_ge(loaded, 16)
                for row, index in ((trow, t_index), (hrow, h_index)):
                    pool.indirect_dma_start(AGG, bass.IndirectOffsetOnAxis(ap=index[:, 0:1], axis=0), row[:, :], None,
                                            bounds_check=ROWS - 1, oob_is_err=False).then_inc(written, 16)
                pool.wait_ge(written, 32)

    def node_phase(name, kind, x_in, x_res, x_out):
        own = Phase(name)
        nodes(name, kind, x_in, x_res, x_out, own)
        own.end()

    def nodes(name, kind, x_in, x_res, x_out, s):
        x_got = [s(f"x_got{u}") for u in range(SLOTS)]
        a_got = [s(f"a_got{u}") for u in range(SLOTS)]
        stored = [s(f"stored{u}") for u in range(SLOTS)]
        turned, xt_ready, o_ready = s("turned"), s("xt_ready"), s("o_ready")
        a_done, y_ready, v_ready, r_ready, out_ready = s("a_done"), s("y_ready"), s("v_ready"), s("r_ready"), s("out_ready")
        xb_ready, a_scaled, at_ready, hid_ready, rt_ready = s("xb_ready"), s("a_scaled"), s("at_ready"), s("hid_ready"), s("rt_ready")
        n1_ready, y2_ready, v2_ready, r2_ready, step_sem, pool_steps = s("n1_ready"), s("y2_ready"), s("v2_ready"), s("r2_ready"), s("steps"), s("pool_steps")
        step_sem2, pool_steps2 = s("steps2"), s("pool_steps2")
        d_ready, e_ready, ea_done, xl_ready = s("d_ready"), s("e_ready"), s("ea_done"), s("xl_ready")
        c = ExitStack()
        with c:
            X = [sb(f"{name}_X{u}", [P, RB * C], c=c) for u in range(SLOTS)]
            A = [sb(f"{name}_A{u}", [P, RB * W], c=c) for u in range(SLOTS)]
            Y = [sb(f"{name}_Y{u}", [P, RB * C], c=c) for u in range(SLOTS)]
            B = [sb(f"{name}_B{u}", [P, RB * C], c=c) for u in range(SLOTS)]
            res = kind == "spline2"
            if res:
                R = [sb(f"{name}_R{u}", [P, RB * C], c=c) for u in range(SLOTS)]
            xt = [sb(f"{name}_xt{h}", [P, 512], c=c) for h in range(2)]
            mlp, gat, norm = kind == "mlp", kind == "gat", kind != "spline1"
            if mlp:
                at = [sb(f"{name}_at{h}", [P, 512], c=c) for h in range(2)]
                rt = [sb(f"{name}_rt{h}", [P, 512], c=c) for h in range(2)]
                L = [sb(f"{name}_L{u}", [P, RB * C], c=c) for u in range(SLOTS)]
            if gat:
                g_small = sb(f"{name}_gs", [P, 4, RB * HEADS], c=c)
                g_diff = [sb(f"{name}_gd{k}", [P, 2, RB * HEADS], c=c) for k in range(2)]
                g_exp = [sb(f"{name}_ge{k}", [P, 2, RB * HEADS], c=c) for k in range(2)]
            stat = [[sb(f"{name}_stat{q}{u}", [P, RB, 6], c=c) for u in range(SLOTS)] for q in range(2)]
            tmp = [sb(f"{name}_tmp{q}", [P, 5, RB], c=c) for q in range(2)]
            msum = [[sb(f"{name}_msum{q}{u}", [P, RB], c=c) for u in range(SLOTS)] for q in range(2)]
            var = [[sb(f"{name}_var{q}{u}", [P, RB], c=c) for u in range(SLOTS)] for q in range(2)]
            rstd = [[sb(f"{name}_rstd{q}{u}", [P, RB], c=c) for u in range(SLOTS)] for q in range(2)]
            shift = [[sb(f"{name}_shift{q}{u}", [P, RB], c=c) for u in range(SLOTS)] for q in range(2)]
            block = c.enter_context(nc.Block())
            rows3 = lambda t: t[:, :].rearrange("p (j f) -> p j f", j=RB)
            sums3 = lambda t: t[:, :].rearrange("p (j w) -> p j w", w=W)
            halves = lambda t, h: rows3(t)[:, 4 * h:4 * h + 4, :]
            bank3 = lambda b: psum[b][:, :].rearrange("p (j f) -> p j f", j=4)
            per_row = lambda r: r[:, :].unsqueeze(1).to_broadcast([P, RB, C])

            LAG = 3

            @block.sync
            def _(sp):
                def load(b, u, i):
                    up_to(sp, v_ready if norm else out_ready, b - SLOTS + 1 if not isinstance(b, int) or b >= SLOTS else 0)
                    if mlp:
                        up_to(sp, xl_ready, b - SLOTS + 1 if not isinstance(b, int) or b >= SLOTS else 0)
                    sp.dma_start(X[u][:, :], rows_of(x_in, b, C)).then_inc(x_got[u], 16)
                    sp.dma_start(A[u][:, :], rows_of(AGG, b, W)).then_inc(a_got[u], 16)
                    if res:
                        sp.dma_start(R[u][:, :], rows_of(x_res, b, C)).then_inc(x_got[u], 16)

                def store(b, u):
                    sp.wait_ge(out_ready, b + 1)
                    if isinstance(b, int) and b == BLOCKS - 1:
                        sp.wait_ge(stored[(u - 1) % SLOTS], 16 * ((b - 1) // SLOTS + 1))
                    sp.dma_start(rows_of(x_out, b, C), Y[u][:, :]).then_inc(stored[u], 16)

                def body(b, u, i):
                    load(b, u, i)
                    if not (isinstance(i, int) and i == 0 and u < LAG):
                        store(b - LAG, (u - LAG) % SLOTS)

                node_blocks(sp, body)
                for b in range(BLOCKS - LAG, BLOCKS):
                    store(b, b % SLOTS)
                for u in range(SLOTS):
                    sp.wait_ge(stored[u], 16 * ((BLOCKS - 1 - u) // SLOTS + 1))

            per_x = 32 if res else 16

            @block.gpsimd
            def _(pool):
                links = [Chain(pool, pool_steps, 2), Chain(pool, pool_steps2, 2)]

                def rstd_of(q, b, u):
                    link = links[q]
                    link.start(b)
                    pool.wait_ge((v_ready, v2_ready)[q], b + 1)
                    link(pool.tensor_tensor(rstd[q][u][:, :], var[q][u][:, :], half[:, :], ALU.pow))
                    link(pool.tensor_tensor(msum[q][u][:, :], msum[q][u][:, :], half[:, :], ALU.mult))
                    pool.tensor_tensor(shift[q][u][:, :], msum[q][u][:, :], rstd[q][u][:, :], ALU.mult)\
                        .then_inc((r_ready, r2_ready)[q], 1)

                def body(b, u, i):
                    first = isinstance(i, int) and i == 0
                    pool.wait_ge(x_got[u], (i + 1) * per_x)
                    bias = K[{"mlp": "bu2", "gat": "gbias", "rgcn": "bu2", "spline1": "sb1", "spline2": "sb2"}[kind]]
                    if kind != "rgcn" and kind != "spline1":
                        base = R if res else X
                        pool.tensor_tensor(rows3(B[u]), rows3(base[u]), per_row(bias), ALU.add).then_inc(xb_ready, 1)
                    if mlp:
                        up_to(pool, v2_ready, b - SLOTS + 1 if not isinstance(b, int) or b >= SLOTS else 0)
                        pool.tensor_tensor(rows3(L[u]), rows3(X[u]), per_row(K["ln_b"]), ALU.add).then_inc(xl_ready, 1)
                    if kind == "gat":
                        pool.wait_ge(ea_done, b + 1)
                        v = sums3(A[u])[:, :, 0:C].rearrange("p j (h d) -> p j h d", h=HEADS)
                        pool.tensor_tensor(v, v, g_small[:, 2, :].rearrange("p (j h) -> p j h", h=HEADS).unsqueeze(3)
                                           .to_broadcast([P, RB, HEADS, HD]), ALU.mult).then_inc(a_done, 1)
                    if norm:
                        rstd_of(0, b, u)
                        if mlp and not (first and u < 2):
                            rstd_of(1, b - 2, (u - 2) % SLOTS)

                node_blocks(pool, body)
                if mlp:
                    for b in range(BLOCKS - 2, BLOCKS):
                        rstd_of(1, b, b % SLOTS)

            @block.tensor
            def _(pe):
                def body(b, u, i):
                    pe.wait_ge(x_got[u], (i + 1) * per_x)
                    for h in range(2):
                        up_to(pe, xt_ready, (b - 1) * 2 + h + 1)
                        for j in range(4):
                            q = pe.transpose(psum[h][:, j * P:(j + 1) * P], X[u][:, (4 * h + j) * C:(4 * h + j + 1) * C],
                                             K["ident"][:, :])
                        q.then_inc(turned, 1)
                    if mlp:
                        pe.wait_ge(a_scaled, b + 1)
                        for h in range(2):
                            up_to(pe, at_ready, (b - 1) * 2 + h + 1)
                            for j in range(4):
                                q = pe.transpose(psum[2 + h][:, j * P:(j + 1) * P],
                                                 A[u][:, (4 * h + j) * W:(4 * h + j) * W + C], K["ident"][:, :])
                            q.then_inc(a_done, 1)
                        for h in range(2):
                            up_to(pe, rt_ready, (b - 1) * 2 + h + 1)
                            pe.wait_ge(xt_ready, b * 2 + h + 1)
                            pe.matmul(psum[4 + h][:, :], K["wu1x"][:, :], xt[h][:, :], start=True, stop=False)
                            pe.wait_ge(at_ready, b * 2 + h + 1)
                            pe.matmul(psum[4 + h][:, :], K["wu1a"][:, :], at[h][:, :], start=False, stop=True)\
                                .then_inc(hid_ready, 1)
                        lhs, w, lhs_ready, o = rt, K["wu2"][:, :], rt_ready, 6
                    else:
                        w = {"gat": K["wgat"][:, 0:C], "rgcn": K["loop"][:, :], "spline1": K["root1"][:, :],
                             "spline2": K["root2"][:, :]}[kind]
                        lhs, lhs_ready, o = xt, xt_ready, 6
                    for h in range(2):
                        pe.wait_ge(lhs_ready, b * 2 + h + 1)
                        up_to(pe, y_ready, (b - 1) * 2 + h + 1)
                        for j in range(4):
                            q = pe.matmul(psum[o + h][:, j * C:(j + 1) * C], lhs[h][:, j * P:(j + 1) * P], w,
                                          start=True, stop=True)
                            if gat:
                                if h == 0 and j == 0:
                                    up_to(pe, e_ready, b)
                                r = 4 * h + j
                                q = pe.matmul(psum[4][:, r * HEADS:(r + 1) * HEADS], lhs[h][:, j * P:(j + 1) * P],
                                              K["wself"][:, :], start=True, stop=True)
                        q.then_inc(o_ready, 1)

                node_blocks(pe, body)

            @block.scalar
            def _(act):
                def normalise(q, b, u, o, x, ready):
                    act.wait_ge((r_ready, r2_ready)[q], b + 1)
                    for j in range(RB):
                        ins = act.activation(o[u][:, j * C:(j + 1) * C], x[u][:, j * C:(j + 1) * C], ACT.Identity,
                                             bias=shift[q][u][:, j:j + 1], scale=rstd[q][u][:, j:j + 1])
                    ins.then_inc(ready, 1)

                def body(b, u, i):
                    first = isinstance(i, int) and i == 0
                    for h in range(2):
                        act.wait_ge(turned, b * 2 + h + 1)
                        up_to(act, hid_ready if mlp else o_ready, (b - 1) * 2 + h + 1)
                        act.activation(xt[h][:, :], psum[h][:, :], ACT.Copy).then_inc(xt_ready, 1)
                    if mlp:
                        for h in range(2):
                            act.wait_ge(a_done, b * 2 + h + 1)
                            act.activation(at[h][:, :], psum[2 + h][:, :], ACT.Copy).then_inc(at_ready, 1)
                        for h in range(2):
                            act.wait_ge(hid_ready, b * 2 + h + 1)
                            up_to(act, o_ready, (b - 1) * 2 + h + 1)
                            act.activation(rt[h][:, :], psum[4 + h][:, :], ACT.Relu, bias=bias_u[:, 0:1])\
                                .then_inc(rt_ready, 1)
                        if not (first and u < 1):
                            normalise(0, b - 1, (u - 1) % SLOTS, Y, Y, n1_ready)
                        if not (first and u < 3):
                            normalise(1, b - 3, (u - 3) % SLOTS, Y, Y, out_ready)
                    if gat:
                        act.wait_ge(d_ready, b + 1)
                        up_to(act, y_ready, b - 1, 2)
                        act.activation(g_exp[u % 2][:, :, :], g_diff[u % 2][:, :, :], ACT.Exp).then_inc(e_ready, 1)
                    if norm and not mlp and not (first and u < 2):
                        normalise(0, b - 2, (u - 2) % SLOTS, Y, Y, out_ready)

                node_blocks(act, body)
                if mlp:
                    normalise(0, BLOCKS - 1, (BLOCKS - 1) % SLOTS, Y, Y, n1_ready)
                    for b in range(BLOCKS - 3, BLOCKS):
                        normalise(1, b, b % SLOTS, Y, Y, out_ready)
                elif norm:
                    for b in range(BLOCKS - 2, BLOCKS):
                        normalise(0, b, b % SLOTS, Y, Y, out_ready)

            @block.vector
            def _(dve):
                link = Chain(dve, step_sem, {"mlp": 6, "gat": 16, "rgcn": 5, "spline1": 0, "spline2": 5}[kind])
                link2 = Chain(dve, step_sem2, 6)

                def statistics(link, q, b, u, y):
                    st = stat[q][u]
                    for j in range(RB):
                        ins = dve.bn_stats(st[:, j, :], y[:, j * C:(j + 1) * C])
                    link(ins)
                    s_, d_, dd, m2 = msum[q][u][:, :], tmp[q][:, 1, :], tmp[q][:, 2, :], tmp[q][:, 3, :]
                    me, mo, ve, vo = st[:, :, 1], st[:, :, 4], st[:, :, 2], st[:, :, 5]
                    dve.tensor_tensor(s_, me, mo, ALU.add)
                    dve.tensor_tensor(m2, ve, vo, ALU.add)
                    link(dve.tensor_tensor(d_, me, mo, ALU.subtract))
                    link(dve.tensor_tensor(dd, d_, d_, ALU.mult))
                    link(dve.scalar_tensor_tensor(m2, dd, C / 4.0, m2, ALU.mult, ALU.add))
                    dve.tensor_scalar(var[q][u][:, :], m2, 1.0 / C, LN_EPS, ALU.mult, ALU.add)\
                        .then_inc((v_ready, v2_ready)[q], 1)

                def second(b, u):
                    link2.start(b)
                    dve.wait_ge(n1_ready, b + 1)
                    link2(dve.tensor_tensor(rows3(Y[u]), rows3(Y[u]), per_row(K["ln_g"]), ALU.mult))
                    dve.wait_ge(xl_ready, b + 1)
                    link2(dve.tensor_tensor(Y[u][:, :], Y[u][:, :], L[u][:, :], ALU.add))
                    statistics(link2, 1, b, u, Y[u])

                def body(b, u, i):
                    first = isinstance(i, int) and i == 0
                    if link.per:
                        link.start(b)
                    dve.wait_ge(a_got[u], (i + 1) * 16)
                    up_to(dve, stored[u], i, 16)
                    if mlp:
                        iv = invdeg[:, bass.ds(b, 1), :]
                        link(dve.tensor_scalar(tmp[0][:, 0:1, :], sums3(A[u])[:, :, C:C + 1].rearrange("p j o -> p o j"),
                                               1.0, None, ALU.max))
                        link(dve.reciprocal(iv, tmp[0][:, 0:1, :]))
                        dve.tensor_tensor(sums3(A[u])[:, :, 0:C], sums3(A[u])[:, :, 0:C],
                                          iv.rearrange("p o j -> p (o j)").unsqueeze(2).to_broadcast([P, RB, C]),
                                          ALU.mult).then_inc(a_scaled, 1)
                        dve.wait_ge(xb_ready, b + 1)
                        for h in range(2):
                            dve.wait_ge(o_ready, b * 2 + h + 1)
                            dve.tensor_tensor(halves(Y[u], h), bank3(6 + h), halves(B[u], h), ALU.add).then_inc(y_ready, 1)
                        dve.wait_ge(y_ready, b * 2 + 2)
                        statistics(link, 0, b, u, Y[u])
                        if not (first and u < 2):
                            second(b - 2, (u - 2) % SLOTS)
                    elif gat:
                        k = u % 2
                        n_ = RB * HEADS
                        es, me = g_small[:, 0, :], g_small[:, 1, :]
                        by_row = lambda v: v.rearrange("p (j h) -> p j h", h=HEADS)
                        dve.wait_ge(o_ready, b * 2 + 2)
                        sc = psum[4][:, 0:n_]
                        link(dve.tensor_scalar(me, sc, 0.2, None, ALU.mult))
                        link(dve.tensor_tensor(es, sc, me, ALU.max))
                        s_e, m_e = sums3(A[u])[:, :, C:C + 4], sums3(A[u])[:, :, C + 4:C + 8]
                        link(dve.tensor_scalar(by_row(me), s_e, 0.0, -LOW, ALU.is_equal, ALU.mult))
                        link(dve.tensor_tensor(by_row(me), by_row(me), m_e, ALU.add))
                        link(dve.tensor_tensor(g_small[:, 3, :], me, es, ALU.max))
                        link(dve.tensor_tensor(g_diff[k][:, 0, :], me, g_small[:, 3, :], ALU.subtract))
                        dve.tensor_tensor(g_diff[k][:, 1, :], es, g_small[:, 3, :], ALU.subtract).then_inc(d_ready, 1)
                        dve.wait_ge(e_ready, b + 1)
                        ce, cs = g_exp[k][:, 0, :], g_exp[k][:, 1, :]
                        link(dve.tensor_tensor(by_row(es), s_e, by_row(ce), ALU.mult))
                        link(dve.tensor_tensor(es, es, cs, ALU.add))
                        link(dve.reciprocal(me, es))
                        up_to(dve, a_done, b)
                        dve.tensor_tensor(g_small[:, 2, :], ce, me, ALU.mult).then_inc(ea_done, 1)
                        link(dve.tensor_tensor(g_small[:, 3, :], cs, me, ALU.mult))
                        for h in range(2):
                            w4 = g_small[:, 3, h * 16:(h + 1) * 16]
                            dve.tensor_tensor(Y[u][:, h * 512:(h + 1) * 512].rearrange("p (q d) -> p q d", d=HD),
                                              psum[6 + h][:, :].rearrange("p (q d) -> p q d", d=HD),
                                              w4.unsqueeze(2).to_broadcast([P, 16, HD]), ALU.mult).then_inc(y_ready, 1)
                        dve.wait_ge(y_ready, b * 2 + 2)
                        dve.wait_ge(xb_ready, b + 1)
                        link(dve.tensor_tensor(Y[u][:, :], Y[u][:, :], B[u][:, :], ALU.add))
                        dve.wait_ge(a_done, b + 1)
                        link(dve.tensor_tensor(rows3(Y[u]), rows3(Y[u]), sums3(A[u])[:, :, 0:C], ALU.add))
                        statistics(link, 0, b, u, Y[u])
                    elif kind == "rgcn":
                        for h in range(2):
                            dve.wait_ge(o_ready, b * 2 + h + 1)
                            dve.tensor_tensor(halves(Y[u], h), bank3(6 + h), sums3(A[u])[:, 4 * h:4 * h + 4, 0:C],
                                              ALU.add).then_inc(y_ready, 1)
                        dve.wait_ge(y_ready, b * 2 + 2)
                        dve.wait_ge(x_got[u], (i + 1) * per_x)
                        link(dve.scalar_tensor_tensor(Y[u][:, :], Y[u][:, :], 0.0, X[u][:, :], ALU.max, ALU.add))
                        statistics(link, 0, b, u, Y[u])
                    else:
                        for j in range(RB):
                            h = j // 4
                            if j % 4 == 0:
                                dve.wait_ge(o_ready, b * 2 + h + 1)
                            ins = dve.scalar_tensor_tensor(
                                Y[u][:, j * C:(j + 1) * C], A[u][:, j * W:j * W + C],
                                invdeg[:, bass.ds(b, 1), j], psum[6 + h][:, (j % 4) * C:(j % 4 + 1) * C],
                                ALU.mult, ALU.add)
                            if j % 4 == 3:
                                ins.then_inc(y_ready, 1)
                        dve.wait_ge(y_ready, b * 2 + 2)
                        if kind == "spline1":
                            dve.tensor_tensor(rows3(Y[u]), rows3(Y[u]), per_row(K["sb1"]), ALU.add).then_inc(out_ready, 1)
                        else:
                            dve.wait_ge(xb_ready, b + 1)
                            link(dve.tensor_tensor(Y[u][:, :], Y[u][:, :], B[u][:, :], ALU.add))
                            statistics(link, 0, b, u, Y[u])

                node_blocks(dve, body)
                if mlp:
                    for b in range(BLOCKS - 2, BLOCKS):
                        second(b, b % SLOTS)

    edge_phase("e0", "mlp", D["x"])
    if upto < 1: return
    node_phase("n0", "mlp", D["x"], None, X1)
    if upto < 2: return
    edge_phase("e1", "gat", X1)
    if upto < 3: return
    node_phase("n1", "gat", X1, None, X2)
    if upto < 4: return
    edge_phase("e2", "bases", X2)
    node_phase("n2", "rgcn", X2, None, X3)
    if upto < 5: return
    edge_phase("e3", "spline1", X3)
    node_phase("n3", "spline1", X3, None, HT)
    if upto < 6: return
    edge_phase("e4", "spline2", HT)
    node_phase("n4", "spline2", HT, X3, out)



def _layout(x, src, dst, edge_attr_64, edge_type_64, edge_weight1, L0_gnn_global_state, L0_gnn_Wm1, L0_gnn_bm1,
            L0_gnn_Wm2, L0_gnn_bm2, L0_gnn_Wu1, L0_gnn_bu1, L0_gnn_Wu2, L0_gnn_bu2, L0_gnn_ln_g, L0_gnn_ln_b,
            L1_gnn_W, L1_gnn_att_src, L1_gnn_att_dst, L1_gnn_bias, L2_gnn_v_b, L2_gnn_a_rb, L2_gnn_loop_weight,
            L3_gnn_W1, L3_gnn_root1, L3_gnn_b1, L3_gnn_W2, L3_gnn_root2, L3_gnn_b2):
    import numpy as np

    def runs(a, fill):
        a = np.asarray(a)
        a = a.reshape(a.shape[0], -1)
        a = np.pad(a, ((0, P * TILES - a.shape[0]), (0, 0)), constant_values=fill)
        return a.reshape(P, -1)

    A = np.asarray
    wm1, wu1 = A(L0_gnn_Wm1), A(L0_gnn_Wu1)
    side = lambda w: A(w).transpose(1, 0, 2).reshape(C, -1)
    d = dict(x=A(x), src=runs(src, 0), dst=runs(dst, PAD_DST), etype=runs(edge_type_64, 0),
             eweight=runs(edge_weight1, 0), eattr=runs(edge_attr_64, 0),
             wm1x=wm1[:, :C].T, wm1e=wm1[:, C:C + ED].T, wm1g=wm1[:, C + ED:].T, wm2=A(L0_gnn_Wm2).T,
             wu1x=wu1[:, :C].T, wu1a=wu1[:, C:2 * C].T, wu1g=wu1[:, 2 * C:].T, wu2=A(L0_gnn_Wu2).T,
             gstate=A(L0_gnn_global_state).reshape(-1, 1), bm1=A(L0_gnn_bm1).reshape(-1, 1),
             bu1=A(L0_gnn_bu1).reshape(-1, 1), bm2=A(L0_gnn_bm2).reshape(1, -1), bu2=A(L0_gnn_bu2),
             ln_g=A(L0_gnn_ln_g), ln_b=A(L0_gnn_ln_b), wgat=A(L1_gnn_W), atts=A(L1_gnn_att_src).reshape(-1),
             attd=A(L1_gnn_att_dst).reshape(-1), gbias=A(L1_gnn_bias), vb=side(L2_gnn_v_b),
             arb=A(L2_gnn_a_rb).T.reshape(-1), loop=A(L2_gnn_loop_weight), sw1=side(L3_gnn_W1),
             root1=A(L3_gnn_root1), sb1=A(L3_gnn_b1), sw2=side(L3_gnn_W2), root2=A(L3_gnn_root2), sb2=A(L3_gnn_b2))
    return {k: np.ascontiguousarray(v) for k, v in d.items()}


def kernel(**inputs):
    import concourse.bacc as bacc
    from concourse.bass_utils import run_bass_kernel_spmd

    arrays = _layout(**inputs)
    nc = bacc.Bacc("TRN2", target_bir_lowering=False, num_devices=1)
    D = {k: nc.dram_tensor("in_" + k, v.shape, mybir.dt.from_np(v.dtype), kind="ExternalInput").ap()
         for k, v in arrays.items()}
    out = nc.dram_tensor("out_x", [N, C], F32, kind="ExternalOutput").ap()
    build(nc, D, out)
    r = run_bass_kernel_spmd(nc, [{"in_" + k: v for k, v in arrays.items()}], core_ids=[0])
    return r.results[0]["out_x"]
```

```python
from contextlib import ExitStack

import concourse.bass as bass
from concourse import mybir

F32 = mybir.dt.float32
BF16 = mybir.dt.bfloat16
I32 = mybir.dt.int32
ALU = mybir.AluOpType
ACT = mybir.ActivationFunctionType
AX = mybir.AxisListType

P = 128
C = 128
N = 100000
TILES = 392
RING = 7
ET = 2 * RING
ESTEPS = TILES // ET
ED = 64
RELS = 64
BASES = 4
HEADS = 4
HD = C // HEADS
RB = 8
BLOCK = P * RB
BLOCKS = -(-N // BLOCK)
W = 136
HEAD = N
ROWS = -(-(N + P) // BLOCK) * BLOCK
AWAY = float(1 << 22)
PAD_DST = 1 << 21
LOW = 1.0e30
LN_EPS = 1e-5
FIELDS = 4
SORT_COLS = 14


def up_to(eng, sem, count, per=1):
    if isinstance(count, int) and count <= 0:
        return
    eng.wait_ge(sem, count * per)


def edge_steps(eng, body):
    body(0)
    with eng.Fori(1, ESTEPS - 1) as i:
        body(i)
    body(ESTEPS - 1)


def pipeline(eng, slots, *stages):
    def turn(k, u, i):
        for lag, stage in stages:
            b = k - lag
            if not isinstance(b, int) or 0 <= b < BLOCKS:
                stage(b, (u - lag) % slots, i + (u - lag) // slots)

    furthest = max(lag for lag, _ in stages)
    start, stop = -(-(furthest + slots) // slots), BLOCKS // slots
    for k in range(start * slots):
        turn(k, k % slots, k // slots)
    with eng.Fori(start, stop) as i:
        for u in range(slots):
            turn(i * slots + u, u, i)
    for k in range(stop * slots, BLOCKS + furthest):
        turn(k, k % slots, k // slots)


def block_rows(block):
    return min(block * BLOCK, N - BLOCK) if isinstance(block, int) else block * BLOCK


def rows_of(table, block, width):
    return table[bass.ds(block_rows(block), BLOCK), :].rearrange("(p j) f -> p (j f)", p=P)


class Chain:

    def __init__(self, eng, sem, per):
        self.eng, self.sem, self.per, self.k, self.item = eng, sem, per, 0, 0

    def start(self, item):
        self.item, self.k = item, 0

    def __call__(self, instruction):
        self.k += 1
        assert self.k <= self.per
        instruction.then_inc(self.sem, 1)
        self.eng.wait_ge(self.sem, self.item * self.per + self.k)


def build(nc, D, out, upto=99):
    with ExitStack() as ctx:
        _build(nc, D, out, ctx, upto)


def _build(nc, D, out, ctx, upto):
    def sb(name, shape, dt=F32, c=ctx):
        return c.enter_context(nc.sbuf_tensor(name, shape, dt))

    def sem(name):
        return ctx.enter_context(nc.semaphore(name))

    class Phase:

        def __init__(self, name):
            self.name, self.sems = name, []

        def __call__(self, what):
            self.sems.append(nc.alloc_semaphore(name=f"{self.name}_{what}"))
            return self.sems[-1]

        def end(self):
            nc.all_engine_barrier()
            nc.clear_and_free_semaphores(self.sems)
            nc.all_engine_barrier()

    AGG = nc.dram_tensor("AGG", [ROWS, W], F32).ap()
    X1 = nc.dram_tensor("X1", [N, C], F32).ap()
    X2 = nc.dram_tensor("X2", [N, C], F32).ap()
    X3 = nc.dram_tensor("X3", [N, C], F32).ap()
    HT = nc.dram_tensor("HT", [N, C], F32).ap()
    head_rows = AGG[HEAD:HEAD + P, :]
    EDGES = nc.dram_tensor("EDGES", [P * TILES, FIELDS], I32).ap()
    ATTRS = nc.dram_tensor("ATTRS", [P * TILES, ED], F32).ap()

    K = {}
    for name in ("ident", "ones"):
        K[name] = sb(name, [P, P])
    wload = []
    def weight(name, rows, cols):
        K[name] = sb("w_" + name, [rows, cols])
        wload.append((K[name][:, :], D[name]))
    weight("wm1x", C, C); weight("wm1e", ED, C); weight("wm1g", 64, C)
    weight("wm2", C, C); weight("wu1x", C, C); weight("wu1a", C, C); weight("wu1g", 64, C)
    weight("wu2", C, C); weight("gstate", 64, 1); weight("bm1", C, 1); weight("bu1", C, 1)
    one3 = sb("one3", [3, P], BF16)
    bm2_parts = sb("bm2_parts", [3, C + 1], BF16)
    bu2_parts = sb("bu2_parts", [3, 4 * C], BF16)
    weight("vb", C, BASES * C); weight("loop", C, C)
    weight("sw1", C, 2 * C); weight("root1", C, C); weight("sw2", C, 2 * C); weight("root2", C, C)
    K["wgat"] = sb("w_gat", [C, C + HEADS])
    K["wdst"] = sb("w_dst", [C, HEADS])
    K["wself"] = sb("w_self", [C, HEADS])
    K["atts"] = sb("w_atts", [C, C]); K["attd"] = sb("w_attd", [C, C])
    K["arb"] = sb("w_arb", [P, BASES * RELS])
    for name in ("bm2", "bu2", "ln_g", "ln_b", "gbias", "sb1", "sb2"):
        K[name] = sb("r_" + name, [P, C])
    src = sb("src", [P, TILES], I32)
    dsti = sb("dsti", [P, TILES], I32)
    dst_gather = sb("dst_gather", [P, TILES], I32)
    target = sb("target", [P, TILES], I32)
    keep = sb("keep", [P, TILES])
    reset = sb("reset", [P, TILES])
    etype = sb("etype", [P, TILES])
    eweight = sb("eweight", [P, TILES])
    eweight1 = sb("eweight1", [P, TILES])
    coef = sb("coef", [P, TILES, BASES])
    invdeg = sb("invdeg", [P, BLOCKS, RB])
    bias_m = sb("bias_m", [C, 1])
    bias_u = sb("bias_u", [C, 1])
    half = sb("half", [P, RB])
    iota_r = sb("iota_r", [P, RELS])
    t_index = sb("t_index", [P, 1], I32)
    h_index = sb("h_index", [P, 1], I32)
    seam = {n: sb("seam_" + n, [P, P]) for n in ("tt", "th", "ht", "hh")}

    src_now = [sb(f"src_now{h}", [P, RING], I32) for h in range(2)]
    dst_now = [sb(f"dst_now{h}", [P, RING], I32) for h in range(2)]
    target_now = [sb(f"target_now{h}", [P, RING], I32) for h in range(2)]
    xs = [sb(f"xs{q}", [P, C]) for q in range(RING)]
    acc = [sb(f"acc{q}", [P, W]) for q in range(RING)]
    hrow = sb("hrow", [P, W])
    trow = sb("trow", [P, W])

    psum = [ctx.enter_context(nc.psum_tensor(f"bank{i}", [P, 512], F32)) for i in range(8)]

    dstf = sb("dstf", [P, TILES])
    etypei = sb("etypei", [P, TILES], I32)
    shift_up = sb("shift_up", [P, P])
    shift_down = sb("shift_down", [P, P])
    unsorted = sb("unsorted", [1, 1], I32)
    edges_in, made, order_steps, order_pe = sem("edges_in"), sem("made"), sem("order_steps"), sem("order_pe")
    with ExitStack() as c0:
        falls = sb("falls", [P, TILES], c=c0)
        ends = sb("ends", [P, 6], c=c0)
        block = c0.enter_context(nc.Block())

        @block.sync
        def _(sp):
            for o, i in ((src, D["src"]), (dsti, D["dst"]), (etypei, D["etype"]), (eweight, D["eweight"])):
                sp.dma_start(o[:, :], i).then_inc(edges_in, 16)

        @block.gpsimd
        def _(pool):
            mats = ((K["ident"], 0), (shift_up, -1), (shift_down, 1))
            for m, _ in mats:
                pool.memset(m[:, :], 0.0).then_inc(made, 1)
            pool.wait_ge(made, 3)
            for m, base in mats:
                pool.affine_select(out=m[:, :], in_=m[:, :], compare_op=ALU.not_equal, fill=1.0,
                                   base=base, pattern=[[-1, P]], channel_multiplier=1).then_inc(made, 1)

        @block.vector
        def _(dve):
            n = [0]

            def link(ins):
                n[0] += 1
                ins.then_inc(order_steps, 1)
                dve.wait_ge(order_steps, n[0])

            link(dve.memset(K["ones"][:, :], 1.0))
            dve.wait_ge(edges_in, 64)
            link(dve.tensor_copy(dstf[:, :], dsti[:, :]))
            link(dve.memset(ends[:, 1:2], 1.0))
            link(dve.tensor_copy(ends[:, 0:1], dstf[:, 0:1]))
            dve.wait_ge(order_pe, 1)
            link(dve.tensor_tensor(falls[:, 1:], dstf[:, :-1], dstf[:, 1:], ALU.is_gt))
            link(dve.tensor_tensor(falls[:, 0:1], dstf[:, TILES - 1:], psum[0][:, 0:1], ALU.is_gt))
            link(dve.tensor_tensor(falls[:, 0:1], falls[:, 0:1], psum[0][:, 1:2], ALU.mult))
            link(dve.tensor_reduce(ends[:, 2:3], falls[:, :], AX.X, ALU.add))
            dve.wait_ge(order_pe, 2)
            link(dve.tensor_copy(unsorted[:, :], psum[1][0:1, 0:1]))

        @block.tensor
        def _(pe):
            pe.wait_ge(made, 6)
            pe.wait_ge(order_steps, 4)
            pe.matmul(psum[0][:, 0:2], shift_up[:, :], ends[:, 0:2], start=True, stop=True).then_inc(order_pe, 1)
            pe.wait_ge(order_steps, 8)
            pe.matmul(psum[1][0:1, 0:1], ends[:, 2:3], K["ones"][:, 0:1], start=True, stop=True).then_inc(order_pe, 1)

    sorting = Phase("sort")
    with ExitStack() as c0:
        steps, on, sent_rows, row_in = sorting("steps"), sorting("on"), sorting("sent_rows"), sorting("row_in")
        iotas, counted, ranked, now_ready = sorting("iotas"), sorting("counted"), sorting("ranked"), sorting("now_ready")
        row = sb("sort_row", [P, TILES], c=c0)
        bound = sb("sort_bound", [P, TILES], c=c0)
        rank = sb("sort_rank", [P, TILES], c=c0)
        ranki = sb("sort_ranki", [P, TILES], I32, c0)
        grid = sb("sort_grid", [P, SORT_COLS, TILES], c=c0)
        counts = sb("sort_counts", [P, SORT_COLS], c=c0)
        earlier = sb("sort_earlier", [P, SORT_COLS, TILES], c=c0)
        tile_no = sb("sort_tile_no", [P, TILES], c=c0)
        runs_ = sb("sort_runs", [P, P], c=c0)
        packed = sb("sort_packed", [P, TILES * FIELDS], I32, c0)
        now = sb("sort_now", [P, 1], I32, c0)
        now_fields = sb("sort_fields", [P, FIELDS], I32, c0)
        now_attrs = sb("sort_attrs", [P, ED], c=c0)
        rowi = sb("sort_rowi", [P, TILES], I32, c0)
        block = c0.enter_context(nc.Block())

        @block.gpsimd
        def _(pool):
            def settle(sem_, value):
                pool.wait_ge(sem_, value)
                pool.sem_inc(on, 1)

            n_unsorted = pool.value_load(unsorted[0:1, 0:1], min_val=0, max_val=P * TILES)
            with pool.If(n_unsorted > 0):
                pool.iota(tile_no[:, :], [[1, TILES]], base=0, channel_multiplier=0,
                          allow_small_or_imprecise_dtypes=True).then_inc(iotas, 1)
                pool.iota(runs_[:, :], [[1, P]], base=0, channel_multiplier=-1,
                          allow_small_or_imprecise_dtypes=True).then_inc(iotas, 1)
                with pool.Fori(0, P) as r:
                    pool.dma_start(rowi[:, :], D["dst"][bass.ds(r, 1), :].to_broadcast([P, TILES])).then_inc(row_in, 16)
                    settle(counted, r + 1)
                settle(ranked, 1)
                with pool.Fori(0, TILES) as t:
                    pool.dma_start(now_attrs[:, :], D["eattr"][:, bass.ds(t * ED, ED)]).then_inc(row_in, 16)
                    pool.tensor_copy(now[:, :], ranki[:, bass.ds(t, 1)]).then_inc(now_ready, 1)
                    pool.tensor_copy(now_fields[:, :], packed[:, bass.ds(t * FIELDS, FIELDS)]).then_inc(now_ready, 1)
                    settle(now_ready, t * 2 + 2)
                    settle(row_in, t * 16 + (16 * P + 16))
                    at = bass.IndirectOffsetOnAxis(ap=now[:, 0:1], axis=0)
                    pool.indirect_dma_start(EDGES, at, now_fields[:, :], None).then_inc(sent_rows, 16)
                    pool.indirect_dma_start(ATTRS, at, now_attrs[:, :], None).then_inc(sent_rows, 16)
                    settle(sent_rows, t * 32 + 32)
                pool.dma_start(packed[:, :], EDGES.rearrange("(p t) f -> p (t f)", p=P)).then_inc(sent_rows, 16)
            with pool.Else():
                pool.sem_inc(on, 1)

        @block.vector
        def _(dve):
            n = [0]

            def link(ins):
                n[0] += 1
                ins.then_inc(steps, 1)
                dve.wait_ge(steps, n[0])

            own = lambda t, cols: t[:, cols].unsqueeze(2).to_broadcast([P, SORT_COLS, TILES])
            all_ = lambda t: t[:, :].unsqueeze(1).to_broadcast([P, SORT_COLS, TILES])
            fields = packed[:, :].rearrange("p (t f) -> p t f", f=FIELDS)
            n_unsorted = dve.value_load(unsorted[0:1, 0:1], min_val=0, max_val=P * TILES)
            with dve.If(n_unsorted > 0):
                dve.wait_ge(iotas, 2)
                link(dve.tensor_scalar(runs_[:, :], runs_[:, :], 0.0, -0.5, ALU.is_lt, ALU.add))
                for g in range(TILES // SORT_COLS):
                    cols = slice(g * SORT_COLS, (g + 1) * SORT_COLS)
                    link(dve.tensor_tensor(grid[:, :, :], all_(dstf), own(dstf, cols), ALU.is_equal))
                    link(dve.tensor_tensor(earlier[:, :, :], all_(tile_no), own(tile_no, cols), ALU.is_lt))
                    link(dve.tensor_tensor(grid[:, :, :], grid[:, :, :], earlier[:, :, :], ALU.mult))
                    link(dve.tensor_reduce(rank[:, cols], grid[:, :, :], AX.X, ALU.add))
                before = n[0]
                per = 2 + 3 * (TILES // SORT_COLS)
                with dve.Fori(0, P) as r:
                    k = [0]

                    def link_r(ins):
                        k[0] += 1
                        ins.then_inc(steps, 1)
                        dve.wait_ge(steps, r * per + (before + k[0]))

                    dve.wait_ge(row_in, r * 16 + 16)
                    link_r(dve.tensor_copy(row[:, :], rowi[:, :]))
                    link_r(dve.tensor_scalar(bound[:, :], dstf[:, :], runs_[:, bass.ds(r, 1)], None, ALU.add))
                    for g in range(TILES // SORT_COLS):
                        cols = slice(g * SORT_COLS, (g + 1) * SORT_COLS)
                        link_r(dve.tensor_tensor(grid[:, :, :], all_(row), own(bound, cols), ALU.is_lt))
                        link_r(dve.tensor_reduce(counts[:, :], grid[:, :, :], AX.X, ALU.add))
                        link_r(dve.tensor_tensor(rank[:, cols], rank[:, cols], counts[:, :], ALU.add))
                    dve.sem_inc(counted, 1)
                n[0] = before + P * per
                link(dve.tensor_copy(ranki[:, :], rank[:, :]))
                for f, t in enumerate((src, dsti, etypei, eweight)):
                    link(dve.tensor_copy(fields[:, :, f], t[:, :].bitcast(I32) if t is eweight else t[:, :]))
                dve.sem_inc(ranked, 1)
                dve.wait_ge(sent_rows, 32 * TILES + 16)
                for f, t in enumerate((src, dsti, etypei, eweight)):
                    link(dve.tensor_copy(t[:, :].bitcast(I32) if t is eweight else t[:, :], fields[:, :, f]))
                link(dve.tensor_copy(dstf[:, :], dsti[:, :]))
            with dve.Else():
                dve.sem_inc(on, 1)
    sorting.end()

    w_in, const_done = sem("w_in"), sem("const_done")
    prep, prep_pe, zeroed, iota_done, cols_ready = sem("prep"), sem("prep_pe"), sem("zeroed"), sem("iota_done"), sem("cols_ready")
    with ExitStack() as c0:
        ZB = 7
        zero = sb("zero", [P, RB * W], c=c0)
        tf = [sb(f"tf{i}", [P, TILES], c=c0) for i in range(4)]
        cols = sb("cols", [P, 12], c=c0)
        hrf = sb("hrf", [P, 1], c=c0)
        rounded = sb("rounded", [3, C], BF16, c0)
        block = c0.enter_context(nc.Block())
        row_loads = [(K[n], D[n]) for n in ("bm2", "bu2", "ln_g", "ln_b", "gbias", "sb1", "sb2", "atts", "attd", "arb")]
        n_w = len(wload) + 1 + len(row_loads)

        @block.sync
        def _(sp):
            for o, i in wload:
                sp.dma_start(o, i).then_inc(w_in, 16)
            sp.dma_start(K["wgat"][:, 0:C], D["wgat"]).then_inc(w_in, 16)
            for o, i in row_loads:
                sp.dma_start(o[:, :], i.partition_broadcast(P)).then_inc(w_in, 16)

        @block.scalar
        def _(act):
            act.wait_ge(const_done, 1)
            dst = AGG.rearrange("(b p j) f -> p b (j f)", p=P, j=RB)
            for b in range(0, ROWS // BLOCK, ZB):
                act.dma_start(dst[:, b:b + ZB, :],
                              zero[:, :].unsqueeze(1).to_broadcast([P, ZB, RB * W])).then_inc(zeroed, 16)
            act.wait_ge(zeroed, 16 * (ROWS // BLOCK // ZB))

        @block.gpsimd
        def _(pool):
            pool.iota(iota_r[:, :], [[1, RELS]], base=0, channel_multiplier=0,
                      allow_small_or_imprecise_dtypes=True).then_inc(iota_done, 1)
            pool.iota(hrf[:, :], [[0, 1]], base=HEAD, channel_multiplier=1,
                      allow_small_or_imprecise_dtypes=True).then_inc(iota_done, 1)

        @block.vector
        def _(dve):
            n = [0]

            def link(ins):
                n[0] += 1
                ins.then_inc(prep, 1)
                dve.wait_ge(prep, n[0])

            nc.vector.memset(zero[:, :], 0.0).then_inc(const_done, 1)
            for u in range(RING):
                link(dve.memset(acc[u][:, :], 0.0))
            link(dve.memset(half[:, :], -0.5))
            link(dve.memset(one3[:, :], 1.0))
            inhead, notend, a, b = [t[:, :] for t in tf]
            link(dve.tensor_copy(etype[:, :], etypei[:, :]))
            link(dve.tensor_scalar(eweight1[:, :], eweight[:, :], -1.0, 1.0, ALU.mult, ALU.add))
            link(dve.tensor_scalar(a, dstf[:, :], float(N - 1), None, ALU.min))
            link(dve.tensor_copy(dst_gather[:, :], a))
            link(dve.memset(keep[:, 0:1], 0.0))
            link(dve.tensor_tensor(keep[:, 1:], dstf[:, 1:], dstf[:, :-1], ALU.is_equal))
            link(dve.tensor_scalar(reset[:, :], keep[:, :], -1.0, LOW, ALU.add, ALU.mult))
            link(dve.tensor_scalar(inhead, dstf[:, :], dstf[:, 0:1], None, ALU.is_equal))
            link(dve.memset(tf[1][:, TILES - 1:], 1.0))
            link(dve.tensor_copy(tf[1][:, 0:TILES - 1], keep[:, 1:]))
            dve.wait_ge(iota_done, 2)
            link(dve.tensor_scalar(a, dstf[:, :], -1.0, hrf[:, 0:1], ALU.mult, ALU.add))
            link(dve.tensor_tensor(a, a, inhead, ALU.mult))
            link(dve.tensor_tensor(a, a, dstf[:, :], ALU.add))
            link(dve.scalar_tensor_tensor(b, notend, AWAY, a, ALU.mult, ALU.add))
            link(dve.tensor_copy(target[:, :], b))
            df, dl, e1, e2, dl1, pl, nl = [cols[:, k:k + 1] for k in range(7)]
            link(dve.tensor_copy(df, dstf[:, 0:1]))
            link(dve.tensor_copy(dl, dstf[:, TILES - 1:]))
            dve.tensor_scalar(dl1, dl, 1.0, None, ALU.add).then_inc(cols_ready, 1)
            dve.wait_ge(prep_pe, 1)
            link(dve.tensor_scalar(pl, psum[2][:, 0:1], -1.0, None, ALU.add))
            link(dve.tensor_scalar(nl, psum[2][:, 1:2], -1.0, None, ALU.add))
            link(dve.tensor_tensor(e1, dl, nl, ALU.is_equal))
            link(dve.scalar_tensor_tensor(e2, e1, AWAY, dl, ALU.mult, ALU.add))
            link(dve.tensor_copy(t_index[:, :], e2))
            link(dve.tensor_tensor(e1, df, pl, ALU.is_equal))
            link(dve.tensor_tensor(e1, e1, tf[0][:, TILES - 1:], ALU.max))
            link(dve.scalar_tensor_tensor(e2, e1, AWAY, df, ALU.mult, ALU.add))
            link(dve.tensor_copy(h_index[:, :], e2))
            link(dve.tensor_scalar(seam["tt"][:, :], K["ones"][:, :], dl, None, ALU.mult))
            dve.tensor_scalar(seam["hh"][:, :], K["ones"][:, :], df, None, ALU.mult).then_inc(cols_ready, 1)
            dve.wait_ge(prep_pe, 2)
            link(dve.tensor_scalar(seam["th"][:, :], psum[0][:, 128:256], dl, None, ALU.is_equal))
            link(dve.tensor_scalar(seam["ht"][:, :], psum[0][:, 0:128], df, None, ALU.is_equal))
            link(dve.tensor_scalar(seam["tt"][:, :], psum[0][:, 0:128], dl, None, ALU.is_equal))
            link(dve.tensor_scalar(seam["hh"][:, :], psum[0][:, 128:256], df, None, ALU.is_equal))
            dve.wait_ge(w_in, 16 * n_w)
            link(dve.tensor_copy(bm2_parts[:, C:], K["ident"][0:3, 0:1]))
            for bias, o in ((K["bm2"], [bm2_parts[:, 0:C]]), (K["bu2"], [bu2_parts[:, j * C:(j + 1) * C] for j in range(4)])):
                rest, part, whole = [t[0:3, 0:C] for t in tf[0:3]]
                link(dve.tensor_copy(rest, bias[0:3, :]))
                link(dve.memset(whole, 0.0))
                for k in range(3):
                    link(dve.tensor_copy(rounded[:, :], rest))
                    link(dve.tensor_copy(part, rounded[:, :]))
                    link(dve.scalar_tensor_tensor(whole, part, K["ident"][0:3, k:k + 1], whole, ALU.mult, ALU.add))
                    link(dve.tensor_tensor(rest, rest, part, ALU.subtract))
                for o_ in o:
                    link(dve.tensor_copy(o_, whole))
            for name, o in (("atts", K["wgat"][:, C:]), ("attd", K["wdst"][:, :])):
                link(dve.tensor_tensor(K[name][:, :], K["wgat"][:, 0:C], K[name][:, :], ALU.mult))
                link(dve.tensor_reduce(o, K[name][:, :].rearrange("p (h d) -> p h d", h=HEADS), AX.X, ALU.add))
            link(dve.tensor_tensor(K["wself"][:, :], K["wgat"][:, C:], K["wdst"][:, :], ALU.add))
            dve.wait_ge(prep_pe, 3)
            link(dve.tensor_tensor(bias_m[:, :], K["bm1"][:, :], psum[1][:, 0:1], ALU.add))
            link(dve.tensor_tensor(bias_u[:, :], K["bu1"][:, :], psum[1][:, 1:2], ALU.add))

        @block.tensor
        def _(pe):
            pe.wait_ge(cols_ready, 1)
            pe.matmul(psum[2][:, 0:1], shift_down[:, :], cols[:, 4:5], start=True, stop=True)
            pe.matmul(psum[2][:, 1:2], shift_up[:, :], cols[:, 4:5], start=True, stop=True).then_inc(prep_pe, 1)
            pe.wait_ge(cols_ready, 2)
            pe.matmul(psum[0][:, 0:128], seam["tt"][:, :], K["ident"][:, :], start=True, stop=True)
            pe.matmul(psum[0][:, 128:256], seam["hh"][:, :], K["ident"][:, :],
                      start=True, stop=True).then_inc(prep_pe, 1)
            pe.wait_ge(w_in, 16 * n_w)
            pe.matmul(psum[1][:, 0:1], K["wm1g"][:, :], K["gstate"][:, :], start=True, stop=True)
            pe.matmul(psum[1][:, 1:2], K["wu1g"][:, :], K["gstate"][:, :],
                      start=True, stop=True).then_inc(prep_pe, 1)

    def edge_phase(name, kind, table):
        own = Phase(name)
        edges(name, kind, table, own)
        own.end()

    def edges(name, kind, table, s):
        two = kind == "gat"
        got = [s(f"got{q}") for q in range(RING)]
        sent = [s(f"sent{q}") for q in range(RING)]
        idx_ready, pool_on = s("idx_ready"), s("pool_on")
        turned, xt_ready = s("turned"), s("xt_ready")
        acc_ready, msg_ready = s("acc_ready"), s("msg_ready")
        c = ExitStack()
        with c:
            xt = [sb(f"{name}_xt{k}", [P, 2 * C], c=c) for k in range(2)]
            if two:
                xd = [sb(f"{name}_xd{q}", [P, C], c=c) for q in range(RING)]
                small = sb(f"{name}_small", [P, 8, HEADS], c=c)
                diff = [sb(f"{name}_diff{k}", [P, 2, HEADS], c=c) for k in range(2)]
                part = [sb(f"{name}_part{k}", [P, 2, HEADS], c=c) for k in range(2)]
                scaled = sb(f"{name}_scaled", [P, C], c=c)
                weighed = sb(f"{name}_weighed", [P, C], c=c)
                diff_ready, part_ready = s("diff_ready"), s("part_ready")
            if kind == "mlp":
                ea = [sb(f"{name}_ea{h}", [P, ET // 2 * ED], c=c) for h in range(2)]
                zt = [sb(f"{name}_zt{k}", [P, C], c=c) for k in range(2)]
                onehot = sb(f"{name}_onehot", [P, ET, RELS], c=c)
                prod = sb(f"{name}_prod", [P, ET, RELS], c=c)
                ea_got = [s(f"ea_got{h}") for h in range(2)]
                eat_ready, hid_ready, zt_ready = s("eat_ready"), s("hid_ready"), s("zt_ready")
            step_sem = s("dve_steps")
            msg_read = s("msg_read") if kind == "bases" else acc_ready
            run = [sb(f"{name}_run{k}", [P, C], c=c) for k in range(2)]
            block = c.enter_context(nc.Block())
            LAG = 1 if kind == "mlp" else 0
            LAG_SUM = 2 if kind == "mlp" else 0

            if kind == "mlp":
                @block.sync
                def _(sp):
                    def load_from(attributes):
                        def body(i):
                            for h in range(2):
                                up_to(sp, turned, i * ET - ET + (h + 1) * RING if not isinstance(i, int) or i else 0)
                                sp.dma_start(ea[h][:, :], attributes[:, bass.ds(i * (ET * ED) + h * (RING * ED), RING * ED)])\
                                  .then_inc(ea_got[h], 16)

                        edge_steps(sp, body)

                    n_unsorted = sp.value_load(unsorted[0:1, 0:1], min_val=0, max_val=P * TILES)
                    with sp.If(n_unsorted > 0):
                        load_from(ATTRS.rearrange("(p t) d -> p (t d)", p=P))
                    with sp.Else():
                        load_from(D["eattr"])

            @block.gpsimd
            def _(pool):
                def gather(h, q):
                    pool.indirect_dma_start(xs[q][:, :], None, table, bass.IndirectOffsetOnAxis(
                        ap=src_now[h][:, q:q + 1], axis=0)).then_inc(got[q], 16)
                    if two:
                        pool.indirect_dma_start(xd[q][:, :], None, table, bass.IndirectOffsetOnAxis(
                            ap=dst_now[h][:, q:q + 1], axis=0)).then_inc(got[q], 16)

                def copy_index(o, table_, t):
                    pool.tensor_copy(o[:, :], table_[:, bass.ds(t, RING)]).then_inc(idx_ready, 1)

                per = 3 if two else 2

                copy_index(src_now[0], src, 0)
                if two:
                    copy_index(dst_now[0], dst_gather, 0)
                pool.wait_ge(idx_ready, per - 1)
                for q in range(RING):
                    gather(0, q)

                def body(i):
                    for h in range(2):
                        last = isinstance(i, int) and i == ESTEPS - 1 and h == 1
                        for q in range(RING):
                            t = i * ET + h * RING + q
                            pool.wait_ge(acc_ready, t + 1)
                            pool.sem_inc(pool_on, 1)
                            if q == 0:
                                copy_index(target_now[h], target, t)
                                if not last:
                                    copy_index(src_now[1 - h], src, t + RING)
                                    if two:
                                        copy_index(dst_now[1 - h], dst_gather, t + RING)
                                pool.wait_ge(idx_ready, per - 1 + (i * 2 + h) * per + (1 if last else per))
                                pool.sem_inc(pool_on, 1)
                            pool.indirect_dma_start(AGG, bass.IndirectOffsetOnAxis(ap=target_now[h][:, q:q + 1], axis=0),
                                                    acc[q][:, :], None, bounds_check=ROWS - 1, oob_is_err=False)\
                                .then_inc(sent[q], 16)
                            if not last:
                                gather(1 - h, q)

                edge_steps(pool, body)
                for q in range(RING):
                    pool.wait_ge(sent[q], 16 * 2 * ESTEPS)

            per_got = 32 if two else 16

            @block.tensor
            def _(pe):
                def turn(i, u, t):
                    k, q = u % 2, u % RING
                    pe.wait_ge(got[q], (i * 2 + u // RING + 1) * per_got)
                    up_to(pe, xt_ready, t - 1)
                    if kind == "mlp":
                        up_to(pe, eat_ready, t - 1)
                        pe.wait_ge(ea_got[u // (ET // 2)], (i + 1) * 16)
                        v = u % (ET // 2)
                        pe.transpose(psum[k][:, 0:C], xs[q][:, :], K["ident"][:, :])
                        pe.transpose(psum[6 + k][0:ED, 0:C], ea[u // (ET // 2)][:, v * ED:(v + 1) * ED],
                                     K["ident"][:, :]).then_inc(turned, 1)
                    elif two:
                        pe.transpose(psum[k][:, 0:C], xs[q][:, :], K["ident"][:, :])
                        pe.transpose(psum[k][:, C:2 * C], xd[q][:, :], K["ident"][:, :]).then_inc(turned, 1)
                    else:
                        pe.transpose(psum[k][:, 0:C], xs[q][:, :], K["ident"][:, :]).then_inc(turned, 1)

                def hidden(u, t):
                    k = u % 2
                    pe.wait_ge(xt_ready, t + 1)
                    pe.wait_ge(eat_ready, t + 1)
                    up_to(pe, zt_ready, t - 1)
                    pe.matmul(psum[2 + k][:, 0:C], K["wm1x"][:, :], xt[k][:, 0:C], start=True, stop=False)
                    pe.matmul(psum[2 + k][:, 0:C], K["wm1e"][:, :], xt[k][0:ED, C:2 * C],
                              start=False, stop=True).then_inc(hid_ready, 1)

                def message(u, t):
                    k = u % 2
                    x_t = xt[k]
                    pe.wait_ge(zt_ready if kind == "mlp" else xt_ready, t + 1)
                    up_to(pe, msg_read, t - 1)
                    if kind == "mlp":
                        pe.matmul(psum[4 + k][:, 0:C + 1], one3[:, :], bm2_parts[:, :], start=True, stop=False)
                        pe.matmul(psum[4 + k][:, 0:C], zt[k][:, :], K["wm2"][:, :],
                                  start=False, stop=True).then_inc(msg_ready, 1)
                    elif two:
                        pe.matmul(psum[4 + k][:, 0:C + HEADS], x_t[:, 0:C], K["wgat"][:, :], start=True, stop=False)
                        pe.matmul(psum[4 + k][:, C:C + HEADS], x_t[:, C:2 * C], K["wdst"][:, :],
                                  start=False, stop=True).then_inc(msg_ready, 1)
                    else:
                        w = K["vb"] if kind == "bases" else K["sw1"] if kind == "spline1" else K["sw2"]
                        n = BASES * C if kind == "bases" else 2 * C
                        pe.matmul(psum[4 + k][:, 0:n], x_t[:, 0:C], w[:, :], start=True, stop=True).then_inc(msg_ready, 1)

                turn(0, 0, 0)

                def body(i):
                    for u in range(ET):
                        t = i * ET + u
                        if u + 1 < ET:
                            turn(i, u + 1, t + 1)
                        elif not (isinstance(i, int) and i == ESTEPS - 1):
                            turn(i + 1, 0, t + 1)
                        if kind == "mlp":
                            hidden(u, t)
                        if not (isinstance(t, int) and t < LAG):
                            message(u - LAG, t - LAG)

                edge_steps(pe, body)
                if LAG:
                    message(ET - 1, TILES - 1)

            @block.scalar
            def _(act):
                def relu(u, t):
                    k = u % 2
                    act.wait_ge(hid_ready, t + 1)
                    up_to(act, msg_ready, t - 1)
                    act.activation(zt[k][:, :], psum[2 + k][:, 0:C], ACT.Relu,
                                   bias=bias_m[:, 0:1]).then_inc(zt_ready, 1)

                def body(i):
                    for u in range(ET):
                        t, k = i * ET + u, u % 2
                        act.wait_ge(turned, t + 1)
                        up_to(act, hid_ready if kind == "mlp" else msg_ready, t - 1)
                        n = 2 * C if two else C
                        act.activation(xt[k][:, 0:n], psum[k][:, 0:n], ACT.Copy).then_inc(xt_ready, 1)
                        if kind == "mlp" and not (isinstance(t, int) and t < LAG):
                            relu(u - LAG, t - LAG)
                        if two:
                            act.wait_ge(diff_ready, t + 1)
                            up_to(act, acc_ready, t - 1)
                            act.activation(part[k][:, :, :], diff[k][:, :, :], ACT.Exp).then_inc(part_ready, 1)

                edge_steps(act, body)
                if LAG:
                    relu(ET - 1, TILES - 1)

            @block.vector
            def _(dve):
                steps = {"mlp": 10, "gat": 9, "bases": 3, "spline1": 2, "spline2": 2}[kind]
                link = Chain(dve, step_sem, steps)

                def column(tensor, t):
                    return tensor[:, bass.ds(t, 1)]

                def coefficients(i, n):
                    lo = bass.ds(i * ET, ET)
                    b = (n - 1) // 2
                    link.start(i)
                    link.k = n
                    if n == 0:
                        link(dve.tensor_tensor(onehot[:, :, :], etype[:, lo].unsqueeze(2).to_broadcast([P, ET, RELS]),
                                               iota_r[:, :].unsqueeze(1).to_broadcast([P, ET, RELS]), ALU.is_equal))
                    elif n == 9:
                        link(dve.tensor_tensor(coef[:, lo, :], coef[:, lo, :],
                                               eweight[:, lo].unsqueeze(2).to_broadcast([P, ET, BASES]), ALU.mult))
                    elif n % 2:
                        link(dve.tensor_tensor(prod[:, :, :], onehot[:, :, :], K["arb"][:, b * RELS:(b + 1) * RELS]
                                               .unsqueeze(1).to_broadcast([P, ET, RELS]), ALU.mult))
                    else:
                        link(dve.tensor_reduce(coef[:, lo, b], prod[:, :, :], AX.X, ALU.add))

                def body(i):
                    for u in range(ET):
                        t, k = i * ET + u, u % 2
                        if kind == "mlp":
                            dve.wait_ge(turned, t + 1)
                            up_to(dve, hid_ready, t - 1)
                            dve.tensor_copy(xt[k][0:ED, C:2 * C], psum[6 + k][0:ED, 0:C]).then_inc(eat_ready, 1)
                        if kind == "bases":
                            weigh_bases(i, u, t)
                        elif not (isinstance(t, int) and t < LAG_SUM):
                            add(i, u - LAG_SUM, t - LAG_SUM)
                        if kind == "mlp" and 1 <= u <= 10:
                            coefficients(i, u - 1)

                def add(i, u, t):
                    k, q = u % 2, u % RING
                    now, before = acc[q], acc[(q - 1) % RING]
                    msg = psum[4 + k]
                    if kind != "mlp":
                        link.start(t)
                    up_to(dve, acc_ready, t)
                    up_to(dve, sent[q], i * 2 + u // RING, 16)
                    if kind == "spline1" or kind == "spline2":
                        link(dve.tensor_scalar(run[0][:, :], before[:, 0:C], column(keep, t), None, ALU.mult))
                    dve.wait_ge(msg_ready, t + 1)
                    if kind == "mlp":
                        dve.scalar_tensor_tensor(now[:, 0:C + 1], before[:, 0:C + 1], column(keep, t),
                                                 msg[:, 0:C + 1], ALU.mult, ALU.add).then_inc(acc_ready, 1)
                    elif kind != "gat":
                        link(dve.scalar_tensor_tensor(run[1][:, :], msg[:, 0:C], column(eweight1, t), run[0][:, :],
                                                      ALU.mult, ALU.add))
                        dve.scalar_tensor_tensor(now[:, 0:C], msg[:, C:2 * C], column(eweight, t), run[1][:, :],
                                                 ALU.mult, ALU.add).then_inc(acc_ready, 1)
                    else:
                        e2, e, m_in = small[:, 0, :], small[:, 1, :], small[:, 2, :]
                        z = msg[:, C:C + HEADS]
                        link(dve.tensor_scalar(e2, z, 0.2, None, ALU.mult))
                        link(dve.tensor_tensor(e, z, e2, ALU.max))
                        link(dve.tensor_scalar(m_in, before[:, C + 4:C + 8], column(reset, t), None, ALU.add))
                        link(dve.tensor_tensor(now[:, C + 4:C + 8], m_in, e, ALU.max))
                        up_to(dve, part_ready, t - 1)
                        link(dve.tensor_tensor(diff[k][:, 1, :], e, now[:, C + 4:C + 8], ALU.subtract))
                        dve.tensor_tensor(diff[k][:, 0, :], m_in, now[:, C + 4:C + 8], ALU.subtract)\
                            .then_inc(diff_ready, 1)
                        dve.wait_ge(part_ready, t + 1)
                        old, new = part[k][:, 0, :], part[k][:, 1, :]
                        heads = lambda v: v.rearrange("p (h d) -> p h d", h=HEADS)
                        spread = lambda v: v.unsqueeze(2).to_broadcast([P, HEADS, HD])
                        link(dve.tensor_tensor(small[:, 3, :], before[:, C:C + 4], old, ALU.mult))
                        link(dve.tensor_tensor(now[:, C:C + 4], small[:, 3, :], new, ALU.add))
                        link(dve.tensor_tensor(heads(scaled[:, :]), heads(before[:, 0:C]), spread(old), ALU.mult))
                        link(dve.tensor_tensor(heads(weighed[:, :]), heads(msg[:, 0:C]), spread(new), ALU.mult))
                        dve.tensor_tensor(now[:, 0:C], scaled[:, :], weighed[:, :], ALU.add).then_inc(acc_ready, 1)
                def weigh_bases(i, u, t):
                    msg, o = psum[4 + u % 2], run[u % 2][:, :]
                    dve.wait_ge(msg_ready, t + 1)
                    for b in range(BASES):
                        m, cf = msg[:, b * C:(b + 1) * C], coef[:, bass.ds(t, 1), b]
                        if b == 0:
                            dve.tensor_scalar(o, m, cf, None, ALU.mult).then_inc(step_sem, 1)
                            if not (isinstance(t, int) and t == 0):
                                add_bases(i, u - 1, t - 1)
                            continue
                        dve.wait_ge(step_sem, t * (BASES - 1) + b)
                        dve.scalar_tensor_tensor(o, m, cf, o, ALU.mult, ALU.add)\
                            .then_inc(step_sem if b + 1 < BASES else msg_read, 1)

                def add_bases(i, u, t):
                    q = u % RING
                    up_to(dve, acc_ready, t)
                    up_to(dve, sent[q], i * 2 + u // RING, 16)
                    dve.wait_ge(msg_read, t + 1)
                    dve.scalar_tensor_tensor(acc[q][:, 0:C], acc[(q - 1) % RING][:, 0:C], column(keep, t), run[u % 2][:, :],
                                             ALU.mult, ALU.add).then_inc(acc_ready, 1)

                edge_steps(dve, body)
                if kind == "bases":
                    add_bases(ESTEPS - 1, ET - 1, TILES - 1)
                for u in range(ET - LAG_SUM, ET):
                    add(ESTEPS - 1, u, TILES - ET + u)

        loaded, joined, copied, written, steps2 = s("seam_loaded"), s("seam_joined"), s("seam_copied"), s("seam_written"), s("seam_steps")
        spread_rows, exped = s("seam_rows"), s("seam_exp")
        c = ExitStack()
        with c:
            tail = acc[RING - 1]
            if two:
                sm = sb(f"{name}_sm", [P, 10, HEADS], c=c)
                mx = sb(f"{name}_mx", [P, HEADS, P], c=c)
                bc = sb(f"{name}_bc", [P, 2, HEADS, P], c=c)
                mask = {m: sb(f"{name}_mask_{m}", [P, P], c=c) for m in seam}
                tr = sb(f"{name}_tr", [P, W], c=c)
            block = c.enter_context(nc.Block())

            @block.sync
            def _(sp):
                sp.dma_start(hrow[:, :], head_rows).then_inc(loaded, 16)

            last = tr if two else tail
            width = C + 8 if not two else C + HEADS

            @block.tensor
            def _(pe):
                pe.wait_ge(loaded, 16)
                if two:
                    pe.wait_ge(spread_rows, 1)
                    for a in range(2):
                        for h in range(HEADS):
                            q = pe.matmul(psum[2 + a][:, h * P:(h + 1) * P], bc[:, a, h, :], K["ident"][:, :],
                                          start=True, stop=True)
                    q.then_inc(spread_rows, 1)
                    pe.wait_ge(exped, 2)
                pe.matmul(psum[0][:, 0:width], seam["tt"][:, :], last[:, 0:width], start=True, stop=False)
                pe.matmul(psum[0][:, 0:width], seam["ht"][:, :], hrow[:, 0:width],
                          start=False, stop=True).then_inc(joined, 1)

            @block.vector
            def _(dve):
                n = [0]

                def link(ins):
                    n[0] += 1
                    ins.then_inc(steps2, 1)
                    dve.wait_ge(steps2, n[0])

                if two:
                    heads = lambda v: v.rearrange("p (h d) -> p h d", h=HEADS)
                    spread = lambda v, k: v.unsqueeze(2).to_broadcast([P, HEADS, k])
                    dve.wait_ge(loaded, 16)
                    nosum, mh, mt = sm[:, 0, :], sm[:, 1, :], tail[:, C + 4:C + 8]
                    link(dve.tensor_scalar(nosum, hrow[:, C:C + 4], 0.0, -LOW, ALU.is_equal, ALU.mult))
                    link(dve.tensor_tensor(mh, hrow[:, C + 4:C + 8], nosum, ALU.add))
                    for m in seam:
                        link(dve.tensor_scalar(mask[m][:, :], seam[m][:, :], -1.0, LOW, ALU.add, ALU.mult))
                    link(dve.tensor_copy(bc[:, 0, :, :], spread(mt, P)))
                    dve.tensor_copy(bc[:, 1, :, :], spread(mh, P)).then_inc(spread_rows, 1)
                    dve.wait_ge(spread_rows, 2)
                    for a, (m_t, m_h) in enumerate((("tt", "th"), ("ht", "hh"))):
                        for b, m in enumerate((m_t, m_h)):
                            link(dve.tensor_tensor(mx[:, :, :], psum[2 + b][:, :].rearrange("p (h j) -> p h j", h=HEADS),
                                                   mask[m][:, :].unsqueeze(1).to_broadcast([P, HEADS, P]), ALU.add))
                            link(dve.tensor_reduce(sm[:, 2 + b, :], mx[:, :, :], AX.X, ALU.max))
                        link(dve.tensor_tensor(sm[:, 4 + a, :], sm[:, 2, :], sm[:, 3, :], ALU.max))
                    link(dve.tensor_tensor(sm[:, 6, :], mt, sm[:, 4, :], ALU.subtract))
                    dve.tensor_tensor(sm[:, 7, :], mh, sm[:, 5, :], ALU.subtract).then_inc(exped, 1)
                    dve.wait_ge(copied, 1)
                    ft, fh = sm[:, 8, :], sm[:, 9, :]
                    for o, i, f in ((tr, tail, ft), (hrow, hrow, fh)):
                        link(dve.tensor_tensor(heads(o[:, 0:C]), heads(i[:, 0:C]), spread(f, HD), ALU.mult))
                        ins = dve.tensor_tensor(o[:, C:C + 4], i[:, C:C + 4], f, ALU.mult)
                        if o is tr:
                            link(ins)
                        else:
                            ins.then_inc(exped, 1)
                    dve.wait_ge(joined, 1)
                    link(dve.tensor_copy(trow[:, C + 4:C + 8], sm[:, 4, :]))
                    link(dve.tensor_copy(hrow[:, C + 4:C + 8], sm[:, 5, :]))
                    dve.tensor_copy(trow[:, 0:width], psum[0][:, 0:width]).then_inc(copied, 1)
                else:
                    dve.wait_ge(joined, 1)
                    dve.tensor_copy(trow[:, 0:width], psum[0][:, 0:width]).then_inc(copied, 1)

            if two:
                @block.scalar
                def _(act):
                    act.wait_ge(exped, 1)
                    act.activation(sm[:, 8:10, :], sm[:, 6:8, :], ACT.Exp).then_inc(copied, 1)

            @block.gpsimd
            def _(pool):
                pool.wait_ge(copied, 2 if two else 1)
                pool.wait_ge(loaded, 16)
                for row, index in ((trow, t_index), (hrow, h_index)):
                    pool.indirect_dma_start(AGG, bass.IndirectOffsetOnAxis(ap=index[:, 0:1], axis=0), row[:, :], None,
                                            bounds_check=ROWS - 1, oob_is_err=False).then_inc(written, 16)
                pool.wait_ge(written, 32)

    def node_phase(name, kind, x_in, x_res, x_out):
        own = Phase(name)
        nodes(name, kind, x_in, x_res, x_out, own)
        own.end()

    def nodes(name, kind, x_in, x_res, x_out, s):
        mlp, gat, res, norm = kind == "mlp", kind == "gat", kind == "spline2", kind != "spline1"
        SLOTS = 6
        x_got = [s(f"x_got{u}") for u in range(SLOTS)]
        a_got = [s(f"a_got{u}") for u in range(SLOTS)]
        r_got = [s(f"r_got{u}") for u in range(SLOTS)] if res else None
        stored = [s(f"stored{u}") for u in range(SLOTS)]
        turned, xt_ready, o_ready = s("turned"), s("xt_ready"), s("o_ready")
        y_ready, v_ready, r_ready, out_ready = s("y_ready"), s("v_ready"), s("r_ready"), s("out_ready")
        step_sem, pool_steps, a_used = s("steps"), s("pool_steps"), s("a_used")
        if mlp:
            a_scaled, a_turned, at_ready, hid_ready, rt_ready = s("a_scaled"), s("a_turned"), s("at_ready"), s("hid_ready"), s("rt_ready")
            n1_ready, xl_ready, v2_ready, r2_ready = s("n1_ready"), s("xl_ready"), s("v2_ready"), s("r2_ready")
            step_sem2, pool_steps2, scale_steps = s("steps2"), s("pool_steps2"), s("scale_steps")
        if gat or res:
            xb_ready = s("xb_ready")
        if gat:
            d_ready, e_ready, w_ready, a_weighed = s("d_ready"), s("e_ready"), s("w_ready"), s("a_weighed")
            score_steps, weigh_steps = s("score_steps"), s("weigh_steps")
        c = ExitStack()
        with c:
            def ring(what, width, n=SLOTS):
                return [sb(f"{name}_{what}{u}", [P, width], c=c) for u in range(n)]

            X, A, Y = ring("X", RB * C), ring("A", RB * W), ring("Y", RB * C)
            if gat or res:
                B = ring("B", RB * C)
            if res:
                R = ring("R", RB * C)
            xt = [ring(f"xt{k}_", 512, 2) for k in range(2)]
            if mlp:
                at = [ring(f"at{k}_", 512, 2) for k in range(2)]
                rt = [ring(f"rt{k}_", 512, 2) for k in range(2)]
                L = ring("L", RB * C)
                degree = sb(f"{name}_degree", [P, 1, RB], c=c)
            if gat:
                g_small = sb(f"{name}_gs", [P, 4, RB * HEADS], c=c)
                g_edges = [sb(f"{name}_ge{k}", [P, RB * HEADS], c=c) for k in range(2)]
                g_diff = [sb(f"{name}_gd{k}", [P, 2, RB * HEADS], c=c) for k in range(2)]
                g_exp = [sb(f"{name}_gx{k}", [P, 2, RB * HEADS], c=c) for k in range(2)]
            stat = [[sb(f"{name}_stat{q}{k}", [P, RB, 6], c=c) for k in range(2)] for q in range(2)]
            tmp = [sb(f"{name}_tmp{q}", [P, 3, RB], c=c) for q in range(2)]
            msum = [ring(f"msum{q}_", RB) for q in range(2)]
            var = [ring(f"var{q}_", RB) for q in range(2)]
            rstd = [ring(f"rstd{q}_", RB) for q in range(2)]
            shift = [ring(f"shift{q}_", RB) for q in range(2)]
            block = c.enter_context(nc.Block())
            rows3 = lambda t: t[:, :].rearrange("p (j f) -> p j f", j=RB)
            sums3 = lambda t: t[:, :].rearrange("p (j w) -> p j w", w=W)
            halves = lambda t, h: rows3(t)[:, 4 * h:4 * h + 4, :]
            bank3 = lambda b: psum[b][:, :].rearrange("p (j f) -> p j f", j=4)
            per_row = lambda r: r[:, :].unsqueeze(1).to_broadcast([P, RB, C])
            out_bank = lambda u, h: (6 if mlp or u % 2 == 0 else 2) + h
            OUT = L if mlp else Y
            per_x = 16

            @block.sync
            def _(sp):
                def load_a(b, u, i):
                    up_to(sp, a_turned if mlp else a_used, b - SLOTS + 1, 2 if mlp else 1)
                    sp.dma_start(A[u][:, :], rows_of(AGG, b, W)).then_inc(a_got[u], 16)

                def load_x(b, u, i):
                    if mlp:
                        up_to(sp, y_ready, b - SLOTS + 1, 2)
                        up_to(sp, xl_ready, b - SLOTS + 1)
                    elif gat:
                        up_to(sp, turned, b - SLOTS + 1, 2)
                        up_to(sp, xb_ready, b - SLOTS + 1)
                    elif kind == "rgcn":
                        up_to(sp, v_ready, b - SLOTS + 1)
                    else:
                        up_to(sp, turned, b - SLOTS + 1, 2)
                    sp.dma_start(X[u][:, :], rows_of(x_in, b, C)).then_inc(x_got[u], 16)
                    if res:
                        up_to(sp, xb_ready, b - SLOTS + 1)
                        sp.dma_start(R[u][:, :], rows_of(x_res, b, C)).then_inc(r_got[u], 16)

                def store(b, u, i):
                    sp.wait_ge(out_ready, b + 1)
                    if isinstance(b, int) and b == BLOCKS - 1:
                        sp.wait_ge(stored[(u - 1) % SLOTS], 16 * ((b - 1) // SLOTS + 1))
                    sp.dma_start(rows_of(x_out, b, C), OUT[u][:, :]).then_inc(stored[u], 16)

                pipeline(sp, SLOTS, *{"mlp": [(0, load_a), (2, load_x), (8, store)],
                                      "gat": [(0, load_a), (0, load_x), (5, store)]}
                         .get(kind, [(0, load_a), (0, load_x), (5, store)]))
                for u in range(SLOTS):
                    sp.wait_ge(stored[u], 16 * ((BLOCKS - 1 - u) // SLOTS + 1))

            @block.gpsimd
            def _(pool):
                links = [Chain(pool, pool_steps, 2), Chain(pool, pool_steps2, 2) if mlp else None]

                def rstd_of(q):
                    def stage(b, u, i):
                        link = links[q]
                        link.start(b)
                        pool.wait_ge((v_ready, v2_ready)[q] if q else v_ready, b + 1)
                        link(pool.tensor_tensor(rstd[q][u][:, :], var[q][u][:, :], half[:, :], ALU.pow))
                        link(pool.tensor_tensor(msum[q][u][:, :], msum[q][u][:, :], half[:, :], ALU.mult))
                        pool.tensor_tensor(shift[q][u][:, :], msum[q][u][:, :], rstd[q][u][:, :], ALU.mult)\
                            .then_inc((r_ready, r2_ready)[q] if q else r_ready, 1)
                    return stage

                def add_bias(b, u, i):
                    up_to(pool, y2_done, b - SLOTS + 1, y2_per)
                    pool.wait_ge((r_got if res else x_got)[u], (i + 1) * 16)
                    pool.tensor_tensor(rows3(B[u]), rows3((R if res else X)[u]), per_row(K["sb2" if res else "gbias"]), ALU.add)\
                        .then_inc(xb_ready, 1)

                def add_ln_b(b, u, i):
                    pool.wait_ge(x_got[u], (i + 1) * 16)
                    up_to(pool, stored[u], i, 16)
                    pool.tensor_tensor(rows3(L[u]), rows3(X[u]), per_row(K["ln_b"]), ALU.add).then_inc(xl_ready, 1)

                def weigh_edges(b, u, i):
                    pool.wait_ge(w_ready, b + 1)
                    v = sums3(A[u])[:, :, 0:C].rearrange("p j (h d) -> p j h d", h=HEADS)
                    pool.tensor_tensor(v, v, g_edges[u % 2][:, :].rearrange("p (j h) -> p j h", h=HEADS).unsqueeze(3)
                                       .to_broadcast([P, RB, HEADS, HD]), ALU.mult).then_inc(a_weighed, 1)

                y2_done, y2_per = a_used, 1
                if mlp:
                    pipeline(pool, SLOTS, (3, rstd_of(0)), (5, rstd_of(1)), (1, add_ln_b))
                elif gat:
                    pipeline(pool, SLOTS, (0, add_bias), (2, weigh_edges), (3, rstd_of(0)))
                elif res:
                    pipeline(pool, SLOTS, (0, add_bias), (1, rstd_of(0)))
                elif norm:
                    pipeline(pool, SLOTS, (1, rstd_of(0)))

            @block.tensor
            def _(pe):
                def turn_x(b, u, i):
                    pe.wait_ge(x_got[u], (i + 1) * 16)
                    for h in range(2):
                        up_to(pe, xt_ready, (b - 1) * 2 + h + 1)
                        for j in range(4):
                            q = pe.transpose(psum[h][:, j * P:(j + 1) * P], X[u][:, (4 * h + j) * C:(4 * h + j + 1) * C],
                                             K["ident"][:, :])
                        q.then_inc(turned, 1)

                def turn_a(b, u, i):
                    pe.wait_ge(a_scaled, b + 1)
                    for h in range(2):
                        up_to(pe, at_ready, (b - 1) * 2 + h + 1)
                        for j in range(4):
                            q = pe.transpose(psum[2 + h][:, j * P:(j + 1) * P],
                                             A[u][:, (4 * h + j) * W:(4 * h + j) * W + C], K["ident"][:, :])
                        q.then_inc(a_turned, 1)

                def hidden(b, u, i):
                    for h in range(2):
                        pe.wait_ge(xt_ready, b * 2 + h + 1)
                        pe.wait_ge(at_ready, b * 2 + h + 1)
                        up_to(pe, rt_ready, (b - 1) * 2 + h + 1)
                        pe.matmul(psum[4 + h][:, :], K["wu1x"][:, :], xt[u % 2][h][:, :], start=True, stop=False)
                        pe.matmul(psum[4 + h][:, :], K["wu1a"][:, :], at[u % 2][h][:, :], start=False, stop=True)\
                            .then_inc(hid_ready, 1)

                def output(b, u, i):
                    w = {"mlp": K["wu2"][:, :], "gat": K["wgat"][:, 0:C], "rgcn": K["loop"][:, :],
                         "spline1": K["root1"][:, :], "spline2": K["root2"][:, :]}[kind]
                    lhs, ready = (rt, rt_ready) if mlp else (xt, xt_ready)
                    for h in range(2):
                        pe.wait_ge(ready, b * 2 + h + 1)
                        up_to(pe, y_ready, (b - (1 if mlp else 2)) * 2 + h + 1)
                        if gat and h == 0:
                            up_to(pe, d_ready, b - 1)
                        bank = out_bank(u, h)
                        if mlp:
                            pe.matmul(psum[bank][:, :], one3[:, :], bu2_parts[:, :], start=True, stop=False)
                        for j in range(4):
                            q = pe.matmul(psum[bank][:, j * C:(j + 1) * C], lhs[u % 2][h][:, j * P:(j + 1) * P], w,
                                          start=not mlp, stop=not mlp or j == 3)
                            if gat:
                                r = 4 * h + j
                                q = pe.matmul(psum[4 + u % 2][:, r * HEADS:(r + 1) * HEADS], lhs[u % 2][h][:, j * P:(j + 1) * P],
                                              K["wself"][:, :], start=True, stop=True)
                        q.then_inc(o_ready, 1)

                if mlp:
                    pipeline(pe, SLOTS, (0, turn_x), (0, turn_a), (1, hidden), (2, output))
                else:
                    pipeline(pe, SLOTS, (0, turn_x), (1, output))

            @block.scalar
            def _(act):
                def copy_x(b, u, i):
                    for h in range(2):
                        act.wait_ge(turned, b * 2 + h + 1)
                        up_to(act, hid_ready if mlp else o_ready, (b - 2) * 2 + h + 1)
                        act.activation(xt[u % 2][h][:, :], psum[h][:, :], ACT.Copy).then_inc(xt_ready, 1)

                def copy_a(b, u, i):
                    for h in range(2):
                        act.wait_ge(a_turned, b * 2 + h + 1)
                        up_to(act, hid_ready, (b - 2) * 2 + h + 1)
                        act.activation(at[u % 2][h][:, :], psum[2 + h][:, :], ACT.Copy).then_inc(at_ready, 1)

                def relu(b, u, i):
                    for h in range(2):
                        act.wait_ge(hid_ready, b * 2 + h + 1)
                        up_to(act, o_ready, (b - 2) * 2 + h + 1)
                        act.activation(rt[u % 2][h][:, :], psum[4 + h][:, :], ACT.Relu, bias=bias_u[:, 0:1])\
                            .then_inc(rt_ready, 1)

                def exp(b, u, i):
                    act.wait_ge(d_ready, b + 1)
                    up_to(act, w_ready, b - 1)
                    act.activation(g_exp[u % 2][:, :, :], g_diff[u % 2][:, :, :], ACT.Exp).then_inc(e_ready, 1)

                def normalise(q, o, ready):
                    def stage(b, u, i):
                        act.wait_ge(r2_ready if q else r_ready, b + 1)
                        for j in range(RB):
                            ins = act.activation(o[u][:, j * C:(j + 1) * C], o[u][:, j * C:(j + 1) * C], ACT.Identity,
                                                 bias=shift[q][u][:, j:j + 1], scale=rstd[q][u][:, j:j + 1])
                        ins.then_inc(ready, 1)
                    return stage

                if mlp:
                    pipeline(act, SLOTS, (0, copy_x), (0, copy_a), (3, normalise(0, Y, n1_ready)), (1, relu),
                             (5, normalise(1, L, out_ready)))
                elif gat:
                    pipeline(act, SLOTS, (0, copy_x), (1, exp), (4, normalise(0, Y, out_ready)))
                elif norm:
                    pipeline(act, SLOTS, (0, copy_x), (3, normalise(0, Y, out_ready)))
                else:
                    pipeline(act, SLOTS, (0, copy_x))

            @block.vector
            def _(dve):
                link = Chain(dve, step_sem, {"mlp": 4, "gat": 4, "rgcn": 5, "spline1": 0, "spline2": 4}[kind])

                def statistics(link, q, b, u, y):
                    st = stat[q][u % 2]
                    for j in range(RB):
                        ins = dve.bn_stats(st[:, j, :], y[:, j * C:(j + 1) * C])
                    link(ins)
                    s_, d_, dd, m2 = msum[q][u][:, :], tmp[q][:, 0, :], tmp[q][:, 1, :], tmp[q][:, 2, :]
                    me, mo, ve, vo = st[:, :, 1], st[:, :, 4], st[:, :, 2], st[:, :, 5]
                    dve.tensor_tensor(s_, me, mo, ALU.add)
                    dve.tensor_tensor(m2, ve, vo, ALU.add)
                    link(dve.tensor_tensor(d_, me, mo, ALU.subtract))
                    link(dve.tensor_tensor(dd, d_, d_, ALU.mult))
                    link(dve.scalar_tensor_tensor(m2, dd, C / 4.0, m2, ALU.mult, ALU.add))
                    dve.tensor_scalar(var[q][u][:, :], m2, 1.0 / C, LN_EPS, ALU.mult, ALU.add)\
                        .then_inc(v2_ready if q else v_ready, 1)

                def scale_sums(b, u, i):
                    steps = Chain(dve, scale_steps, 2)
                    steps.start(b)
                    iv = invdeg[:, bass.ds(b, 1), :]
                    dve.wait_ge(a_got[u], (i + 1) * 16)
                    steps(dve.tensor_scalar(degree[:, :, :], sums3(A[u])[:, :, C:C + 1].rearrange("p j o -> p o j"),
                                            1.0, None, ALU.max))
                    steps(dve.reciprocal(iv, degree[:, :, :]))
                    dve.tensor_tensor(sums3(A[u])[:, :, 0:C], sums3(A[u])[:, :, 0:C],
                                      iv.rearrange("p o j -> p (o j)").unsqueeze(2).to_broadcast([P, RB, C]),
                                      ALU.mult).then_inc(a_scaled, 1)

                def first_norm(b, u, i):
                    link.start(b)
                    dve.wait_ge(x_got[u], (i + 1) * 16)
                    for h in range(2):
                        dve.wait_ge(o_ready, b * 2 + h + 1)
                        dve.tensor_tensor(halves(Y[u], h), bank3(6 + h), halves(X[u], h), ALU.add).then_inc(y_ready, 1)
                    dve.wait_ge(y_ready, b * 2 + 2)
                    statistics(link, 0, b, u, Y[u])

                def second_norm(b, u, i):
                    link2 = Chain(dve, step_sem2, 6)
                    link2.start(b)
                    dve.wait_ge(n1_ready, b + 1)
                    link2(dve.tensor_tensor(rows3(Y[u]), rows3(Y[u]), per_row(K["ln_g"]), ALU.mult))
                    dve.wait_ge(xl_ready, b + 1)
                    link2(dve.tensor_tensor(L[u][:, :], Y[u][:, :], L[u][:, :], ALU.add))
                    statistics(link2, 1, b, u, L[u])

                n_ = RB * HEADS
                by_row = lambda v: v.rearrange("p (j h) -> p j h", h=HEADS)

                def scores(b, u, i):
                    steps = Chain(dve, score_steps, 5)
                    steps.start(b)
                    es, me, mx = g_small[:, 0, :], g_small[:, 1, :], g_small[:, 2, :]
                    diff, sc = g_diff[u % 2], psum[4 + u % 2][:, 0:n_]
                    s_e, m_e = sums3(A[u])[:, :, C:C + 4], sums3(A[u])[:, :, C + 4:C + 8]
                    dve.wait_ge(a_got[u], (i + 1) * 16)
                    steps(dve.tensor_scalar(by_row(me), s_e, 0.0, -LOW, ALU.is_equal, ALU.mult))
                    dve.wait_ge(o_ready, b * 2 + 2)
                    dve.tensor_tensor(by_row(me), by_row(me), m_e, ALU.add)
                    steps(dve.tensor_scalar(es, sc, 0.2, None, ALU.mult))
                    steps(dve.tensor_tensor(es, sc, es, ALU.max))
                    steps(dve.tensor_tensor(mx, me, es, ALU.max))
                    steps(dve.tensor_tensor(diff[:, 0, :], me, mx, ALU.subtract))
                    dve.tensor_tensor(diff[:, 1, :], es, mx, ALU.subtract).then_inc(d_ready, 1)

                def weights(b, u, i):
                    steps = Chain(dve, weigh_steps, 4)
                    steps.start(b)
                    ce, cs = g_exp[u % 2][:, 0, :], g_exp[u % 2][:, 1, :]
                    total, own_w = g_small[:, 3, :], g_own[:, :]
                    dve.wait_ge(e_ready, b + 1)
                    steps(dve.tensor_tensor(by_row(total), sums3(A[u])[:, :, C:C + 4], by_row(ce), ALU.mult))
                    steps(dve.tensor_tensor(total, total, cs, ALU.add))
                    steps(dve.reciprocal(total, total))
                    up_to(dve, a_weighed, b - 1)
                    dve.tensor_tensor(own_w, cs, total, ALU.mult)
                    dve.tensor_tensor(g_edges[u % 2][:, :], ce, total, ALU.mult).then_inc(w_ready, 1)
                    dve.wait_ge(w_ready, b + 1)
                    up_to(dve, stored[u], i, 16)
                    for h in range(2):
                        ins = dve.tensor_tensor(Y[u][:, h * 512:(h + 1) * 512].rearrange("p (q d) -> p q d", d=HD),
                                                psum[out_bank(u, h)][:, :].rearrange("p (q d) -> p q d", d=HD),
                                                own_w[:, h * 16:(h + 1) * 16].unsqueeze(2).to_broadcast([P, 16, HD]), ALU.mult)
                        ins.then_inc(y_ready, 1)
                    dve.wait_ge(y_ready, b * 2 + 2)
                    dve.wait_ge(xb_ready, b + 1)
                    steps(dve.tensor_tensor(Y[u][:, :], Y[u][:, :], B[u][:, :], ALU.add))

                def add_edges(b, u, i):
                    link.start(b)
                    dve.wait_ge(a_weighed, b + 1)
                    ins = dve.tensor_tensor(rows3(Y[u]), rows3(Y[u]), sums3(A[u])[:, :, 0:C], ALU.add)
                    ins.then_inc(a_used, 1)
                    dve.wait_ge(a_used, b + 1)
                    statistics(link, 0, b, u, Y[u])

                def add_sums(b, u, i):
                    if norm:
                        link.start(b)
                    dve.wait_ge(a_got[u], (i + 1) * 16)
                    up_to(dve, stored[u], i, 16)
                    if kind == "rgcn":
                        for h in range(2):
                            dve.wait_ge(o_ready, b * 2 + h + 1)
                            ins = dve.tensor_tensor(halves(Y[u], h), bank3(out_bank(u, h)), sums3(A[u])[:, 4 * h:4 * h + 4, 0:C],
                                                    ALU.add)
                            ins.then_inc(y_ready, 1)
                        dve.wait_ge(y_ready, b * 2 + 2)
                        dve.sem_inc(a_used, 1)
                        dve.wait_ge(x_got[u], (i + 1) * 16)
                        link(dve.scalar_tensor_tensor(Y[u][:, :], Y[u][:, :], 0.0, X[u][:, :], ALU.max, ALU.add))
                        statistics(link, 0, b, u, Y[u])
                        return
                    for j in range(RB):
                        h = j // 4
                        if j % 4 == 0:
                            dve.wait_ge(o_ready, b * 2 + h + 1)
                        ins = dve.scalar_tensor_tensor(
                            Y[u][:, j * C:(j + 1) * C], A[u][:, j * W:j * W + C], invdeg[:, bass.ds(b, 1), j],
                            psum[out_bank(u, h)][:, (j % 4) * C:(j % 4 + 1) * C], ALU.mult, ALU.add)
                        if j % 4 == 3:
                            ins.then_inc(y_ready, 1)
                    dve.wait_ge(y_ready, b * 2 + 2)
                    if kind == "spline1":
                        dve.sem_inc(a_used, 1)
                        dve.tensor_tensor(rows3(Y[u]), rows3(Y[u]), per_row(K["sb1"]), ALU.add).then_inc(out_ready, 1)
                    else:
                        dve.wait_ge(xb_ready, b + 1)
                        ins = dve.tensor_tensor(Y[u][:, :], Y[u][:, :], B[u][:, :], ALU.add)
                        ins.then_inc(a_used, 1)
                        dve.wait_ge(a_used, b + 1)
                        statistics(link, 0, b, u, Y[u])

                if mlp:
                    pipeline(dve, SLOTS, (0, scale_sums), (5, second_norm), (3, first_norm))
                elif gat:
                    g_own = sb(f"{name}_go", [P, RB * HEADS], c=c)
                    pipeline(dve, SLOTS, (2, weights), (1, scores), (3, add_edges))
                else:
                    pipeline(dve, SLOTS, (0, add_sums))

    edge_phase("e0", "mlp", D["x"])
    if upto < 1: return
    node_phase("n0", "mlp", D["x"], None, X1)
    if upto < 2: return
    edge_phase("e1", "gat", X1)
    if upto < 3: return
    node_phase("n1", "gat", X1, None, X2)
    if upto < 4: return
    edge_phase("e2", "bases", X2)
    node_phase("n2", "rgcn", X2, None, X3)
    if upto < 5: return
    edge_phase("e3", "spline1", X3)
    node_phase("n3", "spline1", X3, None, HT)
    if upto < 6: return
    edge_phase("e4", "spline2", HT)
    node_phase("n4", "spline2", HT, X3, out)



def _layout(x, src, dst, edge_attr_64, edge_type_64, edge_weight1, L0_gnn_global_state, L0_gnn_Wm1, L0_gnn_bm1,
            L0_gnn_Wm2, L0_gnn_bm2, L0_gnn_Wu1, L0_gnn_bu1, L0_gnn_Wu2, L0_gnn_bu2, L0_gnn_ln_g, L0_gnn_ln_b,
            L1_gnn_W, L1_gnn_att_src, L1_gnn_att_dst, L1_gnn_bias, L2_gnn_v_b, L2_gnn_a_rb, L2_gnn_loop_weight,
            L3_gnn_W1, L3_gnn_root1, L3_gnn_b1, L3_gnn_W2, L3_gnn_root2, L3_gnn_b2):
    import numpy as np

    def runs(a, fill):
        a = np.asarray(a)
        a = a.reshape(a.shape[0], -1)
        a = np.pad(a, ((0, P * TILES - a.shape[0]), (0, 0)), constant_values=fill)
        return a.reshape(P, -1)

    A = np.asarray
    wm1, wu1 = A(L0_gnn_Wm1), A(L0_gnn_Wu1)
    side = lambda w: A(w).transpose(1, 0, 2).reshape(C, -1)
    d = dict(x=A(x), src=runs(src, 0), dst=runs(dst, PAD_DST), etype=runs(edge_type_64, 0),
             eweight=runs(edge_weight1, 0), eattr=runs(edge_attr_64, 0),
             wm1x=wm1[:, :C].T, wm1e=wm1[:, C:C + ED].T, wm1g=wm1[:, C + ED:].T, wm2=A(L0_gnn_Wm2).T,
             wu1x=wu1[:, :C].T, wu1a=wu1[:, C:2 * C].T, wu1g=wu1[:, 2 * C:].T, wu2=A(L0_gnn_Wu2).T,
             gstate=A(L0_gnn_global_state).reshape(-1, 1), bm1=A(L0_gnn_bm1).reshape(-1, 1),
             bu1=A(L0_gnn_bu1).reshape(-1, 1), bm2=A(L0_gnn_bm2), bu2=A(L0_gnn_bu2),
             ln_g=A(L0_gnn_ln_g), ln_b=A(L0_gnn_ln_b), wgat=A(L1_gnn_W), atts=A(L1_gnn_att_src).reshape(-1),
             attd=A(L1_gnn_att_dst).reshape(-1), gbias=A(L1_gnn_bias), vb=side(L2_gnn_v_b),
             arb=A(L2_gnn_a_rb).T.reshape(-1), loop=A(L2_gnn_loop_weight), sw1=side(L3_gnn_W1),
             root1=A(L3_gnn_root1), sb1=A(L3_gnn_b1), sw2=side(L3_gnn_W2), root2=A(L3_gnn_root2), sb2=A(L3_gnn_b2))
    return {k: np.ascontiguousarray(v) for k, v in d.items()}


def kernel(**inputs):
    import concourse.bacc as bacc
    from concourse.bass_utils import run_bass_kernel_spmd

    arrays = _layout(**inputs)
    nc = bacc.Bacc("TRN2", target_bir_lowering=False, num_devices=1)
    D = {k: nc.dram_tensor("in_" + k, v.shape, mybir.dt.from_np(v.dtype), kind="ExternalInput").ap()
         for k, v in arrays.items()}
    out = nc.dram_tensor("out_x", [N, C], F32, kind="ExternalOutput").ap()
    build(nc, D, out)
    r = run_bass_kernel_spmd(nc, [{"in_" + k: v for k, v in arrays.items()}], core_ids=[0])
    return r.results[0]["out_x"]
```

```python
from contextlib import ExitStack

import concourse.bass as bass
from concourse import mybir

F32 = mybir.dt.float32
BF16 = mybir.dt.bfloat16
I32 = mybir.dt.int32
ALU = mybir.AluOpType
ACT = mybir.ActivationFunctionType
AX = mybir.AxisListType

P = 128
C = 128
N = 100000
TILES = 392
RING = 7
ET = 2 * RING
ESTEPS = TILES // ET
ED = 64
RELS = 64
BASES = 4
HEADS = 4
HD = C // HEADS
RB = 8
BLOCK = P * RB
BLOCKS = -(-N // BLOCK)
G = C + HEADS
W = 136
HEAD = N
ROWS = -(-(N + P) // BLOCK) * BLOCK
AWAY = float(1 << 22)
PAD_DST = 1 << 21
LOW = 1.0e30
LN_EPS = 1e-5
FIELDS = 4
SORT_COLS = 14


def up_to(eng, sem, count, per=1):
    if isinstance(count, int) and count <= 0:
        return
    eng.wait_ge(sem, count * per)


def edge_steps(eng, body):
    body(0)
    with eng.Fori(1, ESTEPS - 1) as i:
        body(i)
    body(ESTEPS - 1)


def pipeline(eng, slots, *stages):
    def turn(k, u, i):
        for lag, stage, *more in stages:
            b = k - lag
            if not isinstance(b, int) or 0 <= b < BLOCKS + sum(more):
                stage(b, (u - lag) % slots, i + (u - lag) // slots)

    furthest = max(lag + sum(more) for lag, _, *more in stages)
    start, stop = -(-(furthest + slots) // slots), BLOCKS // slots
    for k in range(start * slots):
        turn(k, k % slots, k // slots)
    with eng.Fori(start, stop) as i:
        for u in range(slots):
            turn(i * slots + u, u, i)
    for k in range(stop * slots, BLOCKS + furthest):
        turn(k, k % slots, k // slots)


def block_rows(block):
    return min(block * BLOCK, N - BLOCK) if isinstance(block, int) else block * BLOCK


def rows_of(table, block, width):
    return table[bass.ds(block_rows(block), BLOCK), :].rearrange("(p j) f -> p (j f)", p=P)


class Chain:

    def __init__(self, eng, sem, per):
        self.eng, self.sem, self.per, self.k, self.item = eng, sem, per, 0, 0

    def start(self, item):
        self.item, self.k = item, 0

    def step(self, instruction):
        self.k += 1
        assert self.k <= self.per
        instruction.then_inc(self.sem, 1)

    def settle(self):
        self.eng.wait_ge(self.sem, self.item * self.per + self.k)

    def __call__(self, instruction):
        self.step(instruction)
        self.settle()


def build(nc, D, out):
    with ExitStack() as ctx:
        _build(nc, D, out, ctx)


def _build(nc, D, out, ctx):
    def sb(name, shape, dt=F32, c=ctx):
        return c.enter_context(nc.sbuf_tensor(name, shape, dt))

    def sem(name):
        return ctx.enter_context(nc.semaphore(name))

    class Phase:

        def __init__(self, name):
            self.name, self.sems = name, []

        def __call__(self, what):
            self.sems.append(nc.alloc_semaphore(name=f"{self.name}_{what}"))
            return self.sems[-1]

        def end(self):
            nc.all_engine_barrier()
            nc.clear_and_free_semaphores(self.sems)
            nc.all_engine_barrier()

    AGG = nc.dram_tensor("AGG", [ROWS, W], F32).ap()
    X1 = nc.dram_tensor("X1", [N, C], F32).ap()
    X2 = nc.dram_tensor("X2", [N, C], F32).ap()
    X3 = nc.dram_tensor("X3", [N, C], F32).ap()
    HT = nc.dram_tensor("HT", [N, C], F32).ap()
    head_rows = AGG[HEAD:HEAD + P, :]
    EDGES = nc.dram_tensor("EDGES", [P * TILES, FIELDS], I32).ap()
    ATTRS = nc.dram_tensor("ATTRS", [P * TILES, ED], F32).ap()

    K = {}
    for name in ("ident", "ones"):
        K[name] = sb(name, [P, P])
    wload = []
    def weight(name, rows, cols):
        K[name] = sb("w_" + name, [rows, cols])
        wload.append((K[name][:, :], D[name]))
    weight("wm1x", C, C); weight("wm1e", ED, C); weight("wm1g", 64, C)
    weight("wm2", C, C); weight("wu1x", C, C); weight("wu1a", C, C); weight("wu1g", 64, C)
    weight("wu2", C, C); weight("gstate", 64, 1); weight("bm1", C, 1); weight("bu1", C, 1)
    one3 = sb("one3", [3, P], BF16)
    bm2_parts = sb("bm2_parts", [3, C + 1], BF16)
    bu2_parts = sb("bu2_parts", [3, 4 * C], BF16)
    gat_parts = sb("gat_parts", [3, C + HEADS], BF16)
    gat_parts3 = sb("gat_parts3", [3, 3 * (C + HEADS)], BF16)
    weight("vb", C, BASES * C); weight("loop", C, C)
    weight("sw1", C, 2 * C); weight("root1", C, C); weight("sw2", C, 2 * C); weight("root2", C, C)
    K["wgat"] = sb("w_gat", [C, C + HEADS])
    K["wdst"] = sb("w_dst", [C, HEADS])
    K["wnode"] = sb("w_node", [C, C + HEADS])
    K["atts"] = sb("w_atts", [C, C]); K["attd"] = sb("w_attd", [C, C])
    K["arb"] = sb("w_arb", [P, BASES * RELS])
    for name in ("bm2", "bu2", "ln_g", "ln_b", "gbias", "sb1", "sb2"):
        K[name] = sb("r_" + name, [P, C])
    src = sb("src", [P, TILES], I32)
    dsti = sb("dsti", [P, TILES], I32)
    dst_gather = sb("dst_gather", [P, TILES], I32)
    target = sb("target", [P, TILES], I32)
    keep = sb("keep", [P, TILES])
    reset = sb("reset", [P, TILES])
    etype = sb("etype", [P, TILES])
    eweight = sb("eweight", [P, TILES])
    eweight1 = sb("eweight1", [P, TILES])
    coef = sb("coef", [P, TILES, BASES])
    invdeg = sb("invdeg", [P, BLOCKS, RB])
    bias_m = sb("bias_m", [C, 1])
    bias_u = sb("bias_u", [C, 1])
    half = sb("half", [P, 2 * RB])
    iota_r = sb("iota_r", [P, RELS])
    t_index = sb("t_index", [P, 1], I32)
    h_index = sb("h_index", [P, 1], I32)
    seam = {n: sb("seam_" + n, [P, P]) for n in ("tt", "th", "ht", "hh")}

    src_now = [sb(f"src_now{h}", [P, RING], I32) for h in range(2)]
    dst_now = [sb(f"dst_now{h}", [P, RING], I32) for h in range(2)]
    target_now = [sb(f"target_now{h}", [P, RING], I32) for h in range(2)]
    xs = [sb(f"xs{q}", [P, C]) for q in range(RING)]
    acc = [sb(f"acc{q}", [P, W]) for q in range(RING)]
    hrow = sb("hrow", [P, W])
    trow = sb("trow", [P, W])

    psum = [ctx.enter_context(nc.psum_tensor(f"bank{i}", [P, 512], F32)) for i in range(8)]

    dstf = sb("dstf", [P, TILES])
    etypei = sb("etypei", [P, TILES], I32)
    shift_up = sb("shift_up", [P, P])
    shift_down = sb("shift_down", [P, P])
    unsorted = sb("unsorted", [1, 1], I32)
    edges_in, made, order_steps, order_pe = sem("edges_in"), sem("made"), sem("order_steps"), sem("order_pe")
    with ExitStack() as c0:
        falls = sb("falls", [P, TILES], c=c0)
        ends = sb("ends", [P, 6], c=c0)
        block = c0.enter_context(nc.Block())

        @block.sync
        def _(sp):
            for o, i in ((src, D["src"]), (dsti, D["dst"]), (etypei, D["etype"]), (eweight, D["eweight"])):
                sp.dma_start(o[:, :], i).then_inc(edges_in, 16)

        @block.gpsimd
        def _(pool):
            mats = ((K["ident"], 0), (shift_up, -1), (shift_down, 1))
            for m, _ in mats:
                pool.memset(m[:, :], 0.0).then_inc(made, 1)
            pool.wait_ge(made, 3)
            for m, base in mats:
                pool.affine_select(out=m[:, :], in_=m[:, :], compare_op=ALU.not_equal, fill=1.0,
                                   base=base, pattern=[[-1, P]], channel_multiplier=1).then_inc(made, 1)

        @block.vector
        def _(dve):
            n = [0]

            def link(ins):
                n[0] += 1
                ins.then_inc(order_steps, 1)
                dve.wait_ge(order_steps, n[0])

            link(dve.memset(K["ones"][:, :], 1.0))
            dve.wait_ge(edges_in, 64)
            link(dve.tensor_copy(dstf[:, :], dsti[:, :]))
            link(dve.memset(ends[:, 1:2], 1.0))
            link(dve.tensor_copy(ends[:, 0:1], dstf[:, 0:1]))
            dve.wait_ge(order_pe, 1)
            link(dve.tensor_tensor(falls[:, 1:], dstf[:, :-1], dstf[:, 1:], ALU.is_gt))
            link(dve.tensor_tensor(falls[:, 0:1], dstf[:, TILES - 1:], psum[0][:, 0:1], ALU.is_gt))
            link(dve.tensor_tensor(falls[:, 0:1], falls[:, 0:1], psum[0][:, 1:2], ALU.mult))
            link(dve.tensor_reduce(ends[:, 2:3], falls[:, :], AX.X, ALU.add))
            dve.wait_ge(order_pe, 2)
            link(dve.tensor_copy(unsorted[:, :], psum[1][0:1, 0:1]))

        @block.tensor
        def _(pe):
            pe.wait_ge(made, 6)
            pe.wait_ge(order_steps, 4)
            pe.matmul(psum[0][:, 0:2], shift_up[:, :], ends[:, 0:2], start=True, stop=True).then_inc(order_pe, 1)
            pe.wait_ge(order_steps, 8)
            pe.matmul(psum[1][0:1, 0:1], ends[:, 2:3], K["ones"][:, 0:1], start=True, stop=True).then_inc(order_pe, 1)

    sorting = Phase("sort")
    with ExitStack() as c0:
        steps, on, sent_rows, row_in = sorting("steps"), sorting("on"), sorting("sent_rows"), sorting("row_in")
        iotas, counted, ranked, now_ready = sorting("iotas"), sorting("counted"), sorting("ranked"), sorting("now_ready")
        row = sb("sort_row", [P, TILES], c=c0)
        bound = sb("sort_bound", [P, TILES], c=c0)
        rank = sb("sort_rank", [P, TILES], c=c0)
        ranki = sb("sort_ranki", [P, TILES], I32, c0)
        grid = sb("sort_grid", [P, SORT_COLS, TILES], c=c0)
        counts = sb("sort_counts", [P, SORT_COLS], c=c0)
        earlier = sb("sort_earlier", [P, SORT_COLS, TILES], c=c0)
        tile_no = sb("sort_tile_no", [P, TILES], c=c0)
        runs_ = sb("sort_runs", [P, P], c=c0)
        packed = sb("sort_packed", [P, TILES * FIELDS], I32, c0)
        now = sb("sort_now", [P, 1], I32, c0)
        now_fields = sb("sort_fields", [P, FIELDS], I32, c0)
        now_attrs = sb("sort_attrs", [P, ED], c=c0)
        rowi = sb("sort_rowi", [P, TILES], I32, c0)
        block = c0.enter_context(nc.Block())

        @block.gpsimd
        def _(pool):
            def settle(sem_, value):
                pool.wait_ge(sem_, value)
                pool.sem_inc(on, 1)

            n_unsorted = pool.value_load(unsorted[0:1, 0:1], min_val=0, max_val=P * TILES)
            with pool.If(n_unsorted > 0):
                pool.iota(tile_no[:, :], [[1, TILES]], base=0, channel_multiplier=0,
                          allow_small_or_imprecise_dtypes=True).then_inc(iotas, 1)
                pool.iota(runs_[:, :], [[1, P]], base=0, channel_multiplier=-1,
                          allow_small_or_imprecise_dtypes=True).then_inc(iotas, 1)
                with pool.Fori(0, P) as r:
                    pool.dma_start(rowi[:, :], D["dst"][bass.ds(r, 1), :].to_broadcast([P, TILES])).then_inc(row_in, 16)
                    settle(counted, r + 1)
                settle(ranked, 1)
                with pool.Fori(0, TILES) as t:
                    pool.dma_start(now_attrs[:, :], D["eattr"][:, bass.ds(t * ED, ED)]).then_inc(row_in, 16)
                    pool.tensor_copy(now[:, :], ranki[:, bass.ds(t, 1)]).then_inc(now_ready, 1)
                    pool.tensor_copy(now_fields[:, :], packed[:, bass.ds(t * FIELDS, FIELDS)]).then_inc(now_ready, 1)
                    settle(now_ready, t * 2 + 2)
                    settle(row_in, t * 16 + (16 * P + 16))
                    at = bass.IndirectOffsetOnAxis(ap=now[:, 0:1], axis=0)
                    pool.indirect_dma_start(EDGES, at, now_fields[:, :], None).then_inc(sent_rows, 16)
                    pool.indirect_dma_start(ATTRS, at, now_attrs[:, :], None).then_inc(sent_rows, 16)
                    settle(sent_rows, t * 32 + 32)
                pool.dma_start(packed[:, :], EDGES.rearrange("(p t) f -> p (t f)", p=P)).then_inc(sent_rows, 16)
            with pool.Else():
                pool.sem_inc(on, 1)

        @block.vector
        def _(dve):
            n = [0]

            def link(ins):
                n[0] += 1
                ins.then_inc(steps, 1)
                dve.wait_ge(steps, n[0])

            own = lambda t, cols: t[:, cols].unsqueeze(2).to_broadcast([P, SORT_COLS, TILES])
            all_ = lambda t: t[:, :].unsqueeze(1).to_broadcast([P, SORT_COLS, TILES])
            fields = packed[:, :].rearrange("p (t f) -> p t f", f=FIELDS)
            n_unsorted = dve.value_load(unsorted[0:1, 0:1], min_val=0, max_val=P * TILES)
            with dve.If(n_unsorted > 0):
                dve.wait_ge(iotas, 2)
                link(dve.tensor_scalar(runs_[:, :], runs_[:, :], 0.0, -0.5, ALU.is_lt, ALU.add))
                for g in range(TILES // SORT_COLS):
                    cols = slice(g * SORT_COLS, (g + 1) * SORT_COLS)
                    link(dve.tensor_tensor(grid[:, :, :], all_(dstf), own(dstf, cols), ALU.is_equal))
                    link(dve.tensor_tensor(earlier[:, :, :], all_(tile_no), own(tile_no, cols), ALU.is_lt))
                    link(dve.tensor_tensor(grid[:, :, :], grid[:, :, :], earlier[:, :, :], ALU.mult))
                    link(dve.tensor_reduce(rank[:, cols], grid[:, :, :], AX.X, ALU.add))
                before = n[0]
                per = 2 + 3 * (TILES // SORT_COLS)
                with dve.Fori(0, P) as r:
                    k = [0]

                    def link_r(ins):
                        k[0] += 1
                        ins.then_inc(steps, 1)
                        dve.wait_ge(steps, r * per + (before + k[0]))

                    dve.wait_ge(row_in, r * 16 + 16)
                    link_r(dve.tensor_copy(row[:, :], rowi[:, :]))
                    link_r(dve.tensor_scalar(bound[:, :], dstf[:, :], runs_[:, bass.ds(r, 1)], None, ALU.add))
                    for g in range(TILES // SORT_COLS):
                        cols = slice(g * SORT_COLS, (g + 1) * SORT_COLS)
                        link_r(dve.tensor_tensor(grid[:, :, :], all_(row), own(bound, cols), ALU.is_lt))
                        link_r(dve.tensor_reduce(counts[:, :], grid[:, :, :], AX.X, ALU.add))
                        link_r(dve.tensor_tensor(rank[:, cols], rank[:, cols], counts[:, :], ALU.add))
                    dve.sem_inc(counted, 1)
                n[0] = before + P * per
                link(dve.tensor_copy(ranki[:, :], rank[:, :]))
                for f, t in enumerate((src, dsti, etypei, eweight)):
                    link(dve.tensor_copy(fields[:, :, f], t[:, :].bitcast(I32) if t is eweight else t[:, :]))
                dve.sem_inc(ranked, 1)
                dve.wait_ge(sent_rows, 32 * TILES + 16)
                for f, t in enumerate((src, dsti, etypei, eweight)):
                    link(dve.tensor_copy(t[:, :].bitcast(I32) if t is eweight else t[:, :], fields[:, :, f]))
                link(dve.tensor_copy(dstf[:, :], dsti[:, :]))
            with dve.Else():
                dve.sem_inc(on, 1)
    sorting.end()

    w_in, const_done = sem("w_in"), sem("const_done")
    prep, prep_pe, zeroed, iota_done, cols_ready = sem("prep"), sem("prep_pe"), sem("zeroed"), sem("iota_done"), sem("cols_ready")
    with ExitStack() as c0:
        ZB = 7
        zero = sb("zero", [P, RB * W], c=c0)
        tf = [sb(f"tf{i}", [P, TILES], c=c0) for i in range(4)]
        cols = sb("cols", [P, 12], c=c0)
        hrf = sb("hrf", [P, 1], c=c0)
        rounded = sb("rounded", [3, C], BF16, c0)
        block = c0.enter_context(nc.Block())
        row_loads = [(K[n], D[n]) for n in ("bm2", "bu2", "ln_g", "ln_b", "gbias", "sb1", "sb2", "atts", "attd", "arb")]
        n_w = len(wload) + 1 + len(row_loads)

        @block.sync
        def _(sp):
            for o, i in wload:
                sp.dma_start(o, i).then_inc(w_in, 16)
            sp.dma_start(K["wgat"][:, 0:C], D["wgat"]).then_inc(w_in, 16)
            for o, i in row_loads:
                sp.dma_start(o[:, :], i.partition_broadcast(P)).then_inc(w_in, 16)

        @block.scalar
        def _(act):
            act.wait_ge(const_done, 1)
            dst = AGG.rearrange("(b p j) f -> p b (j f)", p=P, j=RB)
            for b in range(0, ROWS // BLOCK, ZB):
                act.dma_start(dst[:, b:b + ZB, :],
                              zero[:, :].unsqueeze(1).to_broadcast([P, ZB, RB * W])).then_inc(zeroed, 16)
            act.wait_ge(zeroed, 16 * (ROWS // BLOCK // ZB))

        @block.gpsimd
        def _(pool):
            pool.iota(iota_r[:, :], [[1, RELS]], base=0, channel_multiplier=0,
                      allow_small_or_imprecise_dtypes=True).then_inc(iota_done, 1)
            pool.iota(hrf[:, :], [[0, 1]], base=HEAD, channel_multiplier=1,
                      allow_small_or_imprecise_dtypes=True).then_inc(iota_done, 1)

        @block.vector
        def _(dve):
            n = [0]

            def link(ins):
                n[0] += 1
                ins.then_inc(prep, 1)
                dve.wait_ge(prep, n[0])

            nc.vector.memset(zero[:, :], 0.0).then_inc(const_done, 1)
            for u in range(RING):
                link(dve.memset(acc[u][:, :], 0.0))
            link(dve.memset(half[:, :], -0.5))
            link(dve.memset(one3[:, :], 1.0))
            inhead, notend, a, b = [t[:, :] for t in tf]
            link(dve.tensor_copy(etype[:, :], etypei[:, :]))
            link(dve.tensor_scalar(eweight1[:, :], eweight[:, :], -1.0, 1.0, ALU.mult, ALU.add))
            link(dve.tensor_scalar(a, dstf[:, :], float(N - 1), None, ALU.min))
            link(dve.tensor_copy(dst_gather[:, :], a))
            link(dve.memset(keep[:, 0:1], 0.0))
            link(dve.tensor_tensor(keep[:, 1:], dstf[:, 1:], dstf[:, :-1], ALU.is_equal))
            link(dve.tensor_scalar(reset[:, :], keep[:, :], -1.0, LOW, ALU.add, ALU.mult))
            link(dve.tensor_scalar(inhead, dstf[:, :], dstf[:, 0:1], None, ALU.is_equal))
            link(dve.memset(tf[1][:, TILES - 1:], 1.0))
            link(dve.tensor_copy(tf[1][:, 0:TILES - 1], keep[:, 1:]))
            dve.wait_ge(iota_done, 2)
            link(dve.tensor_scalar(a, dstf[:, :], -1.0, hrf[:, 0:1], ALU.mult, ALU.add))
            link(dve.tensor_tensor(a, a, inhead, ALU.mult))
            link(dve.tensor_tensor(a, a, dstf[:, :], ALU.add))
            link(dve.scalar_tensor_tensor(b, notend, AWAY, a, ALU.mult, ALU.add))
            link(dve.tensor_copy(target[:, :], b))
            df, dl, e1, e2, dl1, pl, nl = [cols[:, k:k + 1] for k in range(7)]
            link(dve.tensor_copy(df, dstf[:, 0:1]))
            link(dve.tensor_copy(dl, dstf[:, TILES - 1:]))
            dve.tensor_scalar(dl1, dl, 1.0, None, ALU.add).then_inc(cols_ready, 1)
            dve.wait_ge(prep_pe, 1)
            link(dve.tensor_scalar(pl, psum[2][:, 0:1], -1.0, None, ALU.add))
            link(dve.tensor_scalar(nl, psum[2][:, 1:2], -1.0, None, ALU.add))
            link(dve.tensor_tensor(e1, dl, nl, ALU.is_equal))
            link(dve.scalar_tensor_tensor(e2, e1, AWAY, dl, ALU.mult, ALU.add))
            link(dve.tensor_copy(t_index[:, :], e2))
            link(dve.tensor_tensor(e1, df, pl, ALU.is_equal))
            link(dve.tensor_tensor(e1, e1, tf[0][:, TILES - 1:], ALU.max))
            link(dve.scalar_tensor_tensor(e2, e1, AWAY, df, ALU.mult, ALU.add))
            link(dve.tensor_copy(h_index[:, :], e2))
            link(dve.tensor_scalar(seam["tt"][:, :], K["ones"][:, :], dl, None, ALU.mult))
            dve.tensor_scalar(seam["hh"][:, :], K["ones"][:, :], df, None, ALU.mult).then_inc(cols_ready, 1)
            dve.wait_ge(prep_pe, 2)
            link(dve.tensor_scalar(seam["th"][:, :], psum[0][:, 128:256], dl, None, ALU.is_equal))
            link(dve.tensor_scalar(seam["ht"][:, :], psum[0][:, 0:128], df, None, ALU.is_equal))
            link(dve.tensor_scalar(seam["tt"][:, :], psum[0][:, 0:128], dl, None, ALU.is_equal))
            link(dve.tensor_scalar(seam["hh"][:, :], psum[0][:, 128:256], df, None, ALU.is_equal))
            dve.wait_ge(w_in, 16 * n_w)
            link(dve.tensor_copy(bm2_parts[:, C:], K["ident"][0:3, 0:1]))
            link(dve.memset(gat_parts[:, C:], 0.0))
            link(dve.memset(gat_parts3[:, :], 0.0))
            for bias, o in ((K["bm2"], [bm2_parts[:, 0:C]]), (K["bu2"], [bu2_parts[:, j * C:(j + 1) * C] for j in range(4)]),
                            (K["gbias"], [gat_parts[:, 0:C]] + [gat_parts3[:, j * G:j * G + C] for j in range(3)])):
                rest, part, whole = [t[0:3, 0:C] for t in tf[0:3]]
                link(dve.tensor_copy(rest, bias[0:3, :]))
                link(dve.memset(whole, 0.0))
                for k in range(3):
                    link(dve.tensor_copy(rounded[:, :], rest))
                    link(dve.tensor_copy(part, rounded[:, :]))
                    link(dve.scalar_tensor_tensor(whole, part, K["ident"][0:3, k:k + 1], whole, ALU.mult, ALU.add))
                    link(dve.tensor_tensor(rest, rest, part, ALU.subtract))
                for o_ in o:
                    link(dve.tensor_copy(o_, whole))
            for name, o in (("atts", K["wgat"][:, C:]), ("attd", K["wdst"][:, :])):
                link(dve.tensor_tensor(K[name][:, :], K["wgat"][:, 0:C], K[name][:, :], ALU.mult))
                link(dve.tensor_reduce(o, K[name][:, :].rearrange("p (h d) -> p h d", h=HEADS), AX.X, ALU.add))
            link(dve.tensor_tensor(K["wnode"][:, C:], K["wgat"][:, C:], K["wdst"][:, :], ALU.add))
            link(dve.tensor_copy(K["wnode"][:, 0:C], K["wgat"][:, 0:C]))
            dve.wait_ge(prep_pe, 3)
            link(dve.tensor_tensor(bias_m[:, :], K["bm1"][:, :], psum[1][:, 0:1], ALU.add))
            link(dve.tensor_tensor(bias_u[:, :], K["bu1"][:, :], psum[1][:, 1:2], ALU.add))

        @block.tensor
        def _(pe):
            pe.wait_ge(cols_ready, 1)
            pe.matmul(psum[2][:, 0:1], shift_down[:, :], cols[:, 4:5], start=True, stop=True)
            pe.matmul(psum[2][:, 1:2], shift_up[:, :], cols[:, 4:5], start=True, stop=True).then_inc(prep_pe, 1)
            pe.wait_ge(cols_ready, 2)
            pe.matmul(psum[0][:, 0:128], seam["tt"][:, :], K["ident"][:, :], start=True, stop=True)
            pe.matmul(psum[0][:, 128:256], seam["hh"][:, :], K["ident"][:, :],
                      start=True, stop=True).then_inc(prep_pe, 1)
            pe.wait_ge(w_in, 16 * n_w)
            pe.matmul(psum[1][:, 0:1], K["wm1g"][:, :], K["gstate"][:, :], start=True, stop=True)
            pe.matmul(psum[1][:, 1:2], K["wu1g"][:, :], K["gstate"][:, :],
                      start=True, stop=True).then_inc(prep_pe, 1)

    def edge_phase(name, kind, table):
        own = Phase(name)
        edges(name, kind, table, own)
        own.end()

    def edges(name, kind, table, s):
        two = kind == "gat"
        got = [s(f"got{q}") for q in range(RING)]
        sent = [s(f"sent{q}") for q in range(RING)]
        idx_ready, pool_on = s("idx_ready"), s("pool_on")
        turned, xt_ready = s("turned"), s("xt_ready")
        acc_ready, msg_ready = s("acc_ready"), s("msg_ready")
        c = ExitStack()
        with c:
            xt = [sb(f"{name}_xt{k}", [P, 2 * C], c=c) for k in range(2)]
            if two:
                xd = [sb(f"{name}_xd{q}", [P, C], c=c) for q in range(RING)]
                small = sb(f"{name}_small", [P, 8, HEADS], c=c)
                diff = [sb(f"{name}_diff{k}", [P, 2, HEADS], c=c) for k in range(2)]
                part = [sb(f"{name}_part{k}", [P, 2, HEADS], c=c) for k in range(2)]
                scaled = sb(f"{name}_scaled", [P, C], c=c)
                weighed = sb(f"{name}_weighed", [P, C], c=c)
                diff_ready, part_ready = s("diff_ready"), s("part_ready")
            if kind == "mlp":
                ea = [sb(f"{name}_ea{h}", [P, ET // 2 * ED], c=c) for h in range(2)]
                zt = [sb(f"{name}_zt{k}", [P, C], c=c) for k in range(2)]
                onehot = sb(f"{name}_onehot", [P, ET, RELS], c=c)
                prod = sb(f"{name}_prod", [P, ET, RELS], c=c)
                ea_got = [s(f"ea_got{h}") for h in range(2)]
                eat_ready, hid_ready, zt_ready = s("eat_ready"), s("hid_ready"), s("zt_ready")
            step_sem = s("dve_steps")
            msg_read = s("msg_read") if kind == "bases" else acc_ready
            run = [sb(f"{name}_run{k}", [P, C], c=c) for k in range(2)]
            block = c.enter_context(nc.Block())
            LAG = 1 if kind == "mlp" else 0
            LAG_SUM = 2 if kind == "mlp" else 0

            if kind == "mlp":
                @block.sync
                def _(sp):
                    def load_from(attributes):
                        def body(i):
                            for h in range(2):
                                up_to(sp, turned, i * ET - ET + (h + 1) * RING if not isinstance(i, int) or i else 0)
                                sp.dma_start(ea[h][:, :], attributes[:, bass.ds(i * (ET * ED) + h * (RING * ED), RING * ED)])\
                                  .then_inc(ea_got[h], 16)

                        edge_steps(sp, body)

                    n_unsorted = sp.value_load(unsorted[0:1, 0:1], min_val=0, max_val=P * TILES)
                    with sp.If(n_unsorted > 0):
                        load_from(ATTRS.rearrange("(p t) d -> p (t d)", p=P))
                    with sp.Else():
                        load_from(D["eattr"])

            @block.gpsimd
            def _(pool):
                def gather(h, q):
                    pool.indirect_dma_start(xs[q][:, :], None, table, bass.IndirectOffsetOnAxis(
                        ap=src_now[h][:, q:q + 1], axis=0)).then_inc(got[q], 16)
                    if two:
                        pool.indirect_dma_start(xd[q][:, :], None, table, bass.IndirectOffsetOnAxis(
                            ap=dst_now[h][:, q:q + 1], axis=0)).then_inc(got[q], 16)

                def copy_index(o, table_, t):
                    pool.tensor_copy(o[:, :], table_[:, bass.ds(t, RING)]).then_inc(idx_ready, 1)

                per = 3 if two else 2

                copy_index(src_now[0], src, 0)
                if two:
                    copy_index(dst_now[0], dst_gather, 0)
                pool.wait_ge(idx_ready, per - 1)
                for q in range(RING):
                    gather(0, q)

                def body(i):
                    for h in range(2):
                        last = isinstance(i, int) and i == ESTEPS - 1 and h == 1
                        for q in range(RING):
                            t = i * ET + h * RING + q
                            pool.wait_ge(acc_ready, t + 1)
                            pool.sem_inc(pool_on, 1)
                            if q == 0:
                                copy_index(target_now[h], target, t)
                                if not last:
                                    copy_index(src_now[1 - h], src, t + RING)
                                    if two:
                                        copy_index(dst_now[1 - h], dst_gather, t + RING)
                                pool.wait_ge(idx_ready, per - 1 + (i * 2 + h) * per + (1 if last else per))
                                pool.sem_inc(pool_on, 1)
                            pool.indirect_dma_start(AGG, bass.IndirectOffsetOnAxis(ap=target_now[h][:, q:q + 1], axis=0),
                                                    acc[q][:, :], None, bounds_check=ROWS - 1, oob_is_err=False)\
                                .then_inc(sent[q], 16)
                            if not last:
                                gather(1 - h, q)

                edge_steps(pool, body)
                for q in range(RING):
                    pool.wait_ge(sent[q], 16 * 2 * ESTEPS)

            per_got = 32 if two else 16

            @block.tensor
            def _(pe):
                def turn(i, u, t):
                    k, q = u % 2, u % RING
                    pe.wait_ge(got[q], (i * 2 + u // RING + 1) * per_got)
                    up_to(pe, xt_ready, t - 1)
                    if kind == "mlp":
                        up_to(pe, eat_ready, t - 1)
                        pe.wait_ge(ea_got[u // (ET // 2)], (i + 1) * 16)
                        v = u % (ET // 2)
                        pe.transpose(psum[k][:, 0:C], xs[q][:, :], K["ident"][:, :])
                        pe.transpose(psum[6 + k][0:ED, 0:C], ea[u // (ET // 2)][:, v * ED:(v + 1) * ED],
                                     K["ident"][:, :]).then_inc(turned, 1)
                    elif two:
                        pe.transpose(psum[k][:, 0:C], xs[q][:, :], K["ident"][:, :])
                        pe.transpose(psum[k][:, C:2 * C], xd[q][:, :], K["ident"][:, :]).then_inc(turned, 1)
                    else:
                        pe.transpose(psum[k][:, 0:C], xs[q][:, :], K["ident"][:, :]).then_inc(turned, 1)

                def hidden(u, t):
                    k = u % 2
                    pe.wait_ge(xt_ready, t + 1)
                    pe.wait_ge(eat_ready, t + 1)
                    up_to(pe, zt_ready, t - 1)
                    pe.matmul(psum[2 + k][:, 0:C], K["wm1x"][:, :], xt[k][:, 0:C], start=True, stop=False)
                    pe.matmul(psum[2 + k][:, 0:C], K["wm1e"][:, :], xt[k][0:ED, C:2 * C],
                              start=False, stop=True).then_inc(hid_ready, 1)

                def message(u, t):
                    k = u % 2
                    x_t = xt[k]
                    pe.wait_ge(zt_ready if kind == "mlp" else xt_ready, t + 1)
                    up_to(pe, msg_read, t - 1)
                    if kind == "mlp":
                        pe.matmul(psum[4 + k][:, 0:C + 1], one3[:, :], bm2_parts[:, :], start=True, stop=False)
                        pe.matmul(psum[4 + k][:, 0:C], zt[k][:, :], K["wm2"][:, :],
                                  start=False, stop=True).then_inc(msg_ready, 1)
                    elif two:
                        pe.matmul(psum[4 + k][:, 0:C + HEADS], one3[:, :], gat_parts[:, :], start=True, stop=False)
                        pe.matmul(psum[4 + k][:, 0:C + HEADS], x_t[:, 0:C], K["wgat"][:, :], start=False, stop=False)
                        pe.matmul(psum[4 + k][:, C:C + HEADS], x_t[:, C:2 * C], K["wdst"][:, :],
                                  start=False, stop=True).then_inc(msg_ready, 1)
                    else:
                        w = K["vb"] if kind == "bases" else K["sw1"] if kind == "spline1" else K["sw2"]
                        n = BASES * C if kind == "bases" else 2 * C
                        pe.matmul(psum[4 + k][:, 0:n], x_t[:, 0:C], w[:, :], start=True, stop=True).then_inc(msg_ready, 1)

                turn(0, 0, 0)

                def body(i):
                    for u in range(ET):
                        t = i * ET + u
                        if u + 1 < ET:
                            turn(i, u + 1, t + 1)
                        elif not (isinstance(i, int) and i == ESTEPS - 1):
                            turn(i + 1, 0, t + 1)
                        if kind == "mlp":
                            hidden(u, t)
                        if not (isinstance(t, int) and t < LAG):
                            message(u - LAG, t - LAG)

                edge_steps(pe, body)
                if LAG:
                    message(ET - 1, TILES - 1)

            @block.scalar
            def _(act):
                def relu(u, t):
                    k = u % 2
                    act.wait_ge(hid_ready, t + 1)
                    up_to(act, msg_ready, t - 1)
                    act.activation(zt[k][:, :], psum[2 + k][:, 0:C], ACT.Relu,
                                   bias=bias_m[:, 0:1]).then_inc(zt_ready, 1)

                def body(i):
                    for u in range(ET):
                        t, k = i * ET + u, u % 2
                        act.wait_ge(turned, t + 1)
                        up_to(act, hid_ready if kind == "mlp" else msg_ready, t - 1)
                        n = 2 * C if two else C
                        act.activation(xt[k][:, 0:n], psum[k][:, 0:n], ACT.Copy).then_inc(xt_ready, 1)
                        if kind == "mlp" and not (isinstance(t, int) and t < LAG):
                            relu(u - LAG, t - LAG)
                        if two:
                            act.wait_ge(diff_ready, t + 1)
                            up_to(act, acc_ready, t - 1)
                            act.activation(part[k][:, :, :], diff[k][:, :, :], ACT.Exp).then_inc(part_ready, 1)

                edge_steps(act, body)
                if LAG:
                    relu(ET - 1, TILES - 1)

            @block.vector
            def _(dve):
                steps = {"mlp": 10, "gat": 9, "bases": 3, "spline1": 2, "spline2": 2}[kind]
                link = Chain(dve, step_sem, steps)

                def column(tensor, t):
                    return tensor[:, bass.ds(t, 1)]

                def coefficients(i, n):
                    lo = bass.ds(i * ET, ET)
                    b = (n - 1) // 2
                    link.start(i)
                    link.k = n
                    if n == 0:
                        link(dve.tensor_tensor(onehot[:, :, :], etype[:, lo].unsqueeze(2).to_broadcast([P, ET, RELS]),
                                               iota_r[:, :].unsqueeze(1).to_broadcast([P, ET, RELS]), ALU.is_equal))
                    elif n == 9:
                        link(dve.tensor_tensor(coef[:, lo, :], coef[:, lo, :],
                                               eweight[:, lo].unsqueeze(2).to_broadcast([P, ET, BASES]), ALU.mult))
                    elif n % 2:
                        link(dve.tensor_tensor(prod[:, :, :], onehot[:, :, :], K["arb"][:, b * RELS:(b + 1) * RELS]
                                               .unsqueeze(1).to_broadcast([P, ET, RELS]), ALU.mult))
                    else:
                        link(dve.tensor_reduce(coef[:, lo, b], prod[:, :, :], AX.X, ALU.add))

                def body(i):
                    for u in range(ET):
                        t, k = i * ET + u, u % 2
                        if kind == "mlp":
                            dve.wait_ge(turned, t + 1)
                            up_to(dve, hid_ready, t - 1)
                            dve.tensor_copy(xt[k][0:ED, C:2 * C], psum[6 + k][0:ED, 0:C]).then_inc(eat_ready, 1)
                        if kind == "bases":
                            weigh_bases(i, u, t)
                        elif not (isinstance(t, int) and t < LAG_SUM):
                            add(i, u - LAG_SUM, t - LAG_SUM)
                        if kind == "mlp" and 1 <= u <= 10:
                            coefficients(i, u - 1)

                def add(i, u, t):
                    k, q = u % 2, u % RING
                    now, before = acc[q], acc[(q - 1) % RING]
                    msg = psum[4 + k]
                    if kind != "mlp":
                        link.start(t)
                    up_to(dve, acc_ready, t)
                    up_to(dve, sent[q], i * 2 + u // RING, 16)
                    if kind == "spline1" or kind == "spline2":
                        link(dve.tensor_scalar(run[0][:, :], before[:, 0:C], column(keep, t), None, ALU.mult))
                    dve.wait_ge(msg_ready, t + 1)
                    if kind == "mlp":
                        dve.scalar_tensor_tensor(now[:, 0:C + 1], before[:, 0:C + 1], column(keep, t),
                                                 msg[:, 0:C + 1], ALU.mult, ALU.add).then_inc(acc_ready, 1)
                    elif kind != "gat":
                        link(dve.scalar_tensor_tensor(run[1][:, :], msg[:, 0:C], column(eweight1, t), run[0][:, :],
                                                      ALU.mult, ALU.add))
                        dve.scalar_tensor_tensor(now[:, 0:C], msg[:, C:2 * C], column(eweight, t), run[1][:, :],
                                                 ALU.mult, ALU.add).then_inc(acc_ready, 1)
                    else:
                        e2, e, m_in = small[:, 0, :], small[:, 1, :], small[:, 2, :]
                        z = msg[:, C:C + HEADS]
                        link(dve.tensor_scalar(e2, z, 0.2, None, ALU.mult))
                        link(dve.tensor_tensor(e, z, e2, ALU.max))
                        link(dve.tensor_scalar(m_in, before[:, C + 4:C + 8], column(reset, t), None, ALU.add))
                        link(dve.tensor_tensor(now[:, C + 4:C + 8], m_in, e, ALU.max))
                        up_to(dve, part_ready, t - 1)
                        link(dve.tensor_tensor(diff[k][:, 1, :], e, now[:, C + 4:C + 8], ALU.subtract))
                        dve.tensor_tensor(diff[k][:, 0, :], m_in, now[:, C + 4:C + 8], ALU.subtract)\
                            .then_inc(diff_ready, 1)
                        dve.wait_ge(part_ready, t + 1)
                        old, new = part[k][:, 0, :], part[k][:, 1, :]
                        heads = lambda v: v.rearrange("p (h d) -> p h d", h=HEADS)
                        spread = lambda v: v.unsqueeze(2).to_broadcast([P, HEADS, HD])
                        link(dve.tensor_tensor(small[:, 3, :], before[:, C:C + 4], old, ALU.mult))
                        link(dve.tensor_tensor(now[:, C:C + 4], small[:, 3, :], new, ALU.add))
                        link(dve.tensor_tensor(heads(scaled[:, :]), heads(before[:, 0:C]), spread(old), ALU.mult))
                        link(dve.tensor_tensor(heads(weighed[:, :]), heads(msg[:, 0:C]), spread(new), ALU.mult))
                        dve.tensor_tensor(now[:, 0:C], scaled[:, :], weighed[:, :], ALU.add).then_inc(acc_ready, 1)
                def weigh_bases(i, u, t):
                    msg, o = psum[4 + u % 2], run[u % 2][:, :]
                    dve.wait_ge(msg_ready, t + 1)
                    for b in range(BASES):
                        m, cf = msg[:, b * C:(b + 1) * C], coef[:, bass.ds(t, 1), b]
                        if b == 0:
                            dve.tensor_scalar(o, m, cf, None, ALU.mult).then_inc(step_sem, 1)
                            if not (isinstance(t, int) and t == 0):
                                add_bases(i, u - 1, t - 1)
                            continue
                        dve.wait_ge(step_sem, t * (BASES - 1) + b)
                        dve.scalar_tensor_tensor(o, m, cf, o, ALU.mult, ALU.add)\
                            .then_inc(step_sem if b + 1 < BASES else msg_read, 1)

                def add_bases(i, u, t):
                    q = u % RING
                    up_to(dve, acc_ready, t)
                    up_to(dve, sent[q], i * 2 + u // RING, 16)
                    dve.wait_ge(msg_read, t + 1)
                    dve.scalar_tensor_tensor(acc[q][:, 0:C], acc[(q - 1) % RING][:, 0:C], column(keep, t), run[u % 2][:, :],
                                             ALU.mult, ALU.add).then_inc(acc_ready, 1)

                edge_steps(dve, body)
                if kind == "bases":
                    add_bases(ESTEPS - 1, ET - 1, TILES - 1)
                for u in range(ET - LAG_SUM, ET):
                    add(ESTEPS - 1, u, TILES - ET + u)

        loaded, joined, copied, written, steps2 = s("seam_loaded"), s("seam_joined"), s("seam_copied"), s("seam_written"), s("seam_steps")
        spread_rows, exped = s("seam_rows"), s("seam_exp")
        c = ExitStack()
        with c:
            tail = acc[RING - 1]
            if two:
                sm = sb(f"{name}_sm", [P, 10, HEADS], c=c)
                mx = sb(f"{name}_mx", [P, HEADS, P], c=c)
                bc = sb(f"{name}_bc", [P, 2, HEADS, P], c=c)
                mask = {m: sb(f"{name}_mask_{m}", [P, P], c=c) for m in seam}
                tr = sb(f"{name}_tr", [P, W], c=c)
            block = c.enter_context(nc.Block())

            @block.sync
            def _(sp):
                sp.dma_start(hrow[:, :], head_rows).then_inc(loaded, 16)

            last = tr if two else tail
            width = C + 8 if not two else C + HEADS

            @block.tensor
            def _(pe):
                pe.wait_ge(loaded, 16)
                if two:
                    pe.wait_ge(spread_rows, 1)
                    for a in range(2):
                        for h in range(HEADS):
                            q = pe.matmul(psum[2 + a][:, h * P:(h + 1) * P], bc[:, a, h, :], K["ident"][:, :],
                                          start=True, stop=True)
                    q.then_inc(spread_rows, 1)
                    pe.wait_ge(exped, 2)
                pe.matmul(psum[0][:, 0:width], seam["tt"][:, :], last[:, 0:width], start=True, stop=False)
                pe.matmul(psum[0][:, 0:width], seam["ht"][:, :], hrow[:, 0:width],
                          start=False, stop=True).then_inc(joined, 1)

            @block.vector
            def _(dve):
                n = [0]

                def link(ins):
                    n[0] += 1
                    ins.then_inc(steps2, 1)
                    dve.wait_ge(steps2, n[0])

                if two:
                    heads = lambda v: v.rearrange("p (h d) -> p h d", h=HEADS)
                    spread = lambda v, k: v.unsqueeze(2).to_broadcast([P, HEADS, k])
                    dve.wait_ge(loaded, 16)
                    nosum, mh, mt = sm[:, 0, :], sm[:, 1, :], tail[:, C + 4:C + 8]
                    link(dve.tensor_scalar(nosum, hrow[:, C:C + 4], 0.0, -LOW, ALU.is_equal, ALU.mult))
                    link(dve.tensor_tensor(mh, hrow[:, C + 4:C + 8], nosum, ALU.add))
                    for m in seam:
                        link(dve.tensor_scalar(mask[m][:, :], seam[m][:, :], -1.0, LOW, ALU.add, ALU.mult))
                    link(dve.tensor_copy(bc[:, 0, :, :], spread(mt, P)))
                    dve.tensor_copy(bc[:, 1, :, :], spread(mh, P)).then_inc(spread_rows, 1)
                    dve.wait_ge(spread_rows, 2)
                    for a, (m_t, m_h) in enumerate((("tt", "th"), ("ht", "hh"))):
                        for b, m in enumerate((m_t, m_h)):
                            link(dve.tensor_tensor(mx[:, :, :], psum[2 + b][:, :].rearrange("p (h j) -> p h j", h=HEADS),
                                                   mask[m][:, :].unsqueeze(1).to_broadcast([P, HEADS, P]), ALU.add))
                            link(dve.tensor_reduce(sm[:, 2 + b, :], mx[:, :, :], AX.X, ALU.max))
                        link(dve.tensor_tensor(sm[:, 4 + a, :], sm[:, 2, :], sm[:, 3, :], ALU.max))
                    link(dve.tensor_tensor(sm[:, 6, :], mt, sm[:, 4, :], ALU.subtract))
                    dve.tensor_tensor(sm[:, 7, :], mh, sm[:, 5, :], ALU.subtract).then_inc(exped, 1)
                    dve.wait_ge(copied, 1)
                    ft, fh = sm[:, 8, :], sm[:, 9, :]
                    for o, i, f in ((tr, tail, ft), (hrow, hrow, fh)):
                        link(dve.tensor_tensor(heads(o[:, 0:C]), heads(i[:, 0:C]), spread(f, HD), ALU.mult))
                        ins = dve.tensor_tensor(o[:, C:C + 4], i[:, C:C + 4], f, ALU.mult)
                        if o is tr:
                            link(ins)
                        else:
                            ins.then_inc(exped, 1)
                    dve.wait_ge(joined, 1)
                    link(dve.tensor_copy(trow[:, C + 4:C + 8], sm[:, 4, :]))
                    link(dve.tensor_copy(hrow[:, C + 4:C + 8], sm[:, 5, :]))
                    dve.tensor_copy(trow[:, 0:width], psum[0][:, 0:width]).then_inc(copied, 1)
                else:
                    dve.wait_ge(joined, 1)
                    dve.tensor_copy(trow[:, 0:width], psum[0][:, 0:width]).then_inc(copied, 1)

            if two:
                @block.scalar
                def _(act):
                    act.wait_ge(exped, 1)
                    act.activation(sm[:, 8:10, :], sm[:, 6:8, :], ACT.Exp).then_inc(copied, 1)

            @block.gpsimd
            def _(pool):
                pool.wait_ge(copied, 2 if two else 1)
                pool.wait_ge(loaded, 16)
                for row, index in ((trow, t_index), (hrow, h_index)):
                    pool.indirect_dma_start(AGG, bass.IndirectOffsetOnAxis(ap=index[:, 0:1], axis=0), row[:, :], None,
                                            bounds_check=ROWS - 1, oob_is_err=False).then_inc(written, 16)
                pool.wait_ge(written, 32)

    def node_phase(name, kind, x_in, x_res, x_out):
        own = Phase(name)
        nodes(name, kind, x_in, x_res, x_out, own)
        own.end()

    def nodes(name, kind, x_in, x_res, x_out, s):
        mlp, gat, res, norm = kind == "mlp", kind == "gat", kind == "spline2", kind != "spline1"
        SLOTS = 6
        x_got = [s(f"x_got{u}") for u in range(SLOTS)]
        a_got = [s(f"a_got{u}") for u in range(SLOTS)]
        r_got = [s(f"r_got{u}") for u in range(SLOTS)] if res else None
        stored = [s(f"stored{u}") for u in range(SLOTS)]
        turned, xt_ready, o_ready = s("turned"), s("xt_ready"), s("o_ready")
        y_ready, v_ready, r_ready, out_ready = s("y_ready"), s("v_ready"), s("r_ready"), s("out_ready")
        step_sem, pool_steps, a_used = s("steps"), s("pool_steps"), s("a_used")
        if mlp:
            a_scaled = [s(f"a_scaled{h}") for h in range(2)]
            pool_on, inv_ready, pool_out_ready = s("pool_on"), s("inv_ready"), s("pool_out_ready")
            a_turned, at_ready, hid_ready, rt_ready = s("a_turned"), s("at_ready"), s("hid_ready"), s("rt_ready")
            n1_ready, xl_ready, gained, l_ready = s("n1_ready"), s("xl_ready"), s("gained"), s("l_ready")
            degree_ready = s("degree_ready")
        if kind == "rgcn" or res:
            added = s("added")
        if res:
            xb_ready = s("xb_ready")
        if gat:
            w_applied, own_ready = s("w_applied"), s("own_ready")
            d_ready, e_ready, w_ready, a_weighed = s("d_ready"), s("e_ready"), s("w_ready"), s("a_weighed")
            score_steps, weigh_steps = s("score_steps"), s("weigh_steps")
        c = ExitStack()
        with c:
            def ring(what, width, n=SLOTS):
                return [sb(f"{name}_{what}{u}", [P, width], c=c) for u in range(n)]

            X, A, Y = ring("X", RB * C), ring("A", RB * W), ring("Y", RB * C)
            if res:
                B = ring("B", RB * C)
            if res:
                R = ring("R", RB * C)
            xt = [ring(f"xt{k}_", 512, 2) for k in range(2)]
            if mlp:
                at = [ring(f"at{k}_", 512, 2) for k in range(2)]
                rt = [ring(f"rt{k}_", 512, 2) for k in range(2)]
                L = ring("L", RB * C)
                degree = sb(f"{name}_degree", [P, RB], c=c)
                inverse = ring("inverse", RB, 2)
            if gat:
                g_small = sb(f"{name}_gs", [P, 4, RB * HEADS], c=c)
                g_edges = [sb(f"{name}_ge{k}", [P, RB * HEADS], c=c) for k in range(2)]
                g_diff = [sb(f"{name}_gd{k}", [P, 2, RB * HEADS], c=c) for k in range(2)]
                g_exp = [sb(f"{name}_gx{k}", [P, 2, RB * HEADS], c=c) for k in range(2)]
            ROUND = 2 * RB if mlp else RB
            stat = [sb(f"{name}_stat{k}", [P, ROUND, 6], c=c) for k in range(2)]
            tmp = sb(f"{name}_tmp", [P, 3, ROUND], c=c)
            msum, var, rstd, shift = ring("msum", ROUND), ring("var", ROUND), ring("rstd", ROUND), ring("shift", ROUND)

            def in_round(r):
                if not mlp or not isinstance(r, int):
                    return slice(0, ROUND)
                return slice(0 if r < BLOCKS else RB, ROUND if r >= 2 else RB)

            block = c.enter_context(nc.Block())
            rows3 = lambda t: t[:, :].rearrange("p (j f) -> p j f", j=RB)
            sums3 = lambda t: t[:, :].rearrange("p (j w) -> p j w", w=W)
            halves = lambda t, h: rows3(t)[:, 4 * h:4 * h + 4, :]
            bank3 = lambda b: psum[b][:, :].rearrange("p (j f) -> p j f", j=4)
            per_row = lambda r: r[:, :].unsqueeze(1).to_broadcast([P, RB, C])
            GAT_ROWS = ((0, 3), (3, 3), (6, 2))
            gat_bank = lambda u, g, n: psum[2 + 3 * (u % 2) + g][:, 0:n * G].rearrange("p (r w) -> p r w", w=G)
            out_bank = lambda u, h: (6 if mlp or u % 2 == 0 else 2) + h
            OUT = L if mlp else Y
            ACT_ROWS = 5 if mlp else RB

            @block.sync
            def _(sp):
                def load_a(b, u, i):
                    up_to(sp, a_turned if mlp else a_used, b - SLOTS + 1, 2 if mlp else 1)
                    sp.dma_start(A[u][:, :], rows_of(AGG, b, W)).then_inc(a_got[u], 16)

                def load_x(b, u, i):
                    if mlp:
                        up_to(sp, y_ready, b - SLOTS + 1, 2)
                        up_to(sp, xl_ready, b - SLOTS + 1)
                    elif gat:
                        up_to(sp, turned, b - SLOTS + 1, 2)
                        up_to(sp, a_weighed, b - SLOTS + 1)
                    elif kind == "rgcn":
                        up_to(sp, added, b - SLOTS + 1)
                    else:
                        up_to(sp, turned, b - SLOTS + 1, 2)
                    sp.dma_start(X[u][:, :], rows_of(x_in, b, C)).then_inc(x_got[u], 16)
                    if res:
                        up_to(sp, xb_ready, b - SLOTS + 1)
                        sp.dma_start(R[u][:, :], rows_of(x_res, b, C)).then_inc(r_got[u], 16)

                def store(b, u, i):
                    sp.wait_ge(out_ready, b + 1)
                    if mlp:
                        sp.wait_ge(pool_out_ready, b + 1)
                    if isinstance(b, int) and b == BLOCKS - 1:
                        sp.wait_ge(stored[(u - 1) % SLOTS], 16 * ((b - 1) // SLOTS + 1))
                    sp.dma_start(rows_of(x_out, b, C), OUT[u][:, :]).then_inc(stored[u], 16)

                pipeline(sp, SLOTS, *{"mlp": [(0, load_a), (2, load_x), (9, store)],
                                      "gat": [(0, load_a), (0, load_x), (7, store)]}
                         .get(kind, [(0, load_a), (0, load_x), (6, store)]))
                for u in range(SLOTS):
                    sp.wait_ge(stored[u], 16 * ((BLOCKS - 1 - u) // SLOTS + 1))

            @block.gpsimd
            def _(pool):
                def roots(r, u, i):
                    w = in_round(r)
                    link = Chain(pool, pool_steps, 2)
                    link.start(r)
                    pool.wait_ge(v_ready, r + 1)
                    link(pool.tensor_tensor(rstd[u][:, w], var[u][:, w], half[:, w], ALU.pow))
                    link(pool.tensor_tensor(msum[u][:, w], msum[u][:, w], half[:, w], ALU.mult))
                    pool.tensor_tensor(shift[u][:, w], msum[u][:, w], rstd[u][:, w], ALU.mult).then_inc(r_ready, 1)

                def add_bias(b, u, i):
                    up_to(pool, added, b - SLOTS + 1)
                    pool.wait_ge(r_got[u], (i + 1) * 16)
                    pool.tensor_tensor(rows3(B[u]), rows3(R[u]), per_row(K["sb2"]), ALU.add)\
                        .then_inc(xb_ready, 1)

                def add_ln_b(b, u, i):
                    pool.wait_ge(x_got[u], (i + 1) * 16)
                    up_to(pool, stored[u], i, 16)
                    pool.tensor_tensor(rows3(L[u]), rows3(X[u]), per_row(K["ln_b"]), ALU.add).then_inc(xl_ready, 1)

                def weigh_edges(b, u, i):
                    pool.wait_ge(w_ready, b + 1)
                    v = sums3(A[u])[:, :, 0:C].rearrange("p j (h d) -> p j h d", h=HEADS)
                    pool.tensor_tensor(v, v, g_edges[u % 2][:, :].rearrange("p (j h) -> p j h", h=HEADS).unsqueeze(3)
                                       .to_broadcast([P, RB, HEADS, HD]), ALU.mult).then_inc(w_applied, 1)
                    pool.wait_ge(x_got[u], (i + 1) * 16)
                    pool.wait_ge(w_applied, b + 1)
                    v = sums3(A[u])[:, :, 0:C]
                    pool.tensor_tensor(v, v, rows3(X[u]), ALU.add).then_inc(a_weighed, 1)

                def scale_half(b, u, i):
                    pool.wait_ge(inv_ready, b + 1)
                    v = sums3(A[u])[:, 0:4, 0:C]
                    pool.tensor_tensor(v, v, inverse[u % 2][:, 0:4].unsqueeze(2).to_broadcast([P, 4, C]), ALU.mult)\
                        .then_inc(a_scaled[0], 1)

                def normalise_rest(b, u, i):
                    pool.wait_ge(r_ready, b + 3)
                    pool.sem_inc(pool_on, 1)
                    v = (u + 2) % SLOTS
                    for j in range(ACT_ROWS, RB):
                        row = L[u][:, j * C:(j + 1) * C]
                        ins = pool.tensor_scalar(row, row, rstd[v][:, RB + j:RB + j + 1], shift[v][:, RB + j:RB + j + 1],
                                                 ALU.mult, ALU.add)
                    ins.then_inc(pool_out_ready, 1)

                if mlp:
                    pipeline(pool, SLOTS, (0, scale_half), (4, roots, 2), (6, normalise_rest),
                             (2, add_ln_b))
                elif gat:
                    pipeline(pool, SLOTS, (2, weigh_edges), (3, roots))
                elif res:
                    pipeline(pool, SLOTS, (0, add_bias), (2, roots))
                elif norm:
                    pipeline(pool, SLOTS, (2, roots))

            @block.tensor
            def _(pe):
                def turn_x(b, u, i):
                    pe.wait_ge(x_got[u], (i + 1) * 16)
                    for h in range(2):
                        up_to(pe, xt_ready, (b - 1) * 2 + h + 1)
                        for j in range(4):
                            q = pe.transpose(psum[h][:, j * P:(j + 1) * P], X[u][:, (4 * h + j) * C:(4 * h + j + 1) * C],
                                             K["ident"][:, :])
                        q.then_inc(turned, 1)

                def turn_a(b, u, i):
                    for h in range(2):
                        pe.wait_ge(a_scaled[h], b + 1)
                        up_to(pe, at_ready, (b - 1) * 2 + h + 1)
                        for j in range(4):
                            q = pe.transpose(psum[2 + h][:, j * P:(j + 1) * P],
                                             A[u][:, (4 * h + j) * W:(4 * h + j) * W + C], K["ident"][:, :])
                        q.then_inc(a_turned, 1)

                def hidden(b, u, i):
                    for h in range(2):
                        pe.wait_ge(xt_ready, b * 2 + h + 1)
                        pe.wait_ge(at_ready, b * 2 + h + 1)
                        up_to(pe, rt_ready, (b - 1) * 2 + h + 1)
                        pe.matmul(psum[4 + h][:, :], K["wu1x"][:, :], xt[u % 2][h][:, :], start=True, stop=False)
                        pe.matmul(psum[4 + h][:, :], K["wu1a"][:, :], at[u % 2][h][:, :], start=False, stop=True)\
                            .then_inc(hid_ready, 1)

                def gat_output(b, u, i):
                    up_to(pe, y_ready, (b - 2) * 2 + 2)
                    up_to(pe, d_ready, b - 1)
                    for g, (first, n) in enumerate(GAT_ROWS):
                        bank = psum[2 + 3 * (u % 2) + g]
                        pe.matmul(bank[:, 0:n * G], one3[:, :], gat_parts3[:, 0:n * G], start=True, stop=False)
                        for r in range(n):
                            h, j = divmod(first + r, 4)
                            if j == 0:
                                pe.wait_ge(xt_ready, b * 2 + h + 1)
                            q = pe.matmul(bank[:, r * G:(r + 1) * G], xt[u % 2][h][:, j * P:(j + 1) * P], K["wnode"][:, :],
                                          start=False, stop=r == n - 1)
                            if j == 3:
                                q.then_inc(o_ready, 1)

                def output(b, u, i):
                    w = {"mlp": K["wu2"][:, :], "rgcn": K["loop"][:, :],
                         "spline1": K["root1"][:, :], "spline2": K["root2"][:, :]}[kind]
                    lhs, ready = (rt, rt_ready) if mlp else (xt, xt_ready)
                    for h in range(2):
                        pe.wait_ge(ready, b * 2 + h + 1)
                        up_to(pe, y_ready, (b - (1 if mlp else 2)) * 2 + h + 1)
                        bank = out_bank(u, h)
                        if mlp:
                            pe.matmul(psum[bank][:, :], one3[:, :], bu2_parts[:, :], start=True, stop=False)
                        for j in range(4):
                            q = pe.matmul(psum[bank][:, j * C:(j + 1) * C], lhs[u % 2][h][:, j * P:(j + 1) * P], w,
                                          start=not mlp, stop=not mlp or j == 3)
                        q.then_inc(o_ready, 1)

                if mlp:
                    pipeline(pe, SLOTS, (0, turn_x), (0, turn_a), (1, hidden), (2, output))
                else:
                    pipeline(pe, SLOTS, (0, turn_x), (1, gat_output if gat else output))

            @block.scalar
            def _(act):
                def copy_x(b, u, i):
                    for h in range(2):
                        act.wait_ge(turned, b * 2 + h + 1)
                        up_to(act, hid_ready if mlp else o_ready, (b - 2) * 2 + h + 1)
                        act.activation(xt[u % 2][h][:, :], psum[h][:, :], ACT.Copy).then_inc(xt_ready, 1)

                def copy_a(b, u, i):
                    for h in range(2):
                        act.wait_ge(a_turned, b * 2 + h + 1)
                        up_to(act, hid_ready, (b - 2) * 2 + h + 1)
                        act.activation(at[u % 2][h][:, :], psum[2 + h][:, :], ACT.Copy).then_inc(at_ready, 1)

                def relu(b, u, i):
                    for h in range(2):
                        act.wait_ge(hid_ready, b * 2 + h + 1)
                        up_to(act, o_ready, (b - 2) * 2 + h + 1)
                        act.activation(rt[u % 2][h][:, :], psum[4 + h][:, :], ACT.Relu, bias=bias_u[:, 0:1])\
                            .then_inc(rt_ready, 1)

                def exp(b, u, i):
                    act.wait_ge(d_ready, b + 1)
                    up_to(act, w_ready, b - 1)
                    act.activation(g_exp[u % 2][:, :, :], g_diff[u % 2][:, :, :], ACT.Exp).then_inc(e_ready, 1)

                def normalise(q, o, ready):
                    def stage(b, u, i):
                        act.wait_ge(r_ready, b + (3 if q else 1))
                        v = (u + 2) % SLOTS if q else u
                        for j in range(ACT_ROWS if q else RB):
                            ins = act.activation(o[u][:, j * C:(j + 1) * C], o[u][:, j * C:(j + 1) * C], ACT.Identity,
                                                 bias=shift[v][:, q * RB + j:q * RB + j + 1],
                                                 scale=rstd[v][:, q * RB + j:q * RB + j + 1])
                        ins.then_inc(ready, 1)
                    return stage

                if mlp:
                    pipeline(act, SLOTS, (0, copy_x), (0, copy_a), (4, normalise(0, Y, n1_ready)), (1, relu),
                             (6, normalise(1, L, out_ready)))
                elif gat:
                    pipeline(act, SLOTS, (0, copy_x), (1, exp), (4, normalise(0, Y, out_ready)))
                elif norm:
                    pipeline(act, SLOTS, (0, copy_x), (3, normalise(0, Y, out_ready)))
                else:
                    pipeline(act, SLOTS, (0, copy_x))

            @block.vector
            def _(dve):
                link = Chain(dve, step_sem, 4)

                def statistics(link, r, u, *rows):
                    w, st = in_round(r), stat[u % 2]
                    for k, y in rows:
                        for j in range(RB):
                            ins = dve.bn_stats(st[:, k * RB + j, :], y[:, j * C:(j + 1) * C])
                    link(ins)
                    s_, d_, dd, m2 = msum[u][:, w], tmp[:, 0, w], tmp[:, 1, w], tmp[:, 2, w]
                    me, mo, ve, vo = st[:, w, 1], st[:, w, 4], st[:, w, 2], st[:, w, 5]
                    dve.tensor_tensor(s_, me, mo, ALU.add)
                    dve.tensor_tensor(m2, ve, vo, ALU.add)
                    link(dve.tensor_tensor(d_, me, mo, ALU.subtract))
                    link(dve.tensor_tensor(dd, d_, d_, ALU.mult))
                    link(dve.scalar_tensor_tensor(m2, dd, C / 4.0, m2, ALU.mult, ALU.add))
                    dve.tensor_scalar(var[u][:, w], m2, 1.0 / C, LN_EPS, ALU.mult, ALU.add).then_inc(v_ready, 1)

                def scale_sums(b, u, i):
                    inv = inverse[u % 2]
                    dve.wait_ge(a_got[u], (i + 1) * 16)
                    dve.tensor_scalar(degree[:, :].unsqueeze(2), sums3(A[u])[:, :, C:C + 1], 1.0, None, ALU.max)\
                        .then_inc(degree_ready, 1)
                    dve.wait_ge(degree_ready, b + 1)
                    up_to(dve, a_scaled[0], b - 1)
                    dve.reciprocal(inv[:, :], degree[:, :]).then_inc(inv_ready, 1)
                    dve.wait_ge(inv_ready, b + 1)
                    dve.tensor_copy(invdeg[:, bass.ds(b, 1), :], inv[:, :].unsqueeze(1))
                    v = sums3(A[u])[:, 4:, 0:C]
                    dve.tensor_tensor(v, v, inv[:, 4:].unsqueeze(2).to_broadcast([P, 4, C]), ALU.mult)\
                        .then_inc(a_scaled[1], 1)

                def both_norms(r, u, i):
                    b2, u2 = r - 2, (u - 2) % SLOTS
                    first, second = not isinstance(r, int) or r < BLOCKS, not isinstance(r, int) or r >= 2
                    link.start(r)
                    if second:
                        dve.wait_ge(n1_ready, b2 + 1)
                        dve.tensor_tensor(rows3(Y[u2]), rows3(Y[u2]), per_row(K["ln_g"]), ALU.mult).then_inc(gained, 1)
                    if first:
                        dve.wait_ge(x_got[u], (i + 1) * 16)
                        for h in range(2):
                            dve.wait_ge(o_ready, r * 2 + h + 1)
                            dve.tensor_tensor(halves(Y[u], h), bank3(6 + h), halves(X[u], h), ALU.add).then_inc(y_ready, 1)
                    if second:
                        dve.wait_ge(gained, b2 + 1)
                        dve.wait_ge(xl_ready, b2 + 1)
                        dve.tensor_tensor(L[u2][:, :], Y[u2][:, :], L[u2][:, :], ALU.add).then_inc(l_ready, 1)
                        dve.wait_ge(l_ready, b2 + 1)
                    if first:
                        dve.wait_ge(y_ready, r * 2 + 2)
                    statistics(link, r, u, *([(0, Y[u])] if first else []), *([(1, L[u2])] if second else []))

                by_row = lambda v: v.rearrange("p (j h) -> p j h", h=HEADS)

                def gat_turn(b, u, i):
                    is_block = lambda v: not isinstance(v, int) or 0 <= v < BLOCKS
                    bw, uw, iw = b - 1, (u - 1) % SLOTS, i + (u - 1) // SLOTS
                    ba, ua = b - 2, (u - 2) % SLOTS
                    has_s, has_w, has_a = is_block(b), is_block(bw), is_block(ba)
                    score, weigh, stats = Chain(dve, score_steps, 5), Chain(dve, weigh_steps, 3), link
                    score.start(b), weigh.start(bw), stats.start(ba)
                    es, me, mx = g_small[:, 0, :], g_small[:, 1, :], g_small[:, 2, :]
                    diff = g_diff[u % 2]
                    s_e, m_e = sums3(A[u])[:, :, C:C + 4], sums3(A[u])[:, :, C + 4:C + 8]
                    ce, cs = g_exp[uw % 2][:, 0, :], g_exp[uw % 2][:, 1, :]
                    total = g_small[:, 3, :]
                    st = stat[ua % 2]
                    s_, d_, dd, m2 = msum[ua][:, :], tmp[:, 0, :], tmp[:, 1, :], tmp[:, 2, :]
                    mean_e, mean_o, ve, vo = st[:, :, 1], st[:, :, 4], st[:, :, 2], st[:, :, 5]

                    if has_w:
                        dve.wait_ge(e_ready, bw + 1)
                        weigh.step(dve.tensor_tensor(by_row(total), sums3(A[uw])[:, :, C:C + 4], by_row(ce), ALU.mult))
                    if has_s:
                        dve.wait_ge(a_got[u], (i + 1) * 16)
                        score.step(dve.tensor_scalar(by_row(me), s_e, 0.0, -LOW, ALU.is_equal, ALU.mult))
                    if has_w:
                        weigh.settle()
                        weigh.step(dve.tensor_tensor(total, total, cs, ALU.add))
                    if has_s:
                        score.settle()
                        score.step(dve.tensor_tensor(by_row(me), by_row(me), m_e, ALU.add))
                    if has_w:
                        weigh.settle()
                        weigh(dve.reciprocal(total, total))
                        up_to(dve, a_weighed, bw - 1)
                        dve.tensor_tensor(g_edges[uw % 2][:, :], ce, total, ALU.mult).then_inc(w_ready, 1)
                        dve.tensor_tensor(g_own[:, :], cs, total, ALU.mult).then_inc(own_ready, 1)
                    if has_a:
                        dve.wait_ge(a_weighed, ba + 1)
                        dve.tensor_tensor(rows3(Y[ua]), rows3(Y[ua]), sums3(A[ua])[:, :, 0:C], ALU.add).then_inc(a_used, 1)
                    if has_w:
                        dve.wait_ge(own_ready, bw + 1)
                        up_to(dve, stored[uw], iw, 16)
                        for g, (r, n) in enumerate(GAT_ROWS):
                            heads = lambda v: v.rearrange("p r (h d) -> p r h d", h=HEADS)
                            ins = dve.tensor_tensor(heads(rows3(Y[uw])[:, r:r + n, :]), heads(gat_bank(uw, g, n)[:, :, 0:C]),
                                                    by_row(g_own[:, :])[:, r:r + n, :].unsqueeze(3).to_broadcast([P, n, HEADS, HD]),
                                                    ALU.mult)
                            if g:
                                ins.then_inc(y_ready, 1)
                    if has_a:
                        dve.wait_ge(a_used, ba + 1)
                        for j in range(RB):
                            ins = dve.bn_stats(st[:, j, :], Y[ua][:, j * C:(j + 1) * C])
                        stats.step(ins)
                    if has_s:
                        dve.wait_ge(o_ready, b * 2 + 2)
                        for g, (r, n) in enumerate(GAT_ROWS):
                            ins = dve.tensor_scalar(by_row(es)[:, r:r + n, :], gat_bank(u, g, n)[:, :, C:], 0.2, None, ALU.mult)
                        score.step(ins)
                    if has_a:
                        stats.settle()
                        dve.tensor_tensor(s_, mean_e, mean_o, ALU.add)
                        stats.step(dve.tensor_tensor(d_, mean_e, mean_o, ALU.subtract))
                    if has_s:
                        score.settle()
                        for g, (r, n) in enumerate(GAT_ROWS):
                            ins = dve.tensor_tensor(by_row(es)[:, r:r + n, :], gat_bank(u, g, n)[:, :, C:],
                                                    by_row(es)[:, r:r + n, :], ALU.max)
                        score.step(ins)
                    if has_a:
                        stats.settle()
                        dve.tensor_tensor(m2, ve, vo, ALU.add)
                        stats.step(dve.tensor_tensor(dd, d_, d_, ALU.mult))
                    if has_s:
                        score.settle()
                        score.step(dve.tensor_tensor(mx, me, es, ALU.max))
                    if has_a:
                        stats.settle()
                        stats.step(dve.scalar_tensor_tensor(m2, dd, C / 4.0, m2, ALU.mult, ALU.add))
                    if has_s:
                        score.settle()
                        dve.tensor_tensor(diff[:, 0, :], me, mx, ALU.subtract)
                        dve.tensor_tensor(diff[:, 1, :], es, mx, ALU.subtract).then_inc(d_ready, 1)
                    if has_a:
                        stats.settle()
                        dve.tensor_scalar(var[ua][:, :], m2, 1.0 / C, LN_EPS, ALU.mult, ALU.add).then_inc(v_ready, 1)

                def add_turn(b, u, i):
                    has_b = not isinstance(b, int) or b < BLOCKS
                    has_last = norm and (not isinstance(b, int) or b >= 1)
                    if has_b:
                        dve.wait_ge(a_got[u], (i + 1) * 16)
                        up_to(dve, stored[u], i, 16)
                        if kind == "rgcn":
                            for h in range(2):
                                dve.wait_ge(o_ready, b * 2 + h + 1)
                                dve.tensor_tensor(halves(Y[u], h), bank3(out_bank(u, h)),
                                                  sums3(A[u])[:, 4 * h:4 * h + 4, 0:C], ALU.add).then_inc(y_ready, 1)
                        else:
                            for j in range(RB):
                                h = j // 4
                                if j % 4 == 0:
                                    dve.wait_ge(o_ready, b * 2 + h + 1)
                                ins = dve.scalar_tensor_tensor(
                                    Y[u][:, j * C:(j + 1) * C], A[u][:, j * W:j * W + C], invdeg[:, bass.ds(b, 1), j],
                                    psum[out_bank(u, h)][:, (j % 4) * C:(j % 4 + 1) * C], ALU.mult, ALU.add)
                                if j % 4 == 3:
                                    ins.then_inc(y_ready, 1)
                    if has_last:
                        link.start(b - 1)
                        dve.wait_ge(added, b)
                        statistics(link, b - 1, (u - 1) % SLOTS, (0, Y[(u - 1) % SLOTS]))
                    if has_b:
                        dve.wait_ge(y_ready, b * 2 + 2)
                        dve.sem_inc(a_used, 1)
                        if kind == "rgcn":
                            dve.wait_ge(x_got[u], (i + 1) * 16)
                            dve.scalar_tensor_tensor(Y[u][:, :], Y[u][:, :], 0.0, X[u][:, :], ALU.max, ALU.add)\
                                .then_inc(added, 1)
                        elif kind == "spline1":
                            dve.tensor_tensor(rows3(Y[u]), rows3(Y[u]), per_row(K["sb1"]), ALU.add).then_inc(out_ready, 1)
                        else:
                            dve.wait_ge(xb_ready, b + 1)
                            dve.tensor_tensor(Y[u][:, :], Y[u][:, :], B[u][:, :], ALU.add).then_inc(added, 1)

                if mlp:
                    pipeline(dve, SLOTS, (0, scale_sums), (4, both_norms, 2))
                elif gat:
                    g_own = sb(f"{name}_go", [P, RB * HEADS], c=c)
                    pipeline(dve, SLOTS, (1, gat_turn, 2))
                else:
                    pipeline(dve, SLOTS, (0, add_turn, int(norm)))

    edge_phase("e0", "mlp", D["x"])
    node_phase("n0", "mlp", D["x"], None, X1)
    edge_phase("e1", "gat", X1)
    node_phase("n1", "gat", X1, None, X2)
    edge_phase("e2", "bases", X2)
    node_phase("n2", "rgcn", X2, None, X3)
    edge_phase("e3", "spline1", X3)
    node_phase("n3", "spline1", X3, None, HT)
    edge_phase("e4", "spline2", HT)
    node_phase("n4", "spline2", HT, X3, out)



def _layout(x, src, dst, edge_attr_64, edge_type_64, edge_weight1, L0_gnn_global_state, L0_gnn_Wm1, L0_gnn_bm1,
            L0_gnn_Wm2, L0_gnn_bm2, L0_gnn_Wu1, L0_gnn_bu1, L0_gnn_Wu2, L0_gnn_bu2, L0_gnn_ln_g, L0_gnn_ln_b,
            L1_gnn_W, L1_gnn_att_src, L1_gnn_att_dst, L1_gnn_bias, L2_gnn_v_b, L2_gnn_a_rb, L2_gnn_loop_weight,
            L3_gnn_W1, L3_gnn_root1, L3_gnn_b1, L3_gnn_W2, L3_gnn_root2, L3_gnn_b2):
    import numpy as np

    def runs(a, fill):
        a = np.asarray(a)
        a = a.reshape(a.shape[0], -1)
        a = np.pad(a, ((0, P * TILES - a.shape[0]), (0, 0)), constant_values=fill)
        return a.reshape(P, -1)

    A = np.asarray
    wm1, wu1 = A(L0_gnn_Wm1), A(L0_gnn_Wu1)
    side = lambda w: A(w).transpose(1, 0, 2).reshape(C, -1)
    d = dict(x=A(x), src=runs(src, 0), dst=runs(dst, PAD_DST), etype=runs(edge_type_64, 0),
             eweight=runs(edge_weight1, 0), eattr=runs(edge_attr_64, 0),
             wm1x=wm1[:, :C].T, wm1e=wm1[:, C:C + ED].T, wm1g=wm1[:, C + ED:].T, wm2=A(L0_gnn_Wm2).T,
             wu1x=wu1[:, :C].T, wu1a=wu1[:, C:2 * C].T, wu1g=wu1[:, 2 * C:].T, wu2=A(L0_gnn_Wu2).T,
             gstate=A(L0_gnn_global_state).reshape(-1, 1), bm1=A(L0_gnn_bm1).reshape(-1, 1),
             bu1=A(L0_gnn_bu1).reshape(-1, 1), bm2=A(L0_gnn_bm2), bu2=A(L0_gnn_bu2),
             ln_g=A(L0_gnn_ln_g), ln_b=A(L0_gnn_ln_b), wgat=A(L1_gnn_W), atts=A(L1_gnn_att_src).reshape(-1),
             attd=A(L1_gnn_att_dst).reshape(-1), gbias=A(L1_gnn_bias), vb=side(L2_gnn_v_b),
             arb=A(L2_gnn_a_rb).T.reshape(-1), loop=A(L2_gnn_loop_weight), sw1=side(L3_gnn_W1),
             root1=A(L3_gnn_root1), sb1=A(L3_gnn_b1), sw2=side(L3_gnn_W2), root2=A(L3_gnn_root2), sb2=A(L3_gnn_b2))
    return {k: np.ascontiguousarray(v) for k, v in d.items()}


def kernel(**inputs):
    import concourse.bacc as bacc
    from concourse.bass_utils import run_bass_kernel_spmd

    arrays = _layout(**inputs)
    nc = bacc.Bacc("TRN2", target_bir_lowering=False, num_devices=1)
    D = {k: nc.dram_tensor("in_" + k, v.shape, mybir.dt.from_np(v.dtype), kind="ExternalInput").ap()
         for k, v in arrays.items()}
    out = nc.dram_tensor("out_x", [N, C], F32, kind="ExternalOutput").ap()
    build(nc, D, out)
    r = run_bass_kernel_spmd(nc, [{"in_" + k: v for k, v in arrays.items()}], core_ids=[0])
    return r.results[0]["out_x"]
```
